# Optimizing a Trainium2 kernel written in Bass

```python
import numpy as np
import jax
import jax.numpy as jnp

def _softmax(x, axis=-1):
    return jax.nn.softmax(x, axis=axis)

def _gelu(x):
    return jax.nn.gelu(x, approximate=True)

def _silu(x):
    return jax.nn.silu(x)

def _sigmoid(x):
    return jax.nn.sigmoid(x)

def _layernorm(x, axis=-1, eps=1e-05):
    m = jnp.mean(x, axis=axis, keepdims=True)
    v = jnp.var(x, axis=axis, keepdims=True)
    return (x - m) / jnp.sqrt(v + eps)

def _scatter_add(tgt, idx, src, axis=0):
    return tgt.at[idx].add(src)

def _segment_sum(src, seg, n):
    return jax.ops.segment_sum(src, seg, n)
kernel_name = 'mk_audio_tower_d1_tok_audfeat1024_r4_4cb25a'

def setup_inputs(seed: int=0):
    np.random.seed(seed)
    _w = jnp.asarray

    def _rec_inputs():
        import jax
        import jax.numpy as jnp
        _rk = jax.random.key(seed)
        x = -0.000125008 + 0.999885 * jax.random.normal(jax.random.fold_in(_rk, 1), (32, 375, 256), jnp.float32)
        return x
    x = _rec_inputs()

    def _L0_tok_setup():
        import jax, jax.numpy as jnp
        import numpy as np
        H = 32
        DECAY = 0.9
        key = jax.random.key(seed)
        ks = jax.random.split(key, 6)
        B, T, D = (8, 1024, 256)
        x = jax.random.normal(ks[0], (B, T, D), dtype=jnp.float32)
        s = 1.0 / np.sqrt(D)
        Wv = jax.random.normal(ks[1], (D, D), dtype=jnp.float32) * s
        bv = jax.random.normal(ks[2], (D,), dtype=jnp.float32) * s
        Wo = jax.random.normal(ks[3], (D, D), dtype=jnp.float32) * s
        bo = jax.random.normal(ks[4], (D,), dtype=jnp.float32) * s
        w = jnp.asarray(DECAY ** np.arange(H), dtype=jnp.float32)
        decay_w = w / jnp.sum(w)
        return {'x': x, 'Wv': Wv, 'bv': bv, 'Wo': Wo, 'bo': bo, 'decay_w': decay_w}
    _L0_tok_all = _L0_tok_setup()
    _L0_tok_in = {k: v for k, v in _L0_tok_all.items() if k in ('Wv', 'bv', 'Wo', 'bo', 'decay_w')}
    del _L0_tok_all

    def _L0_attn_setup():
        import jax, jax.numpy as jnp
        import numpy as np
        D_MODEL = 256
        N_HEADS = 16
        HEAD_DIM = D_MODEL // N_HEADS
        key = jax.random.key(seed)
        ks = jax.random.split(key, 9)
        s = 1.0 / np.sqrt(D_MODEL)
        inp = {'x': jax.random.normal(ks[0], (4, 512, D_MODEL), dtype=jnp.float32), 'wq': jax.random.uniform(ks[1], (D_MODEL, D_MODEL), jnp.float32, -s, s), 'bq': jax.random.uniform(ks[2], (D_MODEL,), jnp.float32, -s, s), 'wk': jax.random.uniform(ks[3], (D_MODEL, D_MODEL), jnp.float32, -s, s), 'bk': jax.random.uniform(ks[4], (D_MODEL,), jnp.float32, -s, s), 'wv': jax.random.uniform(ks[5], (D_MODEL, D_MODEL), jnp.float32, -s, s), 'bv': jax.random.uniform(ks[6], (D_MODEL,), jnp.float32, -s, s), 'wo': jax.random.uniform(ks[7], (D_MODEL, D_MODEL), jnp.float32, -s, s), 'bo': jax.random.uniform(ks[8], (D_MODEL,), jnp.float32, -s, s)}
        return inp
    _L0_attn_all = _L0_attn_setup()
    _L0_attn_in = {k: v for k, v in _L0_attn_all.items() if k in ('wq', 'bq', 'wk', 'bk', 'wv', 'bv', 'wo', 'bo')}
    del _L0_attn_all

    def _L0_ffn_setup():
        import jax, jax.numpy as jnp
        import numpy as np
        HIDDEN = 256
        N_ROUTED = 16
        N_SHARED = 2
        TOP_K = 2
        MID_R = HIDDEN // 4
        MID_S = HIDDEN // 2
        key = jax.random.key(seed)
        ks = jax.random.split(key, 8)
        s = 0.02
        return {'x': jax.random.normal(ks[0], (2, 256, HIDDEN), dtype=jnp.float32), 'router_w': jax.random.normal(ks[1], (HIDDEN, N_ROUTED), dtype=jnp.float32) * s, 'wg_r': jax.random.normal(ks[2], (N_ROUTED, HIDDEN, MID_R), dtype=jnp.float32) * s, 'wu_r': jax.random.normal(ks[3], (N_ROUTED, HIDDEN, MID_R), dtype=jnp.float32) * s, 'wd_r': jax.random.normal(ks[4], (N_ROUTED, MID_R, HIDDEN), dtype=jnp.float32) * s, 'wg_s': jax.random.normal(ks[5], (N_SHARED, HIDDEN, MID_S), dtype=jnp.float32) * s, 'wu_s': jax.random.normal(ks[6], (N_SHARED, HIDDEN, MID_S), dtype=jnp.float32) * s, 'wd_s': jax.random.normal(ks[7], (N_SHARED, MID_S, HIDDEN), dtype=jnp.float32) * s}
    _L0_ffn_all = _L0_ffn_setup()
    _L0_ffn_in = {k: v for k, v in _L0_ffn_all.items() if k in ('router_w', 'wg_r', 'wu_r', 'wd_r', 'wg_s', 'wu_s', 'wd_s')}
    del _L0_ffn_all
    return {'x': x, 'L0_tok_Wv': _L0_tok_in['Wv'], 'L0_tok_bv': _L0_tok_in['bv'], 'L0_tok_Wo': _L0_tok_in['Wo'], 'L0_tok_bo': _L0_tok_in['bo'], 'L0_tok_decay_w': _L0_tok_in['decay_w'], 'L0_attn_wq': _L0_attn_in['wq'], 'L0_attn_bq': _L0_attn_in['bq'], 'L0_attn_wk': _L0_attn_in['wk'], 'L0_attn_bk': _L0_attn_in['bk'], 'L0_attn_wv': _L0_attn_in['wv'], 'L0_attn_bv': _L0_attn_in['bv'], 'L0_attn_wo': _L0_attn_in['wo'], 'L0_attn_bo': _L0_attn_in['bo'], 'L0_ffn_router_w': _L0_ffn_in['router_w'], 'L0_ffn_wg_r': _L0_ffn_in['wg_r'], 'L0_ffn_wu_r': _L0_ffn_in['wu_r'], 'L0_ffn_wd_r': _L0_ffn_in['wd_r'], 'L0_ffn_wg_s': _L0_ffn_in['wg_s'], 'L0_ffn_wu_s': _L0_ffn_in['wu_s'], 'L0_ffn_wd_s': _L0_ffn_in['wd_s']}

def reference(x, L0_tok_Wv, L0_tok_bv, L0_tok_Wo, L0_tok_bo, L0_tok_decay_w, L0_attn_wq, L0_attn_bq, L0_attn_wk, L0_attn_bk, L0_attn_wv, L0_attn_bv, L0_attn_wo, L0_attn_bo, L0_ffn_router_w, L0_ffn_wg_r, L0_ffn_wu_r, L0_ffn_wd_r, L0_ffn_wg_s, L0_ffn_wu_s, L0_ffn_wd_s):
    import jax
    import jax.numpy as jnp

    def _L0_tok_ref(x, Wv, bv, Wo, bo, decay_w):
        import jax, jax.numpy as jnp
        import numpy as np
        H = 32
        DECAY = 0.9
        B, T, D = x.shape
        Hlen = decay_w.shape[0]
        x_pad = jnp.pad(x, ((0, 0), (Hlen, 0), (0, 0)))
        kernel = jnp.broadcast_to(decay_w[:, None, None], (Hlen, 1, D))
        s = jax.lax.conv_general_dilated(x_pad, kernel, window_strides=(1,), padding='VALID', dimension_numbers=('NWC', 'WIO', 'NWC'), feature_group_count=D)
        attended = s @ Wv.T + bv * jnp.sum(decay_w)
        return attended @ Wo.T + bo

    def _L0_attn_ref(x, wq, bq, wk, bk, wv, bv, wo, bo):
        import jax, jax.numpy as jnp
        import numpy as np
        D_MODEL = 256
        N_HEADS = 16
        HEAD_DIM = D_MODEL // N_HEADS
        b, s, d = x.shape
        h, hd = (N_HEADS, HEAD_DIM)
        q = (x @ wq + bq).reshape(b, s, h, hd).transpose(0, 2, 1, 3)
        k = (x @ wk + bk).reshape(b, s, h, hd).transpose(0, 2, 1, 3)
        v = (x @ wv + bv).reshape(b, s, h, hd).transpose(0, 2, 1, 3)
        scores = jnp.einsum('bhqd,bhkd->bhqk', q, k) / jnp.sqrt(jnp.float32(hd))
        causal = jnp.tril(jnp.ones((s, s), dtype=bool))
        scores = jnp.where(causal, scores, -jnp.inf)
        weights = jax.nn.softmax(scores, axis=-1)
        attn = jnp.einsum('bhqk,bhkd->bhqd', weights, v)
        attn = attn.transpose(0, 2, 1, 3).reshape(b, s, d)
        return attn @ wo + bo

    def _L0_ffn_ref(x, router_w, wg_r, wu_r, wd_r, wg_s, wu_s, wd_s):
        import jax, jax.numpy as jnp
        import numpy as np
        HIDDEN = 256
        N_ROUTED = 16
        N_SHARED = 2
        TOP_K = 2
        MID_R = HIDDEN // 4
        MID_S = HIDDEN // 2
        orig_shape = x.shape
        flat = x.reshape(-1, orig_shape[-1])
        gs = jnp.einsum('td,ndm->tnm', flat, wg_s)
        us = jnp.einsum('td,ndm->tnm', flat, wu_s)
        out = jnp.einsum('tnm,nmd->td', jax.nn.silu(gs) * us, wd_s)
        logits = (flat @ router_w).astype(jnp.float32)
        probs = jax.nn.softmax(logits, axis=-1)
        weights, indices = jax.lax.top_k(probs, TOP_K)
        weights = weights / (weights.sum(axis=-1, keepdims=True) + 1e-09)
        weights = weights.astype(x.dtype)
        comb = jnp.sum(jax.nn.one_hot(indices, N_ROUTED, dtype=x.dtype) * weights[..., None], axis=1)
        g = jnp.einsum('td,edm->tem', flat, wg_r)
        u = jnp.einsum('td,edm->tem', flat, wu_r)
        h = jax.nn.silu(g) * u
        h = h * comb[:, :, None]
        out = out + jnp.einsum('tem,emd->td', h, wd_r)
        return out.reshape(orig_shape)
    h = _L0_tok_ref(x, L0_tok_Wv, L0_tok_bv, L0_tok_Wo, L0_tok_bo, L0_tok_decay_w)
    h = h + _L0_attn_ref(_layernorm(h, axis=-1), L0_attn_wq, L0_attn_bq, L0_attn_wk, L0_attn_bk, L0_attn_wv, L0_attn_bv, L0_attn_wo, L0_attn_bo)
    h = h + _L0_ffn_ref(_layernorm(h, axis=-1), L0_ffn_router_w, L0_ffn_wg_r, L0_ffn_wu_r, L0_ffn_wd_r, L0_ffn_wg_s, L0_ffn_wu_s, L0_ffn_wd_s)
    return h

_drawn_inputs = setup_inputs


def setup_inputs(seed=0):
    import zlib

    import numpy as np

    out = dict(_drawn_inputs(seed))
    spreads = {}
    factors = {'L0_attn_bq': 8.0,
     'L0_attn_bk': 8.0,
     'L0_ffn_router_w': 3.248,
     'L0_ffn_wg_r': 3.172,
     'L0_ffn_wu_r': 2.985,
     'L0_ffn_wd_r': 2.993}
    for name, (base, spread) in spreads.items():
        noise = np.random.default_rng([zlib.crc32(name.encode()), seed]).standard_normal(out[name].shape)
        drawn = base * np.exp(spread * noise) if base else spread * noise
        out[name] = jnp.asarray(drawn.astype(out[name].dtype))
    for name, factor in factors.items():
        out[name] = (out[name] * factor).astype(out[name].dtype)
    return out
```

```python
from contextlib import ExitStack

import concourse.bass as bass
from concourse import mybir

F32 = mybir.dt.float32
F32R = mybir.dt.float32r
BF16 = mybir.dt.bfloat16
U32 = mybir.dt.uint32
ALU = mybir.AluOpType
ACT = mybir.ActivationFunctionType
AX = mybir.AxisListType

P = 128
BANK = 512
EPS = 1e-5
MASKED = -3.0e38


class Shapes:

    def __init__(self, x, decay_w, wg_r, wg_s):
        self.B, self.S_in, self.D = x.shape
        self.TAPS = decay_w.shape[0]
        self.S = self.S_in + 1
        self.KC = self.D // P
        self.H = 16
        self.HD = self.D // self.H
        self.NT = -(-self.S // P)
        self.T = [min(P, self.S - P * t) for t in range(self.NT)]
        self.T_in = [min(P, self.S_in - P * t) for t in range(self.NT)]
        self.E = wg_r.shape[0]
        self.MR = wg_r.shape[2]
        self.NS = wg_s.shape[0]
        self.RC = self.E * self.MR // P
        assert (self.D, self.NT, self.KC, self.HD, self.TAPS) == (256, 3, 2, 16, 32)
        assert self.E * self.MR == 8 * P and self.NS == 2 and wg_s.shape[2] == P


def wait_alone(eng, semaphore, value, passed):
    eng.wait_ge(semaphore, value)
    eng.sem_inc(passed, 1)


def attention_phase(nc, sem, sh, h2_dram, x, tok_Wv, tok_bv, tok_Wo, tok_bo, decay_w,
                    wq, bq, wk, bk, wv, bv, wo, bo):
    S, D, NT, T, B = sh.S, sh.D, sh.NT, sh.T, sh.B
    BAND = P + sh.TAPS
    GROUPS, UNITS = 4, 7
    CUT = [S - P * t for t in range(NT)]
    OFF = [0, CUT[0], CUT[0] + CUT[1]]
    PW = sum(CUT)
    ROWS = 3 * sh.HD

    with ExitStack() as ctx:
        def sb(name, shape, dt=F32):
            return ctx.enter_context(nc.sbuf_tensor(name, shape, dt))

        bank = [ctx.enter_context(nc.psum_tensor(f"bank{i}", [P, BANK], F32)) for i in range(8)]
        bank_max, bank_exp = bank[0:2], bank[2:4]
        bank_attn, bank_sum = bank[4], bank[5]
        bank_dense = bank[6:8]

        ident = sb("ident", [P, P])
        ident_bf = sb("ident_bf", [P, P], BF16)
        causal = sb("causal", [P, 4, P], BF16)
        band = sb("band", [P, BAND])
        ones_half = sb("ones_half", [P, 2, 32])
        minus_half = sb("minus_half", [P, NT])
        w_mix = [sb(f"w_mix_{s}", [P, 2, D], F32R) for s in ("hi", "lo")]
        w_q = [sb(f"w_q_{s}", [P, 2, D], F32R) for s in ("hi", "lo")]
        w_k = [sb(f"w_k_{s}", [P, 2, D], F32R) for s in ("hi", "lo")]
        w_v = [sb(f"w_v_{s}", [P, 2, D], F32R) for s in ("hi", "lo")]
        w_o = sb("w_o", [P, 2, D])
        bias_mix = sb("bias_mix", [P, D])
        bias_v = sb("bias_v", [P, D])
        bias_o = sb("bias_o", [P, D])
        bias_q = sb("bias_q", [P, 2])
        bias_k = sb("bias_k", [P, 2])

        x_in = [sb(f"x_in{p}", [P, NT, D]) for p in range(2)]
        mixed = [sb(f"mixed_{s}", [P, 2, S], F32R) for s in ("hi", "lo")]
        hid = [sb(f"hid{p}", [P, NT, D]) for p in range(2)]
        resid = [sb(f"resid{p}", [P, NT, D]) for p in range(2)]
        out_rows = [sb(f"out_rows{p}", [P, NT, D]) for p in range(2)]
        normed = sb("normed", [P, NT, D])
        stats = sb("stats", [P, NT, 6])
        moments = sb("moments", [P, NT, 2])
        var_eps = sb("var_eps", [P, NT])
        rstd = sb("rstd", [P, NT])
        nT = [[sb(f"normedT{p}_{s}", [P, 2, S], F32R) for s in ("hi", "lo")] for p in range(2)]
        q_flat = [sb(f"q_flat_{s}", [P, 2, S], F32R) for s in ("hi", "lo")]
        k_flat = [sb(f"k_flat_{s}", [P, 2, S], F32R) for s in ("hi", "lo")]
        q_rows = [sb(f"q_rows{p}", [P, 8, S], F32R) for p in range(2)]
        k_rows = [sb(f"k_rows{p}", [P, 8, S], F32R) for p in range(2)]
        val = [sb(f"val{p}", [P, NT, 8, 64]) for p in range(2)]
        neg_max = sb("neg_max", [P, NT, 2, 8])
        maxT = [sb(f"maxT_{s}", [8, 2, S], F32R) for s in ("hi", "lo")]
        probs = [sb(f"probs{p}", [P, 4, PW]) for p in range(2)]
        recip = sb("recip", [P, S])
        attnT = sb("attnT", [P, 2, S])

        s_load = sem("s_load")
        passed_dve, passed_pool, passed_sp = (sem(f"passed_{e}") for e in ("dve", "pool", "sp"))
        x_loaded = [sem(f"x_loaded{p}") for p in range(2)]
        rows_loaded = [[sem(f"rows_loaded{p}_{h}") for h in range(2)] for p in range(2)]
        max_loaded = [[sem(f"max_loaded{p}_{h}") for h in range(2)] for p in range(2)]
        stored = [sem(f"stored{p}") for p in range(2)]
        dense_done = sem("dense_done")
        dense_hi = sem("dense_hi")
        dense_read = sem("dense_read")
        moments_done = sem("moments_done")
        s_stats = sem("s_stats")
        s_pool = sem("s_pool")
        normed_done = sem("normed_done")
        resid_done = sem("resid_done")
        max_scores = sem("max_scores")
        max_taken = sem("max_taken")
        exp_scores = sem("exp_scores")
        exp_done = sem("exp_done")
        probs_masked = sem("probs_masked")
        pv_done = sem("pv_done")
        s_recip = sem("s_recip")
        attn_done = sem("attn_done")

        flat0 = probs[0][:, :, :].rearrange("p a b -> p (a b)")
        flat1 = probs[1][:, :, :].rearrange("p a b -> p (a b)")
        raw = {n: flat0[:, 512 * i:512 * (i + 1)].rearrange("p (k d) -> p k d", k=2)
               for i, n in enumerate(("wq", "wk", "wv", "tv", "to"))}
        perm = {n: flat1[:, 512 * i:512 * (i + 1)].rearrange("p (k d) -> p k d", k=2)
                for i, n in enumerate(("wq", "wk"))}
        toT = flat1[:, 1024:1536].rearrange("p (k d) -> p k d", k=2)
        mix_raw = flat1[:, 1536:2048].rearrange("p (k d) -> p k d", k=2)
        bvb = flat1[:, 2048:2304].rearrange("p (k m) -> p k m", k=2)
        row = flat1[0:1, 2304:2304 + P + BAND]
        toep = flat1[:, 2600:2600 + BAND]
        decay_b = flat0[:, 2560:2592]
        decay_sum = flat0[:, 2592:2593]
        bv_col = flat0[:, 2594:2596]
        bo_b = flat0[:, 2600:2856]
        bias_raw = flat1[:, 2760:2764]
        taps_dram = nc.dram_tensor("taps_row", [1, P + BAND], F32, kind="Internal").ap()

        def chunked(w):
            return w.rearrange("(k p) d -> p k d", k=2)

        def per_row(v):
            return v.rearrange("(a d) -> a d", a=1).partition_broadcast(P)

        with nc.Block() as block:
            row_set = sem("row_set")
            taps_in = sem("taps_in")
            taps_out = sem("taps_out")
            toep_in = sem("toep_in")
            zeroed = sem("zeroed")
            idents = sem("idents")
            toT_ps = sem("toT_ps")
            toT_sb = sem("toT_sb")
            mix_ps = sem("mix_ps")
            v_chain = sem("v_chain")
            loads = [0]

            @block.sync
            def _(eng):
                def load(dst, src):
                    eng.dma_start(dst, src).then_inc(s_load, 16)
                    loads[0] += 16
                load(raw["to"], chunked(tok_Wo))
                load(raw["tv"], chunked(tok_Wv))
                load(raw["wq"], chunked(wq))
                load(raw["wk"], chunked(wk))
                load(raw["wv"], chunked(wv))
                load(w_o[:, :, :], chunked(wo))
                load(bias_v[:, :], per_row(bv))
                load(bias_o[:, :], per_row(bo))
                load(bo_b, per_row(tok_bo))
                load(decay_b, per_row(decay_w))
                for k in range(2):
                    load(bv_col[:, k:k + 1], tok_bv.rearrange("(k p a) -> k p a", k=2, a=1)[k])
                for col, b in ((0, bq), (2, bk)):
                    by_head = b.rearrange("(h j e f a) -> h j e f a", h=2, j=4, e=2, a=1)
                    for e in range(2):
                        for h in range(2):
                            for j in range(4):
                                p0 = 64 * h + j
                                load(bias_raw[p0:p0 + 61:4, col + e:col + e + 1], by_head[h, j, e])
                eng.wait_ge(row_set, 1)
                eng.dma_start(row[:, P - 1:P - 1 + sh.TAPS],
                              decay_w.rearrange("(a d) -> a d", a=1)).then_inc(taps_in, 16)
                eng.wait_ge(taps_in, 16)
                eng.dma_start(taps_dram, row).then_inc(taps_out, 16)
                eng.wait_ge(taps_out, 16)
                eng.dma_start(toep, bass.AP(taps_dram.tensor, 0, [[1, P], [1, BAND]])).then_inc(toep_in, 16)

            @block.gpsimd
            def _(eng):
                eng.memset(row, 0.0).then_inc(row_set, 1)
                eng.memset(ident[:, :], 0.0).then_inc(zeroed, 1)
                eng.memset(causal[:, :, :], 0.0).then_inc(zeroed, 1)
                eng.wait_ge(zeroed, 2)
                eng.affine_select(out=ident[:, :], in_=ident[:, :], compare_op=ALU.not_equal, fill=1.0,
                                  base=0, pattern=[[-1, P]], channel_multiplier=1).then_inc(idents, 1)
                eng.affine_select(out=causal[:, :, :], in_=causal[:, :, :], compare_op=ALU.is_ge,
                                  fill=MASKED, base=0, pattern=[[0, 4], [-1, P]],
                                  channel_multiplier=1).then_inc(idents, 1)
                eng.memset(minus_half[:, :], -0.5)
                eng.memset(ones_half[:, :, :], 0.0).then_inc(zeroed, 1)
                for p in range(2):
                    eng.memset(val[p][:, :, :, :], 0.0)
                    eng.memset(k_rows[p][:, :, :].bitcast(F32), 1.0)
                eng.wait_ge(zeroed, 3)
                for e in range(2):
                    eng.memset(ones_half[:, e, 16 * e:16 * e + 16], 1.0)

            @block.tensor
            def _(eng):
                eng.wait_ge(idents, 2)
                eng.wait_ge(s_load, loads[0])
                for i in range(2):
                    for j in range(2):
                        last = eng.transpose(bank[j][:, i * P:(i + 1) * P],
                                             raw["to"][:, i, j * P:(j + 1) * P], ident[:, :])
                last.then_inc(toT_ps, 1)
                eng.wait_ge(toT_sb, 1)
                for j in range(2):
                    for k in range(2):
                        eng.matmul(bank[2 + j][:, 0:D], raw["tv"][:, k, j * P:(j + 1) * P], toT[:, k, :],
                                   start=(k == 0), stop=(k == 1))
                for k in range(2):
                    last = eng.matmul(bank[4][:, 0:D], bvb[:, k, :], toT[:, k, :],
                                      start=(k == 0), stop=(k == 1))
                last.then_inc(mix_ps, 1)

            @block.vector
            def _(eng):
                chain = [0]

                def link(ins):
                    chain[0] += 1
                    ins.then_inc(v_chain, 1)
                    eng.wait_ge(v_chain, chain[0])

                eng.wait_ge(s_load, loads[0])
                link(eng.tensor_reduce(decay_sum, decay_b, AX.X, ALU.add))
                link(eng.memset(bvb, 1.0))
                for k in range(2):
                    link(eng.tensor_scalar(bvb[:, k, :], bvb[:, k, :], bv_col[:, k:k + 1], decay_sum,
                                           ALU.mult, ALU.mult))
                eng.wait_ge(toT_ps, 1)
                eng.tensor_copy(toT[:, 0, :], bank[0][:, 0:D])
                link(eng.tensor_copy(toT[:, 1, :], bank[1][:, 0:D]))
                eng.sem_inc(toT_sb, 1)
                for n, scale in (("wq", sh.HD ** -0.5), ("wk", 1.0)):
                    for e in range(2):
                        for h in range(2):
                            for k in range(2):
                                dst = perm[n][:, k, 128 * e + 64 * h:128 * e + 64 * h + 64]
                                src = raw[n][:, k, 128 * h:128 * h + 128].rearrange("p (j e f) -> p j e f", j=4, e=2)
                                last = eng.tensor_scalar(dst.rearrange("p (f j) -> p j f", j=4), src[:, :, e, :],
                                                         scale, None, ALU.mult)
                link(last)
                link(eng.tensor_scalar(bias_q[:, :], bias_raw[:, 0:2], sh.HD ** -0.5, None, ALU.mult))
                link(eng.tensor_copy(bias_k[:, :], bias_raw[:, 2:4]))
                for full, (hi, lo) in ((perm["wq"], w_q), (perm["wk"], w_k), (raw["wv"], w_v)):
                    link(eng.tensor_copy(hi[:, :, :], full))
                    link(eng.tensor_tensor(lo[:, :, :], full, hi[:, :, :].bitcast(F32), ALU.subtract))
                eng.wait_ge(mix_ps, 1)
                for j in range(2):
                    link(eng.tensor_copy(mix_raw[:, j, :], bank[2 + j][:, 0:D]))
                link(eng.tensor_copy(w_mix[0][:, :, :], mix_raw))
                link(eng.tensor_tensor(w_mix[1][:, :, :], mix_raw, w_mix[0][:, :, :].bitcast(F32), ALU.subtract))
                link(eng.tensor_tensor(bias_mix[:, :], bank[4][:, 0:D], bo_b, ALU.add))
                link(eng.tensor_copy(ident_bf[:, :], ident[:, :]))
                eng.wait_ge(toep_in, 16)
                link(eng.tensor_copy(band[:, :], toep[:, ::-1]))

        FIRST, LAST = -2, B
        LOOP_FROM, LOOPS = 1, (B - 6) // 2
        DENSE = 16

        class Step:
            def __init__(self, b, i, first_dense):
                self.b, self.i, self.first = b, i, first_dense
                self.real = b + 2 * i if isinstance(i, int) else b
                self.front = 0 <= self.real + 2 < B
                self.maxima = 0 <= self.real + 1 < B
                self.attend = 0 <= self.real < B
                self.finish = 0 <= self.real - 1 < B
                names = self.names(self.real)
                self.dense = {n: first_dense + k for k, n in enumerate(names)}
                self.after = first_dense + len(names)

            @staticmethod
            def names(b):
                front, maxima, attend, finish = (0 <= b + d < B for d in (2, 1, 0, -1))
                return (["maxT1"] * attend + ["conv0", "conv1"] * front + ["out0", "out1"] * finish
                        + ["hid0", "hid1"] * front + ["val0", "val1"] * maxima
                        + ["nT0", "nT1", "q0", "q1", "k0", "k1"] * front + ["maxT0"] * maxima)

            def at(self, stage_shift, per, c):
                return (self.b + stage_shift) * per + c + self.i * (2 * per)

            def turn(self, stage_shift, per=1, c=0):
                n = self.b + stage_shift
                return (n // 2) * per + c + self.i * per

            def product(self, name):
                k = self.dense[name]
                return k % 2, k + self.i * (2 * DENSE)

            def read_before(self, name):
                names = self.names(self.real - 1)
                return self.first - len(names) + names.index(name) + 1 + self.i * (2 * DENSE)

        def run_steps(eng, step_fn):
            at = 0
            for b in range(FIRST, LOOP_FROM):
                s = Step(b, 0, at)
                step_fn(s)
                at = s.after
            with eng.Fori(0, LOOPS) as i:
                for b in (LOOP_FROM, LOOP_FROM + 1):
                    s = Step(b, i, at)
                    assert s.after - at == DENSE
                    step_fn(s)
                    at = s.after
            for b in range(LOOP_FROM + 2, LAST - 2 * (LOOPS - 1) + 1):
                s = Step(b, LOOPS - 1, at)
                step_fn(s)
                at = s.after

        assert LOOP_FROM + 2 * LOOPS + 2 < B

        MAX_UNITS = [(0, (0, 1, 2, 3)), (1, (0, 1)), (1, (2, 3)), (2, (0,)), (2, (1,)), (2, (2,)), (2, (3,))]
        EXP_UNITS = [(0, (0,)), (0, (1,)), (0, (2,)), (0, (3,)), (1, (0, 1)), (1, (2, 3)), (2, (0, 1, 2, 3))]
        KEYS_OF = [P, 2 * P, S]

        with nc.Block() as block:

            @block.tensor
            def _(eng):
                def open_bank(st, name):
                    par, k = st.product(name)
                    if st.dense[name] >= 2:
                        eng.wait_ge(dense_read, k - 1)
                    return bank_dense[par]

                def close(ins):
                    ins.then_inc(dense_done, 1)

                def split_product(out, pairs):
                    terms = [(a[i], m[j]) for a, m in pairs for i, j in ((0, 0), (0, 1), (1, 0))]
                    for n, (a, m) in enumerate(terms):
                        last = eng.matmul(out, a, m, start=(n == 0), stop=(n == len(terms) - 1),
                                          skip_group_check=True)
                    return last

                def split_rows(bank_, out, pairs, first):
                    terms = [(a[i], m[j]) for a, m in pairs for i, j in ((0, 0), (0, 1), (1, 0))]
                    for n, (a, m) in enumerate(terms):
                        last = eng.matmul(out, a, m, start=(first and n == 0), stop=(n == len(terms) - 1),
                                          skip_group_check=True)
                    return last

                def conv(st, j):
                    if j == 0:
                        eng.wait_ge(x_loaded[st.b % 2], st.turn(2, 32, 32))
                    ps = open_bank(st, f"conv{j}")
                    xs = x_in[st.b % 2]
                    for t in range(NT):
                        n = min(BAND, S - t * P)
                        kk = sh.T_in[t]
                        last = eng.matmul(ps[:, t * P:t * P + n], xs[0:kk, t, j * P:(j + 1) * P],
                                          band[0:kk, 0:n], start=(t == 0), stop=(t == NT - 1),
                                          skip_group_check=True)
                    close(last)

                def by_token(st, name, tiles, lhs, rhs):
                    ps = open_bank(st, name)
                    for n, t in enumerate(tiles):
                        tok = slice(t * P, t * P + T[t])
                        last = split_rows(ps, ps[0:T[t], n * D:(n + 1) * D],
                                          [([lhs[0][:, k, tok], lhs[1][:, k, tok]],
                                            [rhs[0][:, k, :], rhs[1][:, k, :]]) for k in range(2)], n == 0)
                    close(last)

                def hid_rows(st, n):
                    if n == 0:
                        par, k = st.product("conv1")
                        eng.wait_ge(dense_read, k + 1)
                    by_token(st, f"hid{n}", [(0, 1), (2,)][n], mixed, w_mix)

                def normed_T(st, j):
                    ps = open_bank(st, f"nT{j}")
                    if j == 0:
                        eng.wait_ge(normed_done, st.at(2, NT, NT))
                    for t in range(NT):
                        last = eng.transpose(ps[:, t * P:t * P + T[t]], normed[0:T[t], t, j * P:(j + 1) * P],
                                             ident[0:T[t], 0:T[t]])
                    close(last)

                def query_key(st, name, j, w):
                    ps = open_bank(st, f"{name}{j}")
                    if name == "q" and j == 0:
                        par, k = st.product("nT1")
                        eng.wait_ge(dense_read, k + 1)
                    src = nT[st.b % 2]
                    close(split_product(ps[:, 0:S], [([w[0][:, k, j * P:(j + 1) * P], w[1][:, k, j * P:(j + 1) * P]],
                                                      [src[0][:, k, :], src[1][:, k, :]]) for k in range(2)]))

                def values(st, n):
                    by_token(st, f"val{n}", [(0, 1), (2,)][n], nT[(st.b + 1) % 2], w_v)

                def out_rows_(st, n):
                    if n == 0:
                        eng.wait_ge(attn_done, st.at(-1, 2, 2))
                    ps = open_bank(st, f"out{n}")
                    for m, t in enumerate([(0, 1), (2,)][n]):
                        for k in range(2):
                            last = eng.matmul(ps[0:T[t], m * D:(m + 1) * D], attnT[:, k, t * P:t * P + T[t]],
                                              w_o[:, k, :], start=(m == 0 and k == 0), stop=(k == 1),
                                              skip_group_check=True)
                    close(last)

                def max_T(st, half, shift):
                    ps = open_bank(st, f"maxT{half}")
                    eng.wait_ge(max_taken, st.at(shift, GROUPS * UNITS, 2 * UNITS * (half + 1)))
                    for t in range(NT):
                        last = eng.transpose(ps[0:8, t * P:t * P + T[t]], neg_max[0:T[t], t, half, :],
                                             ident[0:T[t], 0:T[t]])
                    close(last)

                def scores_for_max(st, g, u):
                    n = g * UNITS + u
                    par = n % 2
                    if u == 0 and g % 2 == 0:
                        eng.wait_ge(rows_loaded[(st.b + 1) % 2][g // 2], st.turn(1, 192, 192))
                    if not (st.b + 1 == 0 and isinstance(st.i, int) and n < 2):
                        eng.wait_ge(max_taken, st.at(1, GROUPS * UNITS, n - 1))
                    ps = bank_max[par]
                    t, heads = MAX_UNITS[u]
                    q, k = q_rows[(st.b + 1) % 2], k_rows[(st.b + 1) % 2]
                    w = KEYS_OF[t]
                    c = g % 2
                    for m, j in enumerate(heads):
                        slot = 4 * (g // 2) + j
                        eng.matmul(ps[0:T[t], m * w:(m + 1) * w],
                                   q[64 * c:64 * c + ROWS, slot, t * P:t * P + T[t]],
                                   k[64 * c:64 * c + ROWS, slot, 0:w], start=(m == 0), stop=False,
                                   skip_group_check=True)
                    d = T[t]
                    dst = ps[0:d, 0:len(heads) * w].rearrange("q (m w) -> q m w", w=w)[:, :, t * P:t * P + d]
                    eng.matmul(dst, ident_bf[0:d, 0:d], causal[0:d, 0:len(heads), 0:d], start=False, stop=True,
                               skip_group_check=True).then_inc(max_scores, 1)

                def scores_for_exp(st, g, u):
                    n = g * UNITS + u
                    par = n % 2
                    if u == 0 and g % 2 == 0:
                        eng.wait_ge(max_loaded[st.b % 2][g // 2], st.turn(0, 64, 64))
                    if not (st.b == 0 and isinstance(st.i, int) and n < 2):
                        eng.wait_ge(exp_done, st.at(0, GROUPS * UNITS, n - 1))
                    ps = bank_exp[par]
                    t, heads = EXP_UNITS[u]
                    q, k = q_rows[st.b % 2], k_rows[st.b % 2]
                    w = CUT[t]
                    c = g % 2
                    for m, j in enumerate(heads):
                        slot = 4 * (g // 2) + j
                        last = eng.matmul(ps[0:T[t], m * w:(m + 1) * w],
                                          k[64 * c:64 * c + ROWS + 2, slot, t * P:t * P + T[t]],
                                          q[64 * c:64 * c + ROWS + 2, slot, t * P:S],
                                          start=(m == 0), stop=(m == len(heads) - 1), skip_group_check=True)
                    last.then_inc(exp_scores, 1)

                def products_with_values(st, g, shift):
                    par = (st.b + shift) % 2
                    e = g % 2
                    if g == 0:
                        eng.wait_ge(dense_read, st.read_before("val1"))
                    if e == 0 and not (st.b == 0 and isinstance(st.i, int) and g == 0):
                        eng.wait_ge(attn_done, st.at(shift, 2, g // 2))
                    for t in range(NT):
                        eng.wait_ge(probs_masked, st.at(shift, GROUPS * NT, g * NT + t + 1))
                        for what, out in enumerate((bank_attn, bank_sum)):
                            for j in range(4):
                                kk = T[t]
                                lhs = ones_half[0:kk, e, :] if what else \
                                    val[par][0:kk, t, 4 * (g // 2) + j, 32 * e:32 * e + 32]
                                last = eng.matmul(out[32 * j:32 * j + 32, t * P:S], lhs,
                                                  probs[g % 2][0:kk, j, OFF[t]:OFF[t] + CUT[t]],
                                                  start=(e == 0 and t == 0), stop=(e == 1 and t == NT - 1),
                                                  tile_position=(0, 32 * j), skip_group_check=True)
                    last.then_inc(pv_done, 1)

                def step(st):
                    for n in range(GROUPS * UNITS):
                        g, u = divmod(n, UNITS)
                        if st.maxima:
                            scores_for_max(st, g, u)
                        if st.attend:
                            scores_for_exp(st, g, u)
                        if n == 0 and st.attend:
                            max_T(st, 1, 0)
                        if n == 1 and st.front:
                            conv(st, 0)
                            conv(st, 1)
                        if u == 2:
                            if g == 0 and st.finish:
                                products_with_values(st, 3, -1)
                            if g > 0 and st.attend:
                                products_with_values(st, g - 1, 0)
                        if st.finish and n in (4, 5):
                            out_rows_(st, n - 4)
                        if st.front and n in (7, 8):
                            hid_rows(st, n - 7)
                        if st.maxima and n in (10, 11):
                            values(st, n - 10)
                        if st.front and n in (13, 14):
                            normed_T(st, n - 13)
                        if st.front and n in (17, 18):
                            query_key(st, "q", n - 17, w_q)
                        if st.front and n in (19, 20):
                            query_key(st, "k", n - 19, w_k)
                        if n == 22 and st.maxima:
                            max_T(st, 0, 1)
                run_steps(eng, step)

            @block.scalar
            def _(eng):
                def take_hi(st, name, dst, rows=P, bias=None):
                    par, k = st.product(name)
                    eng.wait_ge(dense_done, k + 1)
                    src = bank_dense[par][0:rows, 0:S]
                    if bias is None:
                        ins = eng.activation(dst, src, ACT.Copy)
                    else:
                        ins = eng.activation(dst, src, ACT.Identity, bias=bias)
                    ins.then_inc(dense_hi, 1)

                def exps(st, g, u):
                    n = g * UNITS + u
                    if u == 0 and not (isinstance(st.i, int) and st.b == 0 and g < 2):
                        eng.wait_ge(pv_done, st.at(0, GROUPS, g - 1))
                    eng.wait_ge(exp_scores, st.at(0, GROUPS * UNITS, n + 1))
                    t, heads = EXP_UNITS[u]
                    w = CUT[t]
                    first = heads[0]
                    eng.activation(probs[g % 2][0:T[t], first:first + len(heads), OFF[t]:OFF[t] + w],
                                   bank_exp[n % 2][0:T[t], 0:len(heads) * w].rearrange("k (m w) -> k m w", w=w),
                                   ACT.Exp).then_inc(exp_done, 1)

                def step(st):
                    for n in range(GROUPS * UNITS):
                        g, u = divmod(n, UNITS)
                        if st.attend:
                            exps(st, g, u)
                        if n == 0 and st.attend:
                            take_hi(st, "maxT1", maxT[0][0:8, 1, :], 8)
                        if n == 1 and st.front:
                            for j in range(2):
                                take_hi(st, f"conv{j}", mixed[0][:, j, :])
                        if st.front and n in (13, 14):
                            take_hi(st, f"nT{n - 13}", nT[st.b % 2][0][:, n - 13, :])
                        if st.front and n in (17, 18):
                            if n == 17:
                                if not (isinstance(st.i, int) and st.b == FIRST):
                                    for h in range(2):
                                        eng.wait_ge(rows_loaded[(st.b + 1) % 2][h], st.turn(1, 192, 192))
                            take_hi(st, f"q{n - 17}", q_flat[0][:, n - 17, :], bias=bias_q[:, n - 17:n - 16])
                        if st.front and n in (19, 20):
                            take_hi(st, f"k{n - 19}", k_flat[0][:, n - 19, :], bias=bias_k[:, n - 19:n - 18])
                        if n == 22 and st.maxima:
                            take_hi(st, "maxT0", maxT[0][0:8, 0, :], 8)
                run_steps(eng, step)

            @block.vector
            def _(eng):
                HI = ["maxT1", "conv0", "conv1", "nT0", "nT1", "q0", "q1", "k0", "k1", "maxT0"]

                def take_lo(st, name, dst, hi, rows=P, bias=None):
                    par, k = st.product(name)
                    eng.wait_ge(dense_hi, st.hi_at + [m for m in HI if m in st.dense].index(name) + 1)
                    src = bank_dense[par][0:rows, 0:S]
                    if bias is None:
                        ins = eng.tensor_tensor(dst, src, hi.bitcast(F32), ALU.subtract)
                    else:
                        ins = eng.scalar_tensor_tensor(out=dst, in0=src, scalar=bias, in1=hi.bitcast(F32),
                                                       op0=ALU.add, op1=ALU.subtract)
                    ins.then_inc(dense_read, 1)

                def maxima(st, g, u):
                    n = g * UNITS + u
                    eng.wait_ge(max_scores, st.at(1, GROUPS * UNITS, n + 1))
                    t, heads = MAX_UNITS[u]
                    hf, e = g // 2, g % 2
                    w = KEYS_OF[t]
                    src = bank_max[n % 2][0:T[t], 0:len(heads) * w].rearrange("q (m w) -> q m w", w=w)
                    first = 4 * e + heads[0]
                    dst = neg_max[0:T[t], t, hf, first:first + len(heads)]
                    eng.tensor_reduce(dst, src, AX.X, ALU.max, negate=True).then_inc(max_taken, 1)

                def hid_out(st, n):
                    par, k = st.product(f"hid{n}")
                    if n == 0 and not (isinstance(st.i, int) and st.b < 0):
                        eng.wait_ge(resid_done, st.at(0, NT, NT))
                    eng.wait_ge(dense_done, k + 1)
                    for m, t in enumerate([(0, 1), (2,)][n]):
                        last = eng.tensor_tensor(hid[st.b % 2][0:T[t], t, :], bank_dense[par][0:T[t], m * D:(m + 1) * D],
                                                 bias_mix[0:T[t], :], ALU.add)
                    last.then_inc(dense_read, 1)

                def norm_stats(st):
                    _, k = st.product("hid1")
                    eng.wait_ge(dense_read, k + 1)
                    for t in range(NT):
                        eng.bn_stats(stats[0:T[t], t, :], hid[st.b % 2][0:T[t], t, :]).then_inc(s_stats, 1)
                    for t in range(NT):
                        wait_alone(eng, s_stats, st.at(2, NT, t + 1), passed_dve)
                        eng.bn_aggr(moments[0:T[t], t, :], stats[0:T[t], t, :]).then_inc(moments_done, 1)

                def values(st, n):
                    par, k = st.product(f"val{n}")
                    eng.wait_ge(dense_done, k + 1)
                    for m, t in enumerate([(0, 1), (2,)][n]):
                        dst = val[(st.b + 1) % 2][0:T[t], t, :, :].rearrange("k a (q f) -> k a q f", q=4)[:, :, 0::3, :]
                        src = bank_dense[par][0:T[t], m * D:(m + 1) * D].rearrange("k (a e f) -> k a e f", e=2, f=16)
                        b = bias_v[0:T[t], :].rearrange("k (a e f) -> k a e f", e=2, f=16)
                        last = eng.tensor_tensor(dst, src, b, ALU.add)
                    last.then_inc(dense_read, 1)

                def out_sum(st, n):
                    if n == 0:
                        eng.wait_ge(resid_done, st.at(-1, NT, NT))
                        if not (isinstance(st.i, int) and st.b - 1 < 2):
                            eng.wait_ge(stored[(st.b - 1) % 2], st.turn(-3, 32, 32))
                    par, k = st.product(f"out{n}")
                    eng.wait_ge(dense_done, k + 1)
                    for m, t in enumerate([(0, 1), (2,)][n]):
                        last = eng.tensor_tensor(out_rows[(st.b - 1) % 2][0:T[t], t, :],
                                          bank_dense[par][0:T[t], m * D:(m + 1) * D],
                                          resid[(st.b - 1) % 2][0:T[t], t, :], ALU.add)
                    last.then_inc(dense_read, 1)

                def normalise(st, half, shift):
                    eng.wait_ge(pv_done, st.at(shift, GROUPS, 2 * half + 2))
                    eng.reciprocal(recip[:, :], bank_sum[:, 0:S]).then_inc(s_recip, 1)
                    eng.wait_ge(s_recip, st.at(shift, 2, half + 1))
                    eng.tensor_tensor(attnT[:, half, :], bank_attn[:, 0:S], recip[:, :], ALU.mult)\
                        .then_inc(attn_done, 1)

                def step(st):
                    for n in range(GROUPS * UNITS):
                        g, u = divmod(n, UNITS)
                        if st.maxima:
                            maxima(st, g, u)
                        if n == 1 and st.attend:
                            take_lo(st, "maxT1", maxT[1][0:8, 1, :], maxT[0][0:8, 1, :], 8)
                        if n == 2 and st.front:
                            for j in range(2):
                                take_lo(st, f"conv{j}", mixed[1][:, j, :], mixed[0][:, j, :])
                        if n == 3 and st.finish:
                            normalise(st, 1, -1)
                        if st.finish and n in (5, 6):
                            out_sum(st, n - 5)
                        if st.front and n in (8, 9):
                            hid_out(st, n - 8)
                            if n == 9:
                                norm_stats(st)
                        if st.maxima and n in (11, 12):
                            values(st, n - 11)
                        if st.front and n in (14, 15):
                            j = n - 14
                            take_lo(st, f"nT{j}", nT[st.b % 2][1][:, j, :], nT[st.b % 2][0][:, j, :])
                        if st.attend and n == 17:
                            normalise(st, 0, 0)
                        if st.front and n in (18, 19):
                            j = n - 18
                            take_lo(st, f"q{j}", q_flat[1][:, j, :], q_flat[0][:, j, :], bias=bias_q[:, j:j + 1])
                        if st.front and n in (20, 21):
                            j = n - 20
                            take_lo(st, f"k{j}", k_flat[1][:, j, :], k_flat[0][:, j, :], bias=bias_k[:, j:j + 1])
                        if n == 23 and st.maxima:
                            take_lo(st, "maxT0", maxT[1][0:8, 0, :], maxT[0][0:8, 0, :], 8)

                hi_count = [0]
                FULL_HI = len(HI)

                def counted(st):
                    st.hi_at = hi_count[0] + st.i * (2 * FULL_HI)
                    step(st)
                    hi_count[0] += len([m for m in HI if m in st.dense])
                run_steps(eng, counted)

            @block.gpsimd
            def _(eng):
                def mask(st, g, t):
                    last_unit = (4, 6, 7)[t]
                    wait_alone(eng, exp_done, st.at(0, GROUPS * UNITS, g * UNITS + last_unit), passed_pool)
                    d = T[t]
                    blk = probs[g % 2][0:d, :, OFF[t]:OFF[t] + d]
                    eng.affine_select(out=blk, in_=blk, compare_op=ALU.is_ge, fill=0.0, base=0,
                                      pattern=[[0, 4], [1, d]], channel_multiplier=-1).then_inc(probs_masked, 1)

                def norm(st):
                    wait_alone(eng, moments_done, st.at(2, NT, NT), passed_pool)
                    for t in range(NT):
                        eng.tensor_scalar(var_eps[0:T[t], t:t + 1], moments[0:T[t], t, 1:2], EPS, None,
                                          ALU.add).then_inc(s_pool, 1)
                    eng.wait_ge(s_pool, st.at(2, 2 * NT, NT))
                    for t in range(NT):
                        eng.tensor_tensor(rstd[0:T[t], t:t + 1], var_eps[0:T[t], t:t + 1],
                                          minus_half[0:T[t], t:t + 1], ALU.pow).then_inc(s_pool, 1)
                    wait_alone(eng, s_pool, st.at(2, 2 * NT, 2 * NT), passed_pool)
                    for t in range(NT):
                        eng.tensor_scalar(normed[0:T[t], t, :], hid[st.b % 2][0:T[t], t, :],
                                          moments[0:T[t], t, 0:1], rstd[0:T[t], t:t + 1],
                                          ALU.subtract, ALU.mult).then_inc(normed_done, 1)

                def residual(st):
                    par = (st.b + 1) % 2
                    eng.wait_ge(dense_read, st.read_before("hid1"))
                    if st.finish:
                        _, k = st.product("out1")
                        eng.wait_ge(dense_read, k + 1)
                    for t in range(NT):
                        eng.tensor_tensor(resid[par][0:T[t], t, :], hid[par][0:T[t], t, :],
                                          bias_o[0:T[t], :], ALU.add).then_inc(resid_done, 1)

                def step(st):
                    for g in range(GROUPS):
                        if g == 1 and st.front:
                            norm(st)
                        if st.attend:
                            for t in range(NT):
                                mask(st, g, t)
                        if g == 2 and st.maxima:
                            residual(st)
                run_steps(eng, step)

            @block.sync
            def _(eng):
                def load_x(st):
                    for shift in (2, 3, 4) if st.b == FIRST else (4,):
                        if isinstance(st.i, int) and st.b + shift + 2 * st.i >= B:
                            continue
                        par = (st.b + shift) % 2
                        if shift == 4:
                            _, k = st.product("conv1")
                            wait_alone(eng, dense_done, k + 1, passed_sp)
                        n = st.b + shift + 2 * st.i
                        full = P * (NT - 1)
                        eng.dma_start(x_in[par][:, 0:NT - 1, :],
                                      x[n, 0:full, :].rearrange("(t p) d -> p t d", p=P)).then_inc(x_loaded[par], 16)
                        eng.dma_start(x_in[par][0:sh.T_in[-1], NT - 1, :], x[n, full:, :])\
                            .then_inc(x_loaded[par], 16)

                def rows(st, half):
                    par = st.b % 2
                    if half == 0:
                        _, k = st.product("k1")
                        wait_alone(eng, dense_read, k + 1, passed_sp)
                    if st.attend:
                        eng.wait_ge(exp_done, st.at(0, GROUPS * UNITS, 2 * UNITS * (half + 1)))
                    for flat, dst, order in ((q_flat, q_rows, (0, 0, 1)), (k_flat, k_rows, (0, 1, 0))):
                        for c in range(2):
                            for n, part in enumerate(order):
                                eng.dma_start(dst[par][64 * c + 16 * n:64 * c + 16 * n + 16, 4 * half:4 * half + 4, :]
                                              .bitcast(F32),
                                              flat[part][64 * half:64 * half + 64, c, :].bitcast(F32)
                                              ).then_inc(rows_loaded[par][half], 16)

                def max_rows(st, half, shift):
                    par = (st.b + shift) % 2
                    _, k = st.product(f"maxT{half}")
                    eng.wait_ge(dense_read, k + 1)
                    for c in range(2):
                        for part in range(2):
                            row_ = 64 * c + ROWS + part
                            eng.dma_start(q_rows[par][row_:row_ + 1, 4 * half:4 * half + 4, :].bitcast(F32),
                                          maxT[part][4 * c:4 * c + 4, half, :].bitcast(F32)).then_inc(max_loaded[par][half], 16)

                def store(st):
                    n = st.b - 1 + 2 * st.i
                    par = (st.b - 1) % 2
                    full = P * (NT - 1)
                    _, k = st.product("out1")
                    wait_alone(eng, dense_read, k + 1, passed_sp)
                    eng.dma_start(h2_dram[n, 0:full, :].rearrange("(t p) d -> p t d", p=P),
                                  out_rows[par][:, 0:NT - 1, :]).then_inc(stored[par], 16)
                    eng.dma_start(h2_dram[n, full:, :], out_rows[par][0:T[-1], NT - 1, :]).then_inc(stored[par], 16)

                def step(st):
                    if st.attend:
                        max_rows(st, 1, 0)
                    if st.front:
                        load_x(st)
                    if st.finish:
                        store(st)
                    if st.front:
                        rows(st, 0)
                    if st.maxima:
                        max_rows(st, 0, 1)
                    if st.front:
                        rows(st, 1)
                run_steps(eng, step)
                for par in range(2):
                    eng.wait_ge(stored[par], 32 * (B // 2))



def expert_phase(nc, sem, sh, h2_dram, out, router_w, wg_r, wu_r, wd_r, wg_s, wu_s, wd_s):
    S, D, NT, T, B, E = sh.S, sh.D, sh.NT, sh.T, sh.B, sh.E
    RC = sh.RC
    C = RC + sh.NS
    RING = 2
    TILES = [(0, 1), (2,)]
    FULL = P * (NT - 1)

    with ExitStack() as ctx:
        def sb(name, shape, dt=F32):
            return ctx.enter_context(nc.sbuf_tensor(name, shape, dt))

        bank = [ctx.enter_context(nc.psum_tensor(f"ebank{i}", [P, BANK], F32)) for i in range(8)]
        bank_gate, bank_up, bank_y, bank_prep = bank[0:2], bank[2:4], bank[4:6], bank[6:8]

        ident = sb("e_ident", [P, P])
        minus_half = sb("e_minus_half", [P, NT])
        expert_no = sb("expert_no", [P, NT, E])
        w_gate = [sb(f"w_gate_{s}", [P, 2, C, P], F32R) for s in ("hi", "lo")]
        w_up = [sb(f"w_up_{s}", [P, 2, C, P], F32R) for s in ("hi", "lo")]
        w_down = [sb(f"w_down_{s}", [P, C, D], F32R) for s in ("hi", "lo")]
        w_router = [sb(f"w_router_{s}", [P, 2, E], F32R) for s in ("hi", "lo")]
        raw_gate = sb("raw_gate", [P, 2, C, P])
        raw_up = sb("raw_up", [P, 2, C, P])
        raw_down = sb("raw_down", [P, C, D])
        raw_router = sb("raw_router", [P, 2, E])

        h2 = [sb(f"h2_{p}", [P, NT, D]) for p in range(2)]
        y_rows = [sb(f"y_rows{p}", [P, NT, D]) for p in range(2)]
        normed = sb("e_normed", [P, NT, D])
        stats = sb("e_stats", [P, NT, 6])
        moments = sb("e_moments", [P, NT, 2])
        var_eps = sb("e_var_eps", [P, NT])
        rstd = sb("e_rstd", [P, NT])
        nT = [[sb(f"e_normedT{p}_{s}", [P, 2, S], F32R) for s in ("hi", "lo")] for p in range(2)]
        logits = sb("logits", [P, NT, E])
        top = sb("top", [P, NT, 8])
        top_no = sb("top_no", [P, NT, 8], U32)
        top_nof = sb("top_nof", [P, NT, 2])
        shifted = sb("shifted", [P, NT, E])
        exps = sb("exps", [P, NT, E])
        chosen = sb("chosen", [P, NT, E])
        chosen2 = sb("chosen2", [P, NT, E])
        all_sum = sb("all_sum", [P, NT])
        top_sum = sb("top_sum", [P, NT])
        inv_sum = sb("inv_sum", [P, NT])
        comb = sb("comb", [P, NT, E])
        combT = sb("combT", [E, S])
        comb_all = [sb(f"comb_all{p}", [P, RC, S]) for p in range(2)]
        tanh = [sb(f"tanh{p}", [P, S]) for p in range(2)]
        gated = [sb(f"gated{p}", [P, S]) for p in range(2)]
        hidden = [sb(f"hidden{p}", [P, S]) for p in range(2)]
        weighted = [sb(f"weighted{p}", [P, S]) for p in range(2)]
        hid_hi = [sb(f"hid_hi{p}", [P, S], F32R) for p in range(RING)]
        hid_lo = [sb(f"hid_lo{p}", [P, S], F32R) for p in range(RING)]

        comb_dram = [nc.dram_tensor(f"comb_dram{p}", [E, S], F32, kind="Internal").ap() for p in range(2)]

        w_loaded = sem("w_loaded")
        passed_dve, passed_pool, passed_sp = (sem(f"e_passed_{e}") for e in ("dve", "pool", "sp"))
        e_zeroed = sem("e_zeroed")
        e_consts = sem("e_consts")
        w_chain = sem("w_chain")
        h2_loaded = [sem(f"h2_loaded{p}") for p in range(2)]
        comb_stored = [sem(f"comb_stored{p}") for p in range(2)]
        comb_loaded = [sem(f"comb_loaded{p}") for p in range(2)]
        y_stored = [sem(f"y_stored{p}") for p in range(2)]
        e_stats_done = sem("e_stats_done")
        e_moments_done = sem("e_moments_done")
        e_pool = sem("e_pool")
        e_normed_done = sem("e_normed_done")
        prep_done = sem("prep_done")
        nT_hi_done = sem("nT_hi_done")
        prep_read = sem("prep_read")
        route = sem("route")
        route_exp = sem("route_exp")
        gate_done = sem("gate_done")
        up_done = sem("up_done")
        tanh_done = sem("tanh_done")
        gated_done = sem("gated_done")
        hidden_done = sem("hidden_done")
        weighted_done = sem("weighted_done")
        hi_done = sem("hi_done")
        lo_done = sem("lo_done")
        down_done = sem("down_done")
        y_done = sem("y_done")
        y_read = sem("y_read")

        with nc.Block() as block:
            @block.sync
            def _(eng):
                def load(dst, src):
                    eng.dma_start(dst, src).then_inc(w_loaded, 16)
                for raw_, routed, shared in ((raw_gate, wg_r, wg_s), (raw_up, wu_r, wu_s)):
                    for k in range(2):
                        for e2 in range(2):
                            load(raw_[:, k, 0:RC, sh.MR * e2:sh.MR * (e2 + 1)],
                                 routed.rearrange("(c e) (k p) m -> e k p c m", e=2, k=2)[e2, k])
                        load(raw_[:, k, RC:C, :], shared.rearrange("n (k p) m -> k p n m", k=2)[k])
                load(raw_down[:, 0:RC, :], wd_r.rearrange("(c e) m d -> (e m) c d", e=2))
                load(raw_down[:, RC:C, :], wd_s.rearrange("n m d -> m n d"))
                load(raw_router[:, :, :], router_w.rearrange("(k p) e -> p k e", k=2))

            @block.gpsimd
            def _(eng):
                eng.memset(ident[:, :], 0.0).then_inc(e_zeroed, 1)
                eng.wait_ge(e_zeroed, 1)
                eng.affine_select(out=ident[:, :], in_=ident[:, :], compare_op=ALU.not_equal, fill=1.0,
                                  base=0, pattern=[[-1, P]], channel_multiplier=1)
                eng.memset(minus_half[:, :], -0.5)
                eng.memset(logits[:, :, :], 0.0)
                eng.iota(expert_no[:, :, :], pattern=[[0, NT], [1, E]], base=0, channel_multiplier=0,
                         allow_small_or_imprecise_dtypes=True).then_inc(e_consts, 1)

            @block.vector
            def _(eng):
                eng.wait_ge(w_loaded, 16 * 15)
                n = 0
                for full, (hi, lo) in ((raw_gate, w_gate), (raw_up, w_up), (raw_down, w_down),
                                       (raw_router, w_router)):
                    n += 1
                    if len(full.shape) == 4:
                        full, hi, lo = (a[:, :, :, :] for a in (full, hi, lo))
                    else:
                        full, hi, lo = (a[:, :, :] for a in (full, hi, lo))
                    eng.tensor_copy(hi, full).then_inc(w_chain, 1)
                    eng.wait_ge(w_chain, n)
                    eng.tensor_tensor(lo, full, hi.bitcast(F32), ALU.subtract)

        LOOPS = (B - 2) // 2

        class Step:
            def __init__(self, n, i):
                self.n, self.i = n, i
                real = n + 2 * i if isinstance(i, int) else n
                self.prep = real + 1 < B
                self.experts = real >= 0
                self.load = isinstance(i, int) is False or real + 2 < B

            def at(self, shift, per, c):
                return (self.n + shift) * per + c + self.i * (2 * per)

            def turn(self, shift, per, c=0):
                return ((self.n + shift) // 2) * per + c + self.i * per

            def early(self, n):
                return isinstance(self.i, int) and self.i == 0 and self.n < n

        def run_steps(eng, step_fn):
            step_fn(Step(-1, 0))
            step_fn(Step(0, 0))
            step_fn(Step(1, 0))
            with eng.Fori(1, LOOPS) as i:
                step_fn(Step(0, i))
                step_fn(Step(1, i))
            step_fn(Step(0, LOOPS))
            step_fn(Step(1, LOOPS))

        ROUTE = 13

        def ring_hi(st, c):
            return hid_hi[c % RING]

        def ring_lo(st, c):
            return hid_lo[c % RING]

        with nc.Block() as block:

            @block.tensor
            def _(eng):
                def split3(out, pairs, first):
                    terms = [(a[i], m[j]) for a, m in pairs for i, j in ((0, 0), (0, 1), (1, 0))]
                    for n, (a, m) in enumerate(terms):
                        last = eng.matmul(out, a, m, start=(first and n == 0), stop=(n == len(terms) - 1),
                                          skip_group_check=True)
                    return last

                def open_prep(st, c):
                    if not (st.n == -1 and c < 2):
                        eng.wait_ge(prep_read, st.at(1, 4, c - 1))

                def normed_T(st):
                    for j in range(2):
                        open_prep(st, j)
                        if j == 0:
                            eng.wait_ge(e_normed_done, st.at(1, NT, NT))
                        for t in range(NT):
                            last = eng.transpose(bank_prep[j][:, t * P:t * P + T[t]],
                                                 normed[0:T[t], t, j * P:(j + 1) * P], ident[0:T[t], 0:T[t]])
                        last.then_inc(prep_done, 1)

                def router(st):
                    eng.wait_ge(prep_read, st.at(1, 4, 2))
                    src = nT[(st.n + 1) % 2]
                    for t in range(NT):
                        tok = slice(t * P, t * P + T[t])
                        last = split3(bank_prep[0][0:T[t], t * E:(t + 1) * E],
                                      [([src[0][:, k, tok], src[1][:, k, tok]],
                                        [w_router[0][:, k, :], w_router[1][:, k, :]]) for k in range(2)], t == 0)
                    last.then_inc(prep_done, 1)

                def comb_T(st):
                    open_prep(st, 3)
                    eng.wait_ge(route, st.at(1, ROUTE, ROUTE))
                    for t in range(NT):
                        last = eng.transpose(bank_prep[1][0:E, t * P:t * P + T[t]], comb[0:T[t], t, :],
                                             ident[0:T[t], 0:T[t]])
                    last.then_inc(prep_done, 1)

                def gate_up(st, c):
                    src = nT[st.n % 2]
                    if not (st.early(1) and c < 2):
                        eng.wait_ge(hidden_done, st.at(0, C, c - 1))
                    for w, ps, done in ((w_gate, bank_gate, gate_done), (w_up, bank_up, up_done)):
                        split3(ps[c % 2][:, 0:S], [([w[0][:, k, c, :], w[1][:, k, c, :]],
                                                    [src[0][:, k, :], src[1][:, k, :]]) for k in range(2)],
                               True).then_inc(done, 1)

                def down(st, c):
                    if c == 0 and not st.early(1):
                        eng.wait_ge(y_read, st.at(0, 1, 0))
                    eng.wait_ge(lo_done, st.at(0, C, c + 1))
                    for b, tiles in enumerate(TILES):
                        for m, t in enumerate(tiles):
                            tok = slice(t * P, t * P + T[t])
                            last = split3(bank_y[b][0:T[t], m * D:(m + 1) * D],
                                          [([ring_hi(st, c)[:, tok], ring_lo(st, c)[:, tok]],
                                            [w_down[0][:, c, :], w_down[1][:, c, :]])], c == 0 and m == 0)
                    last.then_inc(down_done, 1)

                def step(st):
                    for c in range(C + 2):
                        if st.experts and c < C:
                            gate_up(st, c)
                        if st.experts and c >= 2:
                            down(st, c - 2)
                        if st.prep:
                            if c == 4:
                                normed_T(st)
                            if c == 6:
                                router(st)
                            if c == 9:
                                comb_T(st)
                run_steps(eng, step)

            @block.scalar
            def _(eng):
                def tanh_of(st, c):
                    if not (st.early(1) and c < 2):
                        eng.wait_ge(gated_done, st.at(0, C, c - 1))
                    eng.wait_ge(gate_done, st.at(0, C, c + 1))
                    eng.activation(tanh[c % 2][:, :], bank_gate[c % 2][:, 0:S], ACT.Tanh, scale=0.5)\
                        .then_inc(tanh_done, 1)

                def hi_of(st, c):
                    if not (st.early(1) and c < 2):
                        eng.wait_ge(down_done, st.at(0, C, c - 1))
                    eng.wait_ge(weighted_done, st.at(0, C, c + 1))
                    eng.activation(ring_hi(st, c)[:, :], weighted[c % 2][:, :], ACT.Copy).then_inc(hi_done, 1)

                def step(st):
                    for c in range(C + 1):
                        if st.experts and c < C:
                            tanh_of(st, c)
                        if st.experts and c >= 1:
                            hi_of(st, c - 1)
                        if st.prep:
                            if c == 4:
                                for j in range(2):
                                    eng.wait_ge(prep_done, st.at(1, 4, j + 1))
                                    eng.activation(nT[(st.n + 1) % 2][0][:, j, :], bank_prep[j][:, 0:S], ACT.Copy)\
                                        .then_inc(nT_hi_done, 1)
                            if c == 7:
                                eng.wait_ge(route, st.at(1, ROUTE, 4))
                                eng.activation(exps[:, :, :], shifted[:, :, :], ACT.Exp).then_inc(route_exp, 1)
                run_steps(eng, step)

            @block.vector
            def _(eng):
                def gate_times_up(st, c):
                    if c < 2 and st.early(1):
                        pass
                    else:
                        eng.wait_ge(weighted_done, st.at(0, C, c - 1))
                    eng.wait_ge(tanh_done, st.at(0, C, c + 1))
                    eng.scalar_tensor_tensor(out=gated[c % 2][:, :], in0=tanh[c % 2][:, :], scalar=1.0,
                                             in1=bank_gate[c % 2][:, 0:S], op0=ALU.add, op1=ALU.mult)\
                        .then_inc(gated_done, 1)
                    eng.wait_ge(up_done, st.at(0, C, c + 1))
                    eng.wait_ge(gated_done, st.at(0, C, c + 1))
                    eng.scalar_tensor_tensor(out=hidden[c % 2][:, :], in0=gated[c % 2][:, :], scalar=0.5,
                                             in1=bank_up[c % 2][:, 0:S], op0=ALU.mult, op1=ALU.mult)\
                        .then_inc(hidden_done, 1)

                def norm_stats(st):
                    par = (st.n + 1) % 2
                    eng.wait_ge(h2_loaded[par], st.turn(1, 32, 32))
                    for t in range(NT):
                        eng.bn_stats(stats[0:T[t], t, :], h2[par][0:T[t], t, :]).then_inc(e_stats_done, 1)
                    for t in range(NT):
                        wait_alone(eng, e_stats_done, st.at(1, NT, t + 1), passed_dve)
                        eng.bn_aggr(moments[0:T[t], t, :], stats[0:T[t], t, :]).then_inc(e_moments_done, 1)

                def routing(st, part):
                    count = [0]

                    def link(ins):
                        ins.then_inc(route, 1)
                        count[0] += 1
                        wait_alone(eng, route, st.at(1, ROUTE, part[1] + count[0]), passed_dve)

                    if part[0] == 0:
                        eng.wait_ge(prep_done, st.at(1, 4, 3))
                        eng.tensor_copy(logits[:, 0:NT - 1, :],
                                        bank_prep[0][:, 0:(NT - 1) * E].rearrange("p (t e) -> p t e", e=E))
                        eng.tensor_copy(logits[0:T[-1], NT - 1, :], bank_prep[0][0:T[-1], (NT - 1) * E:NT * E])\
                            .then_inc(prep_read, 1)
                        wait_alone(eng, prep_read, st.at(1, 4, 3), passed_dve)
                        for t in range(NT):
                            ins = eng.max(top[:, t, :], logits[:, t, :])
                        link(ins)
                        for t in range(NT):
                            ins = eng.max_index(top_no[:, t, :], top[:, t, :], logits[:, t, :])
                        link(ins)
                        link(eng.tensor_copy(top_nof[:, :, :], top_no[:, :, 0:2]))
                        link(eng.tensor_tensor(shifted[:, :, :], logits[:, :, :],
                                               top[:, :, 0:1].broadcast_to([P, NT, E]), ALU.subtract))
                        link(eng.tensor_tensor(chosen[:, :, :], expert_no[:, :, :],
                                               top_nof[:, :, 0:1].broadcast_to([P, NT, E]), ALU.is_equal))
                        link(eng.tensor_tensor(chosen2[:, :, :], expert_no[:, :, :],
                                               top_nof[:, :, 1:2].broadcast_to([P, NT, E]), ALU.is_equal))
                        link(eng.tensor_tensor(chosen[:, :, :], chosen[:, :, :], chosen2[:, :, :], ALU.add))
                    else:
                        eng.wait_ge(route_exp, st.at(1, 1, 1))
                        link(eng.tensor_reduce(all_sum[:, :], exps[:, :, :], AX.X, ALU.add))
                        link(eng.tensor_tensor(chosen[:, :, :], chosen[:, :, :], exps[:, :, :], ALU.mult))
                        link(eng.tensor_reduce(top_sum[:, :], chosen[:, :, :], AX.X, ALU.add))
                        link(eng.scalar_tensor_tensor(out=top_sum[:, :], in0=all_sum[:, :], scalar=1e-9,
                                                      in1=top_sum[:, :], op0=ALU.mult, op1=ALU.add))
                        link(eng.reciprocal(inv_sum[:, :], top_sum[:, :]))
                        link(eng.tensor_tensor(comb[:, :, :], chosen[:, :, :],
                                               inv_sum[:, :].rearrange("p (t a) -> p t a", a=1)
                                               .broadcast_to([P, NT, E]), ALU.mult))

                def result(st):
                    if not st.early(2):
                        eng.wait_ge(y_stored[st.n % 2], st.turn(-2, 32, 32))
                    eng.wait_ge(down_done, st.at(0, C, C))
                    for b, tiles in enumerate(TILES):
                        for m, t in enumerate(tiles):
                            ins = eng.tensor_tensor(y_rows[st.n % 2][0:T[t], t, :],
                                                    bank_y[b][0:T[t], m * D:(m + 1) * D],
                                                    h2[st.n % 2][0:T[t], t, :], ALU.add)
                    ins.then_inc(y_read, 1)

                def step(st):
                    for c in range(C):
                        if st.experts:
                            gate_times_up(st, c)
                        if st.prep:
                            if c == 2:
                                norm_stats(st)
                            if c == 4:
                                for j in range(2):
                                    eng.wait_ge(nT_hi_done, st.at(1, 2, j + 1))
                                    dst = nT[(st.n + 1) % 2]
                                    eng.tensor_tensor(dst[1][:, j, :], bank_prep[j][:, 0:S],
                                                      dst[0][:, j, :].bitcast(F32), ALU.subtract)\
                                        .then_inc(prep_read, 1)
                            if c == 6:
                                routing(st, (0, 0))
                            if c == 8:
                                routing(st, (1, 7))
                            if c == 9:
                                eng.wait_ge(prep_done, st.at(1, 4, 4))
                                eng.tensor_copy(combT[:, :], bank_prep[1][0:E, 0:S]).then_inc(prep_read, 1)
                    if st.experts:
                        result(st)
                run_steps(eng, step)

            @block.gpsimd
            def _(eng):
                def norm(st):
                    wait_alone(eng, e_moments_done, st.at(1, NT, NT), passed_pool)
                    for t in range(NT):
                        eng.tensor_scalar(var_eps[0:T[t], t:t + 1], moments[0:T[t], t, 1:2], EPS, None,
                                          ALU.add).then_inc(e_pool, 1)
                    eng.wait_ge(e_pool, st.at(1, 2 * NT, NT))
                    for t in range(NT):
                        eng.tensor_tensor(rstd[0:T[t], t:t + 1], var_eps[0:T[t], t:t + 1],
                                          minus_half[0:T[t], t:t + 1], ALU.pow).then_inc(e_pool, 1)
                    wait_alone(eng, e_pool, st.at(1, 2 * NT, 2 * NT), passed_pool)
                    for t in range(NT):
                        eng.tensor_scalar(normed[0:T[t], t, :], h2[(st.n + 1) % 2][0:T[t], t, :],
                                          moments[0:T[t], t, 0:1], rstd[0:T[t], t:t + 1],
                                          ALU.subtract, ALU.mult).then_inc(e_normed_done, 1)

                def weigh(st, c):
                    if not (st.early(1) and c < 2):
                        eng.wait_ge(lo_done, st.at(0, C, c - 1))
                    wait_alone(eng, hidden_done, st.at(0, C, c + 1), passed_pool)
                    if c == 0:
                        eng.wait_ge(comb_loaded[st.n % 2], st.turn(0, 32, 32))
                    if c < RC:
                        eng.tensor_tensor(weighted[c % 2][:, :], hidden[c % 2][:, :],
                                          comb_all[st.n % 2][:, c, :], ALU.mult).then_inc(weighted_done, 1)
                    else:
                        eng.tensor_copy(weighted[c % 2][:, :], hidden[c % 2][:, :]).then_inc(weighted_done, 1)

                def lo_of(st, c):
                    eng.wait_ge(hi_done, st.at(0, C, c + 1))
                    eng.tensor_tensor(ring_lo(st, c)[:, :], weighted[c % 2][:, :],
                                      ring_hi(st, c)[:, :].bitcast(F32), ALU.subtract).then_inc(lo_done, 1)

                def step(st):
                    for c in range(C + 1):
                        if st.experts and c < C:
                            weigh(st, c)
                        if st.experts and c >= 1:
                            lo_of(st, c - 1)
                        if st.prep and c == 2:
                            norm(st)
                run_steps(eng, step)

            @block.sync
            def _(eng):
                def load_h2(par, n):
                    eng.dma_start(h2[par][:, 0:NT - 1, :],
                                  h2_dram[n, 0:FULL, :].rearrange("(t p) d -> p t d", p=P)).then_inc(h2_loaded[par], 16)
                    eng.dma_start(h2[par][0:T[-1], NT - 1, :], h2_dram[n, FULL:, :]).then_inc(h2_loaded[par], 16)

                def step(st):
                    if st.n == -1:
                        load_h2(0, 0)
                        load_h2(1, 1)
                    if st.prep:
                        par = (st.n + 1) % 2
                        eng.wait_ge(prep_read, st.at(1, 4, 4))
                        eng.dma_start(comb_dram[par], combT[:, :]).then_inc(comb_stored[par], 16)
                        wait_alone(eng, comb_stored[par], st.turn(1, 16, 16), passed_sp)
                        if st.n >= 1 or not isinstance(st.i, int) or st.i > 0:
                            eng.wait_ge(weighted_done, st.at(-1, C, C))
                        for e2 in range(2):
                            eng.dma_start(comb_all[par][64 * e2:64 * e2 + 64, :, :],
                                          bass.AP(comb_dram[par].tensor, e2 * S, [[0, 64], [2 * S, RC], [1, S]]))\
                                .then_inc(comb_loaded[par], 16)
                    if st.experts:
                        n = st.n + 2 * st.i
                        wait_alone(eng, y_read, st.at(0, 1, 1), passed_sp)
                        eng.dma_start(out[n, 0:FULL, :].rearrange("(t p) d -> p t d", p=P),
                                      y_rows[st.n % 2][:, 0:NT - 1, :]).then_inc(y_stored[st.n % 2], 16)
                        eng.dma_start(out[n, FULL:, :], y_rows[st.n % 2][0:T[-1], NT - 1, :])\
                            .then_inc(y_stored[st.n % 2], 16)
                        if st.load:
                            load_h2(st.n % 2, n + 2)
                run_steps(eng, step)
                for par in range(2):
                    eng.wait_ge(y_stored[par], 32 * (B // 2))


def audio_tower(nc, x, tok_Wv, tok_bv, tok_Wo, tok_bo, decay_w, wq, bq, wk, bk, wv, bv, wo, bo,
                router_w, wg_r, wu_r, wd_r, wg_s, wu_s, wd_s, out):
    sh = Shapes(x, decay_w, wg_r, wg_s)
    h2_dram = nc.dram_tensor("h2_dram", [sh.B, sh.S, sh.D], F32, kind="Internal").ap()
    with ExitStack() as ctx:
        def sem(name):
            return ctx.enter_context(nc.semaphore(name))

        attention_phase(nc, sem, sh, h2_dram, x, tok_Wv, tok_bv, tok_Wo, tok_bo, decay_w,
                        wq, bq, wk, bk, wv, bv, wo, bo)
        expert_phase(nc, sem, sh, h2_dram, out, router_w, wg_r, wu_r, wd_r, wg_s, wu_s, wd_s)


_INS = ['x', 'L0_tok_Wv', 'L0_tok_bv', 'L0_tok_Wo', 'L0_tok_bo', 'L0_tok_decay_w', 'L0_attn_wq', 'L0_attn_bq',
        'L0_attn_wk', 'L0_attn_bk', 'L0_attn_wv', 'L0_attn_bv', 'L0_attn_wo', 'L0_attn_bo', 'L0_ffn_router_w',
        'L0_ffn_wg_r', 'L0_ffn_wu_r', 'L0_ffn_wd_r', 'L0_ffn_wg_s', 'L0_ffn_wu_s', 'L0_ffn_wd_s']


def kernel(**inputs):
    import numpy as _np
    import concourse.bacc as _bacc
    from concourse import mybir as _mybir
    from concourse.bass_utils import run_bass_kernel_spmd as _run

    nc = _bacc.Bacc("TRN2", target_bir_lowering=False, num_devices=1)
    arrays, args = {}, []
    for name in _INS:
        a = _np.ascontiguousarray(inputs[name])
        arrays[f"in_{name}_dram"] = a
        args.append(nc.dram_tensor(f"in_{name}_dram", a.shape, _mybir.dt.from_np(a.dtype), kind="ExternalInput").ap())
    batch, tokens, dim = inputs["x"].shape
    out = nc.dram_tensor("out_0_dram", (batch, tokens + 1, dim), F32, kind="ExternalOutput").ap()
    audio_tower(nc, *args, out)
    r = _run(nc, [arrays], core_ids=[0])
    return r.results[0]["out_0_dram"]
```

```python
from contextlib import ExitStack

import concourse.bass as bass
from concourse import mybir

F32 = mybir.dt.float32
F32R = mybir.dt.float32r
BF16 = mybir.dt.bfloat16
U32 = mybir.dt.uint32
ALU = mybir.AluOpType
ACT = mybir.ActivationFunctionType
AX = mybir.AxisListType

P = 128
BANK = 512
EPS = 1e-5
MASKED = -3.0e38


class Shapes:

    def __init__(self, x, decay_w, wg_r, wg_s):
        self.B, self.S_in, self.D = x.shape
        self.TAPS = decay_w.shape[0]
        self.S = self.S_in + 1
        self.KC = self.D // P
        self.H = 16
        self.HD = self.D // self.H
        self.NT = -(-self.S // P)
        self.T = [min(P, self.S - P * t) for t in range(self.NT)]
        self.T_in = [min(P, self.S_in - P * t) for t in range(self.NT)]
        self.E = wg_r.shape[0]
        self.MR = wg_r.shape[2]
        self.NS = wg_s.shape[0]
        self.RC = self.E * self.MR // P
        assert (self.D, self.NT, self.KC, self.HD, self.TAPS) == (256, 3, 2, 16, 32)
        assert self.E * self.MR == 8 * P and self.NS == 2 and wg_s.shape[2] == P


def wait_alone(eng, semaphore, value, passed):
    eng.wait_ge(semaphore, value)
    eng.sem_inc(passed, 1)


def attention_phase(nc, sem, sh, h2_dram, x, tok_Wv, tok_bv, tok_Wo, tok_bo, decay_w,
                    wq, bq, wk, bk, wv, bv, wo, bo):
    S, D, NT, T, B = sh.S, sh.D, sh.NT, sh.T, sh.B
    BAND = P + sh.TAPS
    GROUPS, UNITS = 4, 7
    CUT = [S - P * t for t in range(NT)]
    OFF = [0, CUT[0], CUT[0] + CUT[1]]
    PW = sum(CUT)
    ROWS = 3 * sh.HD

    with ExitStack() as ctx:
        def sb(name, shape, dt=F32):
            return ctx.enter_context(nc.sbuf_tensor(name, shape, dt))

        bank = [ctx.enter_context(nc.psum_tensor(f"bank{i}", [P, BANK], F32)) for i in range(8)]
        bank_max, bank_exp = bank[0:2], bank[2:4]
        bank_pv = bank[4:6]
        bank_dense = bank[6:8]

        ident = sb("ident", [P, P])
        ident_bf = sb("ident_bf", [P, P], BF16)
        causal = sb("causal", [P, 4, P], BF16)
        band = sb("band", [P, BAND])
        strip_half = sb("strip_half", [P, 2])
        minus_half = sb("minus_half", [P, NT])
        w_mix = [sb(f"w_mix_{s}", [P, 2, D], F32R) for s in ("hi", "lo")]
        w_q = [sb(f"w_q_{s}", [P, 2, D], F32R) for s in ("hi", "lo")]
        w_k = [sb(f"w_k_{s}", [P, 2, D], F32R) for s in ("hi", "lo")]
        w_v = [sb(f"w_v_{s}", [P, 2, D], F32R) for s in ("hi", "lo")]
        w_o = sb("w_o", [P, 2, D])
        bias_mix = sb("bias_mix", [P, D])
        bias_v = sb("bias_v", [P, D])
        bias_o = sb("bias_o", [P, D])
        bias_q = sb("bias_q", [P, 2])
        bias_k = sb("bias_k", [P, 2])

        x_in = [sb(f"x_in{p}", [P, NT, D]) for p in range(2)]
        mixed = [sb(f"mixed_{s}", [P, 2, S], F32R) for s in ("hi", "lo")]
        hid = [sb(f"hid{p}", [P, NT, D]) for p in range(2)]
        resid = [sb(f"resid{p}", [P, NT, D]) for p in range(2)]
        out_rows = [sb(f"out_rows{p}", [P, NT, D]) for p in range(2)]
        normed = sb("normed", [P, NT, D])
        stats = sb("stats", [P, NT, 6])
        moments = sb("moments", [P, NT, 2])
        var_eps = sb("var_eps", [P, NT])
        rstd = sb("rstd", [P, NT])
        nT = [[sb(f"normedT{p}_{s}", [P, 2, S], F32R) for s in ("hi", "lo")] for p in range(2)]
        q_flat = [sb(f"q_flat_{s}", [P, 2, S], F32R) for s in ("hi", "lo")]
        k_flat = [sb(f"k_flat_{s}", [P, 2, S], F32R) for s in ("hi", "lo")]
        q_rows = [sb(f"q_rows{p}", [P, 8, S], F32R) for p in range(2)]
        k_rows = [sb(f"k_rows{p}", [P, 8, S], F32R) for p in range(2)]
        val = [sb(f"val{p}", [P, NT, 8, 64]) for p in range(2)]
        neg_max = sb("neg_max", [P, NT, 2, 8])
        maxT = [sb(f"maxT_{s}", [8, 2, S], F32R) for s in ("hi", "lo")]
        probs = [sb(f"probs{p}", [P, 4, PW]) for p in range(2)]
        even_attn = sb("even_attn", [P, S])
        even_sum = sb("even_sum", [P, S])
        attn_raw = sb("attn_raw", [P, S])
        sums_swapped = sb("sums_swapped", [P, S])
        sums = sb("sums", [P, S])
        recip = sb("recip", [P, S])
        attnT = sb("attnT", [P, 2, S])

        s_load = sem("s_load")
        passed_dve, passed_pool, passed_sp = (sem(f"passed_{e}") for e in ("dve", "pool", "sp"))
        x_loaded = [sem(f"x_loaded{p}") for p in range(2)]
        rows_loaded = [[sem(f"rows_loaded{p}_{h}") for h in range(2)] for p in range(2)]
        max_loaded = [[sem(f"max_loaded{p}_{h}") for h in range(2)] for p in range(2)]
        stored = [sem(f"stored{p}") for p in range(2)]
        dense_done = sem("dense_done")
        dense_hi = sem("dense_hi")
        dense_read = sem("dense_read")
        moments_done = sem("moments_done")
        s_stats = sem("s_stats")
        var_done = sem("var_done")
        rstd_done = sem("rstd_done")
        normed_done = sem("normed_done")
        resid_done = sem("resid_done")
        max_scores = sem("max_scores")
        max_taken = sem("max_taken")
        exp_scores = sem("exp_scores")
        exp_done = sem("exp_done")
        probs_masked = sem("probs_masked")
        pv_done = sem("pv_done")
        even_kept = sem("even_kept")
        pv_read = sem("pv_read")
        sums_ready = sem("sums_ready")
        recip_done = sem("recip_done")
        attn_done = sem("attn_done")

        flat0 = probs[0][:, :, :].rearrange("p a b -> p (a b)")
        flat1 = probs[1][:, :, :].rearrange("p a b -> p (a b)")
        raw = {n: flat0[:, 512 * i:512 * (i + 1)].rearrange("p (k d) -> p k d", k=2)
               for i, n in enumerate(("wq", "wk", "wv", "tv", "to"))}
        perm = {n: flat1[:, 512 * i:512 * (i + 1)].rearrange("p (k d) -> p k d", k=2)
                for i, n in enumerate(("wq", "wk"))}
        toT = flat1[:, 1024:1536].rearrange("p (k d) -> p k d", k=2)
        mix_raw = flat1[:, 1536:2048].rearrange("p (k d) -> p k d", k=2)
        bvb = flat1[:, 2048:2304].rearrange("p (k m) -> p k m", k=2)
        row = flat1[0:1, 2304:2304 + P + BAND]
        toep = flat1[:, 2600:2600 + BAND]
        decay_b = flat0[:, 2560:2592]
        decay_sum = flat0[:, 2592:2593]
        bv_col = flat0[:, 2594:2596]
        bo_b = flat0[:, 2600:2856]
        bias_raw = flat1[:, 2760:2764]
        taps_dram = nc.dram_tensor("taps_row", [1, P + BAND], F32, kind="Internal").ap()

        def chunked(w):
            return w.rearrange("(k p) d -> p k d", k=2)

        def per_row(v):
            return v.rearrange("(a d) -> a d", a=1).partition_broadcast(P)

        with nc.Block() as block:
            row_set = sem("row_set")
            taps_in = sem("taps_in")
            taps_out = sem("taps_out")
            toep_in = sem("toep_in")
            zeroed = sem("zeroed")
            idents = sem("idents")
            toT_ps = sem("toT_ps")
            toT_sb = sem("toT_sb")
            mix_ps = sem("mix_ps")
            v_chain = sem("v_chain")
            loads = [0]

            @block.sync
            def _(eng):
                def load(dst, src):
                    eng.dma_start(dst, src).then_inc(s_load, 16)
                    loads[0] += 16
                load(raw["to"], chunked(tok_Wo))
                load(raw["tv"], chunked(tok_Wv))
                load(raw["wq"], chunked(wq))
                load(raw["wk"], chunked(wk))
                load(raw["wv"], chunked(wv))
                load(w_o[:, :, :], chunked(wo))
                load(bias_v[:, :], per_row(bv))
                load(bias_o[:, :], per_row(bo))
                load(bo_b, per_row(tok_bo))
                load(decay_b, per_row(decay_w))
                for k in range(2):
                    load(bv_col[:, k:k + 1], tok_bv.rearrange("(k p a) -> k p a", k=2, a=1)[k])
                for col, b in ((0, bq), (2, bk)):
                    by_head = b.rearrange("(h j e f a) -> h j e f a", h=2, j=4, e=2, a=1)
                    for e in range(2):
                        for h in range(2):
                            for j in range(4):
                                p0 = 64 * h + j
                                load(bias_raw[p0:p0 + 61:4, col + e:col + e + 1], by_head[h, j, e])
                eng.wait_ge(row_set, 1)
                eng.dma_start(row[:, P - 1:P - 1 + sh.TAPS],
                              decay_w.rearrange("(a d) -> a d", a=1)).then_inc(taps_in, 16)
                eng.wait_ge(taps_in, 16)
                eng.dma_start(taps_dram, row).then_inc(taps_out, 16)
                eng.wait_ge(taps_out, 16)
                eng.dma_start(toep, bass.AP(taps_dram.tensor, 0, [[1, P], [1, BAND]])).then_inc(toep_in, 16)

            @block.gpsimd
            def _(eng):
                eng.memset(row, 0.0).then_inc(row_set, 1)
                eng.memset(ident[:, :], 0.0).then_inc(zeroed, 1)
                eng.memset(causal[:, :, :], 0.0).then_inc(zeroed, 1)
                eng.wait_ge(zeroed, 2)
                eng.affine_select(out=ident[:, :], in_=ident[:, :], compare_op=ALU.not_equal, fill=1.0,
                                  base=0, pattern=[[-1, P]], channel_multiplier=1).then_inc(idents, 1)
                eng.affine_select(out=causal[:, :, :], in_=causal[:, :, :], compare_op=ALU.is_ge,
                                  fill=MASKED, base=0, pattern=[[0, 4], [-1, P]],
                                  channel_multiplier=1).then_inc(idents, 1)
                eng.memset(minus_half[:, :], -0.5)
                eng.memset(moments[:, :, :], 1.0)
                for p in range(2):
                    eng.memset(val[p][:, :, :, :], 1.0)
                    eng.memset(k_rows[p][:, :, :].bitcast(F32), 1.0)
                    eng.memset(q_rows[p][:, :, :].bitcast(F32), 0.0)

            @block.tensor
            def _(eng):
                eng.wait_ge(idents, 2)
                eng.wait_ge(s_load, loads[0])
                for i in range(2):
                    for j in range(2):
                        last = eng.transpose(bank[j][:, i * P:(i + 1) * P],
                                             raw["to"][:, i, j * P:(j + 1) * P], ident[:, :])
                last.then_inc(toT_ps, 1)
                eng.wait_ge(toT_sb, 1)
                for j in range(2):
                    for k in range(2):
                        eng.matmul(bank[2 + j][:, 0:D], raw["tv"][:, k, j * P:(j + 1) * P], toT[:, k, :],
                                   start=(k == 0), stop=(k == 1))
                for k in range(2):
                    last = eng.matmul(bank[4][:, 0:D], bvb[:, k, :], toT[:, k, :],
                                      start=(k == 0), stop=(k == 1))
                last.then_inc(mix_ps, 1)

            @block.vector
            def _(eng):
                chain = [0]

                def link(ins):
                    chain[0] += 1
                    ins.then_inc(v_chain, 1)
                    eng.wait_ge(v_chain, chain[0])

                eng.wait_ge(s_load, loads[0])
                link(eng.tensor_reduce(decay_sum, decay_b, AX.X, ALU.add))
                link(eng.memset(bvb, 1.0))
                for k in range(2):
                    link(eng.tensor_scalar(bvb[:, k, :], bvb[:, k, :], bv_col[:, k:k + 1], decay_sum,
                                           ALU.mult, ALU.mult))
                eng.wait_ge(toT_ps, 1)
                eng.tensor_copy(toT[:, 0, :], bank[0][:, 0:D])
                link(eng.tensor_copy(toT[:, 1, :], bank[1][:, 0:D]))
                eng.sem_inc(toT_sb, 1)
                for n, scale in (("wq", sh.HD ** -0.5), ("wk", 1.0)):
                    for e in range(2):
                        for h in range(2):
                            for k in range(2):
                                dst = perm[n][:, k, 128 * e + 64 * h:128 * e + 64 * h + 64]
                                src = raw[n][:, k, 128 * h:128 * h + 128].rearrange("p (j e f) -> p j e f", j=4, e=2)
                                last = eng.tensor_scalar(dst.rearrange("p (f j) -> p j f", j=4), src[:, :, e, :],
                                                         scale, None, ALU.mult)
                link(last)
                link(eng.tensor_scalar(bias_q[:, :], bias_raw[:, 0:2], sh.HD ** -0.5, None, ALU.mult))
                link(eng.tensor_copy(bias_k[:, :], bias_raw[:, 2:4]))
                for full, (hi, lo) in ((perm["wq"], w_q), (perm["wk"], w_k), (raw["wv"], w_v)):
                    link(eng.tensor_copy(hi[:, :, :], full))
                    link(eng.tensor_tensor(lo[:, :, :], full, hi[:, :, :].bitcast(F32), ALU.subtract))
                eng.wait_ge(mix_ps, 1)
                for j in range(2):
                    link(eng.tensor_copy(mix_raw[:, j, :], bank[2 + j][:, 0:D]))
                link(eng.tensor_copy(w_mix[0][:, :, :], mix_raw))
                link(eng.tensor_tensor(w_mix[1][:, :, :], mix_raw, w_mix[0][:, :, :].bitcast(F32), ALU.subtract))
                link(eng.tensor_tensor(bias_mix[:, :], bank[4][:, 0:D], bo_b, ALU.add))
                link(eng.tensor_copy(ident_bf[:, :], ident[:, :]))
                link(eng.tensor_reduce(strip_half[:, :], ident[:, :].rearrange("p (j e f) -> p e j f", j=4, e=2),
                                       AX.XY, ALU.add))
                eng.wait_ge(toep_in, 16)
                link(eng.tensor_copy(band[:, :], toep[:, ::-1]))

        FIRST, LAST = -3, B
        LOOP_FROM, LOOPS = 1, (B - 6) // 2
        DENSE = 16

        class Step:
            def __init__(self, b, i, first_dense):
                self.b, self.i, self.first = b, i, first_dense
                self.real = b + 2 * i if isinstance(i, int) else b
                self.mix = 0 <= self.real + 3 < B
                self.front = 0 <= self.real + 2 < B
                self.maxima = 0 <= self.real + 1 < B
                self.attend = 0 <= self.real < B
                self.finish = 0 <= self.real - 1 < B
                names = self.names(self.real)
                self.dense = {n: first_dense + k for k, n in enumerate(names)}
                self.after = first_dense + len(names)

            @staticmethod
            def names(b):
                mix, front, maxima, attend, finish = (0 <= b + d < B for d in (3, 2, 1, 0, -1))
                return (["hid0", "hid1"] * front + ["maxT1"] * attend + ["val0"] * maxima
                        + ["nT0", "nT1", "q0", "q1", "k0", "k1"] * front + ["maxT0"] * maxima
                        + ["out0", "out1"] * finish + ["conv0", "conv1"] * mix + ["val1"] * maxima)

            def at(self, stage_shift, per, c):
                return (self.b + stage_shift) * per + c + self.i * (2 * per)

            def turn(self, stage_shift, per=1, c=0):
                n = self.b + stage_shift
                return (n // 2) * per + c + self.i * per

            def product(self, name):
                k = self.dense[name]
                return k % 2, k + self.i * (2 * DENSE)

            def read_before(self, name):
                names = self.names(self.real - 1)
                return self.first - len(names) + names.index(name) + 1 + self.i * (2 * DENSE)

        def run_steps(eng, step_fn):
            at = 0
            for b in range(FIRST, LOOP_FROM):
                s = Step(b, 0, at)
                step_fn(s)
                at = s.after
            with eng.Fori(0, LOOPS) as i:
                for b in (LOOP_FROM, LOOP_FROM + 1):
                    s = Step(b, i, at)
                    assert s.after - at == DENSE
                    step_fn(s)
                    at = s.after
            for b in range(LOOP_FROM + 2, LAST - 2 * (LOOPS - 1) + 1):
                s = Step(b, LOOPS - 1, at)
                step_fn(s)
                at = s.after

        assert LOOP_FROM + 2 * LOOPS + 2 < B

        MAX_UNITS = [(0, (0, 1, 2, 3)), (1, (0, 1)), (1, (2, 3)), (2, (0,)), (2, (1,)), (2, (2,)), (2, (3,))]
        EXP_UNITS = [(0, (0,)), (0, (1,)), (0, (2,)), (0, (3,)), (1, (0, 1)), (1, (2, 3)), (2, (0, 1, 2, 3))]
        KEYS_OF = [P, 2 * P, S]

        with nc.Block() as block:

            @block.tensor
            def _(eng):
                def open_bank(st, name):
                    par, k = st.product(name)
                    if st.dense[name] >= 2:
                        eng.wait_ge(dense_read, k - 1)
                    return bank_dense[par]

                def close(ins):
                    ins.then_inc(dense_done, 1)

                def split_product(out, pairs):
                    terms = [(a[i], m[j]) for a, m in pairs for i, j in ((0, 0), (0, 1), (1, 0))]
                    for n, (a, m) in enumerate(terms):
                        last = eng.matmul(out, a, m, start=(n == 0), stop=(n == len(terms) - 1),
                                          skip_group_check=True)
                    return last

                def split_rows(bank_, out, pairs, first):
                    terms = [(a[i], m[j]) for a, m in pairs for i, j in ((0, 0), (0, 1), (1, 0))]
                    for n, (a, m) in enumerate(terms):
                        last = eng.matmul(out, a, m, start=(first and n == 0), stop=(n == len(terms) - 1),
                                          skip_group_check=True)
                    return last

                def conv(st, j):
                    if j == 0:
                        eng.wait_ge(x_loaded[(st.b + 1) % 2], st.turn(3, 32, 32))
                    ps = open_bank(st, f"conv{j}")
                    xs = x_in[(st.b + 1) % 2]
                    for t in range(NT):
                        n = min(BAND, S - t * P)
                        kk = sh.T_in[t]
                        last = eng.matmul(ps[:, t * P:t * P + n], xs[0:kk, t, j * P:(j + 1) * P],
                                          band[0:kk, 0:n], start=(t == 0), stop=(t == NT - 1),
                                          skip_group_check=True)
                    close(last)

                def by_token(st, name, tiles, lhs, rhs):
                    ps = open_bank(st, name)
                    for n, t in enumerate(tiles):
                        tok = slice(t * P, t * P + T[t])
                        last = split_rows(ps, ps[0:T[t], n * D:(n + 1) * D],
                                          [([lhs[0][:, k, tok], lhs[1][:, k, tok]],
                                            [rhs[0][:, k, :], rhs[1][:, k, :]]) for k in range(2)], n == 0)
                    close(last)

                def hid_rows(st, n):
                    if n == 0:
                        eng.wait_ge(dense_read, st.read_before("conv1"))
                    by_token(st, f"hid{n}", [(0, 1), (2,)][n], mixed, w_mix)

                def normed_T(st, j):
                    ps = open_bank(st, f"nT{j}")
                    if j == 0:
                        eng.wait_ge(normed_done, st.at(2, NT, NT))
                    for t in range(NT):
                        last = eng.transpose(ps[:, t * P:t * P + T[t]], normed[0:T[t], t, j * P:(j + 1) * P],
                                             ident[0:T[t], 0:T[t]])
                    close(last)

                def query_key(st, name, j, w):
                    ps = open_bank(st, f"{name}{j}")
                    if name == "q" and j == 0:
                        par, k = st.product("nT1")
                        eng.wait_ge(dense_read, k + 1)
                    src = nT[st.b % 2]
                    close(split_product(ps[:, 0:S], [([w[0][:, k, j * P:(j + 1) * P], w[1][:, k, j * P:(j + 1) * P]],
                                                      [src[0][:, k, :], src[1][:, k, :]]) for k in range(2)]))

                def values(st, n):
                    by_token(st, f"val{n}", [(0, 1), (2,)][n], nT[(st.b + 1) % 2], w_v)

                def out_rows_(st, n):
                    if n == 0:
                        eng.wait_ge(attn_done, st.at(-1, 2, 2))
                    ps = open_bank(st, f"out{n}")
                    for m, t in enumerate([(0, 1), (2,)][n]):
                        for k in range(2):
                            last = eng.matmul(ps[0:T[t], m * D:(m + 1) * D], attnT[:, k, t * P:t * P + T[t]],
                                              w_o[:, k, :], start=(m == 0 and k == 0), stop=(k == 1),
                                              skip_group_check=True)
                    close(last)

                def max_T(st, half, shift):
                    ps = open_bank(st, f"maxT{half}")
                    eng.wait_ge(max_taken, st.at(shift, GROUPS * UNITS, 2 * UNITS * (half + 1)))
                    for t in range(NT):
                        last = eng.transpose(ps[0:8, t * P:t * P + T[t]], neg_max[0:T[t], t, half, :],
                                             ident[0:T[t], 0:T[t]])
                    close(last)

                def scores_for_max(st, g, u):
                    n = g * UNITS + u
                    par = n % 2
                    if u == 0 and g % 2 == 0:
                        eng.wait_ge(rows_loaded[(st.b + 1) % 2][g // 2], st.turn(1, 192, 192))
                    if not (st.b + 1 == 0 and isinstance(st.i, int) and n < 2):
                        eng.wait_ge(max_taken, st.at(1, GROUPS * UNITS, n - 1))
                    ps = bank_max[par]
                    t, heads = MAX_UNITS[u]
                    q, k = q_rows[(st.b + 1) % 2], k_rows[(st.b + 1) % 2]
                    w = KEYS_OF[t]
                    c = g % 2
                    for m, j in enumerate(heads):
                        slot = 4 * (g // 2) + j
                        eng.matmul(ps[0:T[t], m * w:(m + 1) * w],
                                   q[64 * c:64 * c + ROWS, slot, t * P:t * P + T[t]],
                                   k[64 * c:64 * c + ROWS, slot, 0:w], start=(m == 0), stop=False,
                                   skip_group_check=True)
                    d = T[t]
                    dst = ps[0:d, 0:len(heads) * w].rearrange("q (m w) -> q m w", w=w)[:, :, t * P:t * P + d]
                    eng.matmul(dst, ident_bf[0:d, 0:d], causal[0:d, 0:len(heads), 0:d], start=False, stop=True,
                               skip_group_check=True).then_inc(max_scores, 1)

                def scores_for_exp(st, g, u):
                    n = g * UNITS + u
                    par = n % 2
                    if u == 0 and g % 2 == 0:
                        eng.wait_ge(max_loaded[st.b % 2][g // 2], st.turn(0, 64, 64))
                    if not (st.b == 0 and isinstance(st.i, int) and n < 2):
                        eng.wait_ge(exp_done, st.at(0, GROUPS * UNITS, n - 1))
                    ps = bank_exp[par]
                    t, heads = EXP_UNITS[u]
                    q, k = q_rows[st.b % 2], k_rows[st.b % 2]
                    w = CUT[t]
                    c = g % 2
                    for m, j in enumerate(heads):
                        slot = 4 * (g // 2) + j
                        last = eng.matmul(ps[0:T[t], m * w:(m + 1) * w],
                                          k[64 * c:64 * c + 64, slot, t * P:t * P + T[t]],
                                          q[64 * c:64 * c + 64, slot, t * P:S],
                                          start=(m == 0), stop=(m == len(heads) - 1), skip_group_check=True)
                    last.then_inc(exp_scores, 1)

                def products_with_values(st, g, shift, t):
                    par = (st.b + shift) % 2
                    e = g % 2
                    if g == 0 and t == 0:
                        eng.wait_ge(dense_read, st.read_before("val1"))
                    if t == 0 and not (st.b == 0 and isinstance(st.i, int) and g < 2):
                        eng.wait_ge(pv_read if e else even_kept, st.at(shift, 2, g // 2))
                    eng.wait_ge(probs_masked, st.at(shift, GROUPS * NT, g * NT + t + 1))
                    kk = T[t]
                    for j in range(4):
                        last = eng.matmul(bank_pv[e][32 * j:32 * j + 32, t * P:S],
                                          val[par][0:kk, t, 4 * (g // 2) + j, 32 * e:32 * e + 32],
                                          probs[g % 2][0:kk, j, OFF[t]:OFF[t] + CUT[t]],
                                          start=(t == 0), stop=(t == NT - 1),
                                          tile_position=(0, 32 * j), skip_group_check=True)
                    if t == NT - 1:
                        last.then_inc(pv_done, 1)

                def step(st):
                    for n in range(GROUPS * UNITS):
                        g, u = divmod(n, UNITS)
                        if st.maxima:
                            scores_for_max(st, g, u)
                        if st.attend:
                            scores_for_exp(st, g, u)
                        if st.front and n in (1, 2):
                            hid_rows(st, n - 1)
                        if n == 3 and st.attend:
                            max_T(st, 1, 0)
                        if 2 <= u < 2 + NT:
                            if g == 0 and st.finish:
                                products_with_values(st, 3, -1, u - 2)
                            if g > 0 and st.attend:
                                products_with_values(st, g - 1, 0, u - 2)
                        if st.maxima and n in (5, 26):
                            values(st, (5, 26).index(n))
                        if st.front and n in (7, 8):
                            normed_T(st, n - 7)
                        if st.front and n in (10, 11):
                            query_key(st, "q", n - 10, w_q)
                        if st.front and n in (12, 13):
                            query_key(st, "k", n - 12, w_k)
                        if n == 16 and st.maxima:
                            max_T(st, 0, 1)
                        if st.finish and n in (18, 19):
                            out_rows_(st, n - 18)
                        if st.mix and n in (23, 24):
                            conv(st, n - 23)
                run_steps(eng, step)

            @block.scalar
            def _(eng):
                def take_hi(st, name, dst, rows=P, bias=None):
                    par, k = st.product(name)
                    eng.wait_ge(dense_done, k + 1)
                    src = bank_dense[par][0:rows, 0:S]
                    if bias is None:
                        ins = eng.activation(dst, src, ACT.Copy)
                    else:
                        ins = eng.activation(dst, src, ACT.Identity, bias=bias)
                    ins.then_inc(dense_hi, 1)

                def keep_even(st, half):
                    if not (isinstance(st.i, int) and st.b == 0 and half == 0):
                        eng.wait_ge(pv_read, st.at(0, 2, half))
                    eng.wait_ge(pv_done, st.at(0, GROUPS, 2 * half + 1))
                    eng.activation(even_attn[:, :], bank_pv[0][:, 0:S], ACT.Copy, scale=strip_half[:, 0:1])
                    eng.activation(even_sum[:, :], bank_pv[0][:, 0:S], ACT.Copy, scale=strip_half[:, 1:2])\
                        .then_inc(even_kept, 1)

                def exps(st, g, u):
                    n = g * UNITS + u
                    if u == 0 and not (isinstance(st.i, int) and st.b == 0 and g < 2):
                        eng.wait_ge(pv_done, st.at(0, GROUPS, g - 1))
                    eng.wait_ge(exp_scores, st.at(0, GROUPS * UNITS, n + 1))
                    t, heads = EXP_UNITS[u]
                    w = CUT[t]
                    first = heads[0]
                    eng.activation(probs[g % 2][0:T[t], first:first + len(heads), OFF[t]:OFF[t] + w],
                                   bank_exp[n % 2][0:T[t], 0:len(heads) * w].rearrange("k (m w) -> k m w", w=w),
                                   ACT.Exp).then_inc(exp_done, 1)

                def step(st):
                    for n in range(GROUPS * UNITS):
                        g, u = divmod(n, UNITS)
                        if st.attend:
                            exps(st, g, u)
                        if n == 3 and st.attend:
                            take_hi(st, "maxT1", maxT[0][0:8, 1, :], 8)
                        if st.front and n in (7, 8):
                            take_hi(st, f"nT{n - 7}", nT[st.b % 2][0][:, n - 7, :])
                        if n in (12, 26) and st.attend:
                            keep_even(st, n // 14)
                        if st.front and n in (10, 11):
                            if n == 10:
                                if not (isinstance(st.i, int) and st.b == -2):
                                    for h in range(2):
                                        eng.wait_ge(rows_loaded[(st.b + 1) % 2][h], st.turn(1, 192, 192))
                            take_hi(st, f"q{n - 10}", q_flat[0][:, n - 10, :], bias=bias_q[:, n - 10:n - 9])
                        if st.front and n in (12, 13):
                            take_hi(st, f"k{n - 12}", k_flat[0][:, n - 12, :], bias=bias_k[:, n - 12:n - 11])
                        if n == 16 and st.maxima:
                            take_hi(st, "maxT0", maxT[0][0:8, 0, :], 8)
                        if st.mix and n in (23, 24):
                            take_hi(st, f"conv{n - 23}", mixed[0][:, n - 23, :])
                run_steps(eng, step)

            @block.vector
            def _(eng):
                HALF_1_AT, HALF_0_AT = (5, 10, 12, 13, 14, 15), (19, 21, 22, 23, 26, 27)
                HI = ["maxT1", "nT0", "nT1", "q0", "q1", "k0", "k1", "maxT0", "conv0", "conv1"]

                def take_lo(st, name, dst, hi, rows=P, bias=None):
                    par, k = st.product(name)
                    eng.wait_ge(dense_hi, st.hi_at + [m for m in HI if m in st.dense].index(name) + 1)
                    src = bank_dense[par][0:rows, 0:S]
                    if bias is None:
                        ins = eng.tensor_tensor(dst, src, hi.bitcast(F32), ALU.subtract)
                    else:
                        ins = eng.scalar_tensor_tensor(out=dst, in0=src, scalar=bias, in1=hi.bitcast(F32),
                                                       op0=ALU.add, op1=ALU.subtract)
                    ins.then_inc(dense_read, 1)

                def maxima(st, g, u):
                    n = g * UNITS + u
                    eng.wait_ge(max_scores, st.at(1, GROUPS * UNITS, n + 1))
                    t, heads = MAX_UNITS[u]
                    hf, e = g // 2, g % 2
                    w = KEYS_OF[t]
                    src = bank_max[n % 2][0:T[t], 0:len(heads) * w].rearrange("q (m w) -> q m w", w=w)
                    first = 4 * e + heads[0]
                    dst = neg_max[0:T[t], t, hf, first:first + len(heads)]
                    eng.tensor_reduce(dst, src, AX.X, ALU.max, negate=True).then_inc(max_taken, 1)

                def hid_out(st, n):
                    par, k = st.product(f"hid{n}")
                    if n == 0 and not (isinstance(st.i, int) and st.b < 0):
                        eng.wait_ge(resid_done, st.at(0, NT, NT))
                    eng.wait_ge(dense_done, k + 1)
                    for m, t in enumerate([(0, 1), (2,)][n]):
                        last = eng.tensor_tensor(hid[st.b % 2][0:T[t], t, :], bank_dense[par][0:T[t], m * D:(m + 1) * D],
                                                 bias_mix[0:T[t], :], ALU.add)
                    last.then_inc(dense_read, 1)

                def norm_stats(st):
                    _, k = st.product("hid1")
                    eng.wait_ge(dense_read, k + 1)
                    for t in range(NT):
                        eng.bn_stats(stats[0:T[t], t, :], hid[st.b % 2][0:T[t], t, :]).then_inc(s_stats, 1)
                    for t in range(NT):
                        wait_alone(eng, s_stats, st.at(2, NT, t + 1), passed_dve)
                        eng.bn_aggr(moments[0:T[t], t, :], stats[0:T[t], t, :]).then_inc(moments_done, 1)

                def norm(st):
                    eng.wait_ge(rstd_done, st.at(2, 1, 1))
                    for t in range(NT):
                        eng.tensor_scalar(normed[0:T[t], t, :], hid[st.b % 2][0:T[t], t, :],
                                          moments[0:T[t], t, 0:1], rstd[0:T[t], t:t + 1],
                                          ALU.subtract, ALU.mult).then_inc(normed_done, 1)

                def values(st, n):
                    par, k = st.product(f"val{n}")
                    eng.wait_ge(dense_done, k + 1)
                    for m, t in enumerate([(0, 1), (2,)][n]):
                        dst = val[(st.b + 1) % 2][0:T[t], t, :, :].rearrange("k a (q f) -> k a q f", q=4)[:, :, 0::3, :]
                        src = bank_dense[par][0:T[t], m * D:(m + 1) * D].rearrange("k (a e f) -> k a e f", e=2, f=16)
                        b = bias_v[0:T[t], :].rearrange("k (a e f) -> k a e f", e=2, f=16)
                        last = eng.tensor_tensor(dst, src, b, ALU.add)
                    last.then_inc(dense_read, 1)

                def out_sum(st, n):
                    if n == 0:
                        eng.wait_ge(resid_done, st.at(-1, NT, NT))
                        if not (isinstance(st.i, int) and st.b - 1 < 2):
                            eng.wait_ge(stored[(st.b - 1) % 2], st.turn(-3, 32, 32))
                    par, k = st.product(f"out{n}")
                    eng.wait_ge(dense_done, k + 1)
                    for m, t in enumerate([(0, 1), (2,)][n]):
                        last = eng.tensor_tensor(out_rows[(st.b - 1) % 2][0:T[t], t, :],
                                          bank_dense[par][0:T[t], m * D:(m + 1) * D],
                                          resid[(st.b - 1) % 2][0:T[t], t, :], ALU.add)
                    last.then_inc(dense_read, 1)

                def gather_sums(st, half, shift, piece):
                    if piece == 0:
                        eng.wait_ge(even_kept, st.at(shift, 2, half + 1))
                        eng.wait_ge(pv_done, st.at(shift, GROUPS, 2 * half + 2))
                        if not (isinstance(st.i, int) and st.b + shift == 0 and half == 0):
                            eng.wait_ge(attn_done, st.at(shift, 2, half))
                        eng.scalar_tensor_tensor(out=attn_raw[:, :], in0=bank_pv[1][:, 0:S], scalar=strip_half[:, 1:2],
                                                 in1=even_attn[:, :], op0=ALU.mult, op1=ALU.add)
                        eng.scalar_tensor_tensor(out=sums_swapped[:, :], in0=bank_pv[1][:, 0:S],
                                                 scalar=strip_half[:, 0:1], in1=even_sum[:, :],
                                                 op0=ALU.mult, op1=ALU.add).then_inc(pv_read, 1)
                    elif piece == 1:
                        wait_alone(eng, pv_read, st.at(shift, 2, half + 1), passed_dve)
                        eng.stream_shuffle(sums[:, :], sums_swapped[:, :], [(i + 16) % 32 for i in range(32)])\
                            .then_inc(sums_ready, 1)
                    else:
                        if piece == 2:
                            eng.wait_ge(sums_ready, st.at(shift, 2, half + 1))
                        cols = slice((piece - 2) * (S // 4), (piece - 1) * (S // 4))
                        eng.reciprocal(recip[:, cols], sums[:, cols]).then_inc(recip_done, 1)

                def step(st):
                    for n in range(GROUPS * UNITS):
                        g, u = divmod(n, UNITS)
                        if st.maxima:
                            maxima(st, g, u)
                        if st.front and n in (2, 3):
                            hid_out(st, n - 2)
                            if n == 3:
                                norm_stats(st)
                        if n == 4 and st.attend:
                            take_lo(st, "maxT1", maxT[1][0:8, 1, :], maxT[0][0:8, 1, :], 8)
                        if n == 5 and st.front:
                            norm(st)
                        if st.finish and n in HALF_1_AT:
                            gather_sums(st, 1, -1, HALF_1_AT.index(n))
                        if st.maxima and n in (6, 27):
                            values(st, (6, 27).index(n))
                        if st.front and n in (8, 9):
                            j = n - 8
                            take_lo(st, f"nT{j}", nT[st.b % 2][1][:, j, :], nT[st.b % 2][0][:, j, :])
                        if st.front and n in (11, 12):
                            j = n - 11
                            take_lo(st, f"q{j}", q_flat[1][:, j, :], q_flat[0][:, j, :], bias=bias_q[:, j:j + 1])
                        if st.front and n in (13, 14):
                            j = n - 13
                            take_lo(st, f"k{j}", k_flat[1][:, j, :], k_flat[0][:, j, :], bias=bias_k[:, j:j + 1])
                        if n == 17 and st.maxima:
                            take_lo(st, "maxT0", maxT[1][0:8, 0, :], maxT[0][0:8, 0, :], 8)
                        if st.attend and n in HALF_0_AT:
                            gather_sums(st, 0, 0, HALF_0_AT.index(n))
                        if st.finish and n in (19, 20):
                            out_sum(st, n - 19)
                        if st.mix and n in (24, 25):
                            j = n - 24
                            take_lo(st, f"conv{j}", mixed[1][:, j, :], mixed[0][:, j, :])

                hi_count = [0]
                FULL_HI = len(HI)

                def counted(st):
                    st.hi_at = hi_count[0] + st.i * (2 * FULL_HI)
                    step(st)
                    hi_count[0] += len([m for m in HI if m in st.dense])
                run_steps(eng, counted)

            @block.gpsimd
            def _(eng):
                def mask(st, g, t):
                    last_unit = (4, 6, 7)[t]
                    wait_alone(eng, exp_done, st.at(0, GROUPS * UNITS, g * UNITS + last_unit), passed_pool)
                    d = T[t]
                    blk = probs[g % 2][0:d, :, OFF[t]:OFF[t] + d]
                    eng.affine_select(out=blk, in_=blk, compare_op=ALU.is_ge, fill=0.0, base=0,
                                      pattern=[[0, 4], [1, d]], channel_multiplier=-1).then_inc(probs_masked, 1)

                def norm_scale(st):
                    wait_alone(eng, moments_done, st.at(2, NT, NT), passed_pool)
                    eng.tensor_scalar(var_eps[:, :], moments[:, :, 1], EPS, None, ALU.add).then_inc(var_done, 1)
                    eng.wait_ge(var_done, st.at(2, 1, 1))
                    eng.tensor_tensor(rstd[:, :], var_eps[:, :], minus_half[:, :], ALU.pow).then_inc(rstd_done, 1)

                def normalise(st, half, shift):
                    if shift == 0:
                        if st.finish:
                            _, k = st.product("out1")
                            eng.wait_ge(dense_read, k + 1)
                    elif 0 <= st.real - 2:
                        eng.wait_ge(dense_read, st.read_before("out1"))
                    eng.wait_ge(recip_done, st.at(shift, 8, 4 * half + 4))
                    eng.tensor_tensor(attnT[:, half, :], attn_raw[:, :], recip[:, :], ALU.mult).then_inc(attn_done, 1)

                def residual(st):
                    par = (st.b + 1) % 2
                    eng.wait_ge(dense_read, st.read_before("hid1"))
                    if st.finish:
                        _, k = st.product("out1")
                        eng.wait_ge(dense_read, k + 1)
                    for t in range(NT):
                        eng.tensor_tensor(resid[par][0:T[t], t, :], hid[par][0:T[t], t, :],
                                          bias_o[0:T[t], :], ALU.add).then_inc(resid_done, 1)

                def step(st):
                    if st.front:
                        norm_scale(st)
                    for g in range(GROUPS):
                        if st.attend:
                            for t in range(NT):
                                mask(st, g, t)
                        if g == 1 and st.finish:
                            normalise(st, 1, -1)
                        if g == 2 and st.maxima:
                            residual(st)
                    if st.attend:
                        normalise(st, 0, 0)
                run_steps(eng, step)

            @block.sync
            def _(eng):
                def load_x(st):
                    for shift in (3, 4, 5) if st.b == FIRST else (5,):
                        if isinstance(st.i, int) and st.b + shift + 2 * st.i >= B:
                            continue
                        par = (st.b + shift) % 2
                        if shift == 5:
                            _, k = st.product("conv1")
                            wait_alone(eng, dense_done, k + 1, passed_sp)
                        n = st.b + shift + 2 * st.i
                        full = P * (NT - 1)
                        eng.dma_start(x_in[par][:, 0:NT - 1, :],
                                      x[n, 0:full, :].rearrange("(t p) d -> p t d", p=P)).then_inc(x_loaded[par], 16)
                        eng.dma_start(x_in[par][0:sh.T_in[-1], NT - 1, :], x[n, full:, :])\
                            .then_inc(x_loaded[par], 16)

                def rows(st, half):
                    par = st.b % 2
                    if half == 0:
                        _, k = st.product("k1")
                        wait_alone(eng, dense_read, k + 1, passed_sp)
                    if st.attend:
                        eng.wait_ge(exp_done, st.at(0, GROUPS * UNITS, 2 * UNITS * (half + 1)))
                    for flat, dst, order in ((q_flat, q_rows, (0, 0, 1)), (k_flat, k_rows, (0, 1, 0))):
                        for c in range(2):
                            for n, part in enumerate(order):
                                eng.dma_start(dst[par][64 * c + 16 * n:64 * c + 16 * n + 16, 4 * half:4 * half + 4, :]
                                              .bitcast(F32),
                                              flat[part][64 * half:64 * half + 64, c, :].bitcast(F32)
                                              ).then_inc(rows_loaded[par][half], 16)

                def max_rows(st, half, shift):
                    par = (st.b + shift) % 2
                    _, k = st.product(f"maxT{half}")
                    eng.wait_ge(dense_read, k + 1)
                    for c in range(2):
                        for part in range(2):
                            row_ = 64 * c + ROWS + part
                            eng.dma_start(q_rows[par][row_:row_ + 1, 4 * half:4 * half + 4, :].bitcast(F32),
                                          maxT[part][4 * c:4 * c + 4, half, :].bitcast(F32)).then_inc(max_loaded[par][half], 16)

                def store(st):
                    n = st.b - 1 + 2 * st.i
                    par = (st.b - 1) % 2
                    full = P * (NT - 1)
                    _, k = st.product("out1")
                    wait_alone(eng, dense_read, k + 1, passed_sp)
                    eng.dma_start(h2_dram[n, 0:full, :].rearrange("(t p) d -> p t d", p=P),
                                  out_rows[par][:, 0:NT - 1, :]).then_inc(stored[par], 16)
                    eng.dma_start(h2_dram[n, full:, :], out_rows[par][0:T[-1], NT - 1, :]).then_inc(stored[par], 16)

                def step(st):
                    if st.attend:
                        max_rows(st, 1, 0)
                    if st.front:
                        rows(st, 0)
                    if st.maxima:
                        max_rows(st, 0, 1)
                    if st.finish:
                        store(st)
                    if st.mix:
                        load_x(st)
                    if st.front:
                        rows(st, 1)
                run_steps(eng, step)
                for par in range(2):
                    eng.wait_ge(stored[par], 32 * (B // 2))



def expert_phase(nc, sem, sh, h2_dram, out, router_w, wg_r, wu_r, wd_r, wg_s, wu_s, wd_s):
    S, D, NT, T, B, E = sh.S, sh.D, sh.NT, sh.T, sh.B, sh.E
    RC = sh.RC
    C = RC + sh.NS
    RING = 4
    TILES = [(0, 1), (2,)]
    FULL = P * (NT - 1)

    with ExitStack() as ctx:
        def sb(name, shape, dt=F32):
            return ctx.enter_context(nc.sbuf_tensor(name, shape, dt))

        bank = [ctx.enter_context(nc.psum_tensor(f"ebank{i}", [P, BANK], F32)) for i in range(8)]
        bank_gate, bank_up, bank_y, bank_prep = bank[0:2], bank[2:4], bank[4:6], bank[6:8]

        ident = sb("e_ident", [P, P])
        minus_half = sb("e_minus_half", [P, NT])
        expert_no = sb("expert_no", [P, NT, E])
        w_gate = [sb(f"w_gate_{s}", [P, 2, C, P], F32R) for s in ("hi", "lo")]
        w_up = [sb(f"w_up_{s}", [P, 2, C, P], F32R) for s in ("hi", "lo")]
        w_down = [sb(f"w_down_{s}", [P, C, D], F32R) for s in ("hi", "lo")]
        w_router = [sb(f"w_router_{s}", [P, 2, E], F32R) for s in ("hi", "lo")]
        raw_gate = sb("raw_gate", [P, 2, C, P])
        raw_up = sb("raw_up", [P, 2, C, P])
        raw_down = sb("raw_down", [P, C, D])
        raw_router = sb("raw_router", [P, 2, E])

        h2 = [sb(f"h2_{p}", [P, NT, D]) for p in range(2)]
        y_rows = [sb(f"y_rows{p}", [P, NT, D]) for p in range(2)]
        normed = sb("e_normed", [P, NT, D])
        stats = sb("e_stats", [P, NT, 6])
        moments = sb("e_moments", [P, NT, 2])
        var_eps = sb("e_var_eps", [P, NT])
        rstd = sb("e_rstd", [P, NT])
        nT = [[sb(f"e_normedT{p}_{s}", [P, 2, S], F32R) for s in ("hi", "lo")] for p in range(2)]
        logits = sb("logits", [P, NT, E])
        top = sb("top", [P, NT, 8])
        top_no = sb("top_no", [P, NT, 8], U32)
        top_nof = sb("top_nof", [P, NT, 2])
        shifted = sb("shifted", [P, NT, E])
        exps = sb("exps", [P, NT, E])
        chosen = sb("chosen", [P, NT, E])
        chosen2 = sb("chosen2", [P, NT, E])
        all_sum = sb("all_sum", [P, NT])
        top_sum = sb("top_sum", [P, NT])
        inv_sum = sb("inv_sum", [P, NT])
        comb = sb("comb", [P, NT, E])
        combT = sb("combT", [E, S])
        comb_all = [sb(f"comb_all{p}", [P, RC, S]) for p in range(2)]
        tanh = [sb(f"tanh{p}", [P, S]) for p in range(2)]
        gated = [sb(f"gated{p}", [P, S]) for p in range(2)]
        hidden = [sb(f"hidden{p}", [P, S]) for p in range(2)]
        weighted = [sb(f"weighted{p}", [P, S]) for p in range(2)]
        hid_hi = [sb(f"hid_hi{p}", [P, S], F32R) for p in range(RING)]
        hid_lo = [sb(f"hid_lo{p}", [P, S], F32R) for p in range(RING)]

        comb_dram = [nc.dram_tensor(f"comb_dram{p}", [E, S], F32, kind="Internal").ap() for p in range(2)]

        w_loaded = sem("w_loaded")
        passed_dve, passed_pool, passed_sp = (sem(f"e_passed_{e}") for e in ("dve", "pool", "sp"))
        e_zeroed = sem("e_zeroed")
        e_consts = sem("e_consts")
        w_chain = sem("w_chain")
        h2_loaded = [sem(f"h2_loaded{p}") for p in range(2)]
        comb_stored = [sem(f"comb_stored{p}") for p in range(2)]
        comb_loaded = [sem(f"comb_loaded{p}") for p in range(2)]
        y_stored = [sem(f"y_stored{p}") for p in range(2)]
        e_stats_done = sem("e_stats_done")
        e_moments_done = sem("e_moments_done")
        e_var_done = sem("e_var_done")
        e_rstd_done = sem("e_rstd_done")
        e_normed_done = sem("e_normed_done")
        prep_done = sem("prep_done")
        nT_hi_done = sem("nT_hi_done")
        prep_read = sem("prep_read")
        route = sem("route")
        route_exp = sem("route_exp")
        gate_done = sem("gate_done")
        up_done = sem("up_done")
        tanh_done = sem("tanh_done")
        gated_done = sem("gated_done")
        hidden_done = sem("hidden_done")
        weighted_done = sem("weighted_done")
        hi_done = sem("hi_done")
        lo_done = sem("lo_done")
        down_done = sem("down_done")
        h2_kept = sem("h2_kept")
        y_read = sem("y_read")

        with nc.Block() as block:
            @block.sync
            def _(eng):
                def load(dst, src):
                    eng.dma_start(dst, src).then_inc(w_loaded, 16)
                for raw_, routed, shared in ((raw_gate, wg_r, wg_s), (raw_up, wu_r, wu_s)):
                    for k in range(2):
                        for e2 in range(2):
                            load(raw_[:, k, 0:RC, sh.MR * e2:sh.MR * (e2 + 1)],
                                 routed.rearrange("(c e) (k p) m -> e k p c m", e=2, k=2)[e2, k])
                        load(raw_[:, k, RC:C, :], shared.rearrange("n (k p) m -> k p n m", k=2)[k])
                load(raw_down[:, 0:RC, :], wd_r.rearrange("(c e) m d -> (e m) c d", e=2))
                load(raw_down[:, RC:C, :], wd_s.rearrange("n m d -> m n d"))
                load(raw_router[:, :, :], router_w.rearrange("(k p) e -> p k e", k=2))

            @block.gpsimd
            def _(eng):
                eng.memset(ident[:, :], 0.0).then_inc(e_zeroed, 1)
                eng.wait_ge(e_zeroed, 1)
                eng.affine_select(out=ident[:, :], in_=ident[:, :], compare_op=ALU.not_equal, fill=1.0,
                                  base=0, pattern=[[-1, P]], channel_multiplier=1)
                eng.memset(minus_half[:, :], -0.5)
                eng.memset(moments[:, :, :], 1.0)
                eng.memset(logits[:, :, :], 0.0)
                eng.iota(expert_no[:, :, :], pattern=[[0, NT], [1, E]], base=0, channel_multiplier=0,
                         allow_small_or_imprecise_dtypes=True).then_inc(e_consts, 1)

            @block.vector
            def _(eng):
                eng.wait_ge(w_loaded, 16 * 15)
                n = 0
                for full, (hi, lo) in ((raw_gate, w_gate), (raw_up, w_up), (raw_down, w_down),
                                       (raw_router, w_router)):
                    n += 1
                    if len(full.shape) == 4:
                        full, hi, lo = (a[:, :, :, :] for a in (full, hi, lo))
                    else:
                        full, hi, lo = (a[:, :, :] for a in (full, hi, lo))
                    eng.tensor_copy(hi, full).then_inc(w_chain, 1)
                    eng.wait_ge(w_chain, n)
                    eng.tensor_tensor(lo, full, hi.bitcast(F32), ALU.subtract)

        LOOPS = (B - 2) // 2

        class Step:
            def __init__(self, n, i):
                self.n, self.i = n, i
                real = n + 2 * i if isinstance(i, int) else n
                self.prep = real + 1 < B
                self.experts = 0 <= real < B
                self.finish = real >= 1 or not isinstance(i, int)
                self.load = not isinstance(i, int) or real + 3 < B

            def at(self, shift, per, c):
                return (self.n + shift) * per + c + self.i * (2 * per)

            def turn(self, shift, per, c=0):
                return ((self.n + shift) // 2) * per + c + self.i * per

            def early(self, n):
                return isinstance(self.i, int) and self.i == 0 and self.n < n

        def run_steps(eng, step_fn):
            step_fn(Step(-1, 0))
            step_fn(Step(0, 0))
            step_fn(Step(1, 0))
            with eng.Fori(1, LOOPS - 1) as i:
                step_fn(Step(0, i))
                step_fn(Step(1, i))
            for i in (LOOPS - 1, LOOPS):
                step_fn(Step(0, i))
                step_fn(Step(1, i))
            step_fn(Step(2, LOOPS))

        ROUTE = 13

        def weights_of(c):
            return RC + c if c < sh.NS else c - sh.NS

        def ring(parts, n, c):
            return parts[(n * C + c) % RING]

        with nc.Block() as block:

            @block.tensor
            def _(eng):
                def split3(out, pairs, first):
                    terms = [(a[i], m[j]) for a, m in pairs for i, j in ((0, 0), (0, 1), (1, 0))]
                    for n, (a, m) in enumerate(terms):
                        last = eng.matmul(out, a, m, start=(first and n == 0), stop=(n == len(terms) - 1),
                                          skip_group_check=True)
                    return last

                def open_prep(st, c):
                    if not (st.n == -1 and c < 2):
                        eng.wait_ge(prep_read, st.at(1, 4, c - 1))

                def normed_T(st):
                    for j in range(2):
                        open_prep(st, j)
                        if j == 0:
                            eng.wait_ge(e_normed_done, st.at(1, NT, NT))
                        for t in range(NT):
                            last = eng.transpose(bank_prep[j][:, t * P:t * P + T[t]],
                                                 normed[0:T[t], t, j * P:(j + 1) * P], ident[0:T[t], 0:T[t]])
                        last.then_inc(prep_done, 1)

                def router(st):
                    eng.wait_ge(prep_read, st.at(1, 4, 2))
                    src = nT[(st.n + 1) % 2]
                    for t in range(NT):
                        tok = slice(t * P, t * P + T[t])
                        last = split3(bank_prep[0][0:T[t], t * E:(t + 1) * E],
                                      [([src[0][:, k, tok], src[1][:, k, tok]],
                                        [w_router[0][:, k, :], w_router[1][:, k, :]]) for k in range(2)], t == 0)
                    last.then_inc(prep_done, 1)

                def comb_T(st):
                    open_prep(st, 3)
                    eng.wait_ge(route, st.at(1, ROUTE, ROUTE))
                    for t in range(NT):
                        last = eng.transpose(bank_prep[1][0:E, t * P:t * P + T[t]], comb[0:T[t], t, :],
                                             ident[0:T[t], 0:T[t]])
                    last.then_inc(prep_done, 1)

                def gate_up(st, c):
                    src = nT[st.n % 2]
                    if not (st.early(1) and c < 2):
                        eng.wait_ge(hidden_done, st.at(0, C, c - 1))
                    for w, ps, done in ((w_gate, bank_gate, gate_done), (w_up, bank_up, up_done)):
                        split3(ps[c % 2][:, 0:S], [([w[0][:, k, weights_of(c), :], w[1][:, k, weights_of(c), :]],
                                                    [src[0][:, k, :], src[1][:, k, :]]) for k in range(2)],
                               True).then_inc(done, 1)

                def down(st, shift, c):
                    if c == 0 and not st.early(1):
                        eng.wait_ge(y_read, st.at(0, 1, 0))
                    eng.wait_ge(lo_done, st.at(shift, C, c + 1))
                    hi, lo = ring(hid_hi, st.n + shift, c), ring(hid_lo, st.n + shift, c)
                    for b, tiles in enumerate(TILES):
                        for m, t in enumerate(tiles):
                            tok = slice(t * P, t * P + T[t])
                            last = split3(bank_y[b][0:T[t], m * D:(m + 1) * D],
                                          [([hi[:, tok], lo[:, tok]],
                                            [w_down[0][:, weights_of(c), :], w_down[1][:, weights_of(c), :]])],
                                          c == 0 and m == 0)
                    last.then_inc(down_done, 1)

                def step(st):
                    for c in range(C):
                        if st.experts:
                            gate_up(st, c)
                        if c >= 2 and st.experts:
                            down(st, 0, c - 2)
                        if c < 2 and st.finish:
                            down(st, -1, C - 2 + c)
                        if st.prep:
                            if c == 3:
                                normed_T(st)
                            if c == 5:
                                router(st)
                            if c == 8:
                                comb_T(st)
                run_steps(eng, step)

            @block.scalar
            def _(eng):
                def tanh_of(st, c):
                    if not (st.early(1) and c < 2):
                        eng.wait_ge(gated_done, st.at(0, C, c - 1))
                    eng.wait_ge(gate_done, st.at(0, C, c + 1))
                    eng.activation(tanh[c % 2][:, :], bank_gate[c % 2][:, 0:S], ACT.Tanh, scale=0.5)\
                        .then_inc(tanh_done, 1)

                def hi_of(st, shift, c):
                    if not (st.early(1) and c < RING):
                        eng.wait_ge(down_done, st.at(shift, C, c + 1 - RING))
                    if c < sh.NS:
                        eng.wait_ge(hidden_done, st.at(shift, C, c + 1))
                        src = hidden[c % 2]
                    else:
                        eng.wait_ge(weighted_done, st.at(shift, RC, c - sh.NS + 1))
                        src = weighted[c % 2]
                    eng.activation(ring(hid_hi, st.n + shift, c)[:, :], src[:, :], ACT.Copy).then_inc(hi_done, 1)

                def keep_h2(st):
                    par = (st.n + 1) % 2
                    eng.wait_ge(h2_loaded[par], st.turn(1, 32, 32))
                    if not st.early(1):
                        eng.wait_ge(y_stored[par], st.turn(-1, 32, 32))
                    eng.activation(y_rows[par][:, 0:NT - 1, :], h2[par][:, 0:NT - 1, :], ACT.Copy)
                    eng.activation(y_rows[par][0:T[-1], NT - 1, :], h2[par][0:T[-1], NT - 1, :], ACT.Copy)\
                        .then_inc(h2_kept, 1)

                def step(st):
                    for c in range(C):
                        if st.experts:
                            tanh_of(st, c)
                        if c == 0 and st.finish:
                            hi_of(st, -1, C - 1)
                        if c >= 1 and st.experts:
                            hi_of(st, 0, c - 1)
                        if st.prep:
                            if c == 3:
                                for j in range(2):
                                    eng.wait_ge(prep_done, st.at(1, 4, j + 1))
                                    eng.activation(nT[(st.n + 1) % 2][0][:, j, :], bank_prep[j][:, 0:S], ACT.Copy)\
                                        .then_inc(nT_hi_done, 1)
                            if c == 5:
                                keep_h2(st)
                            if c == 6:
                                eng.wait_ge(route, st.at(1, ROUTE, 4))
                                eng.activation(exps[:, :, :], shifted[:, :, :], ACT.Exp).then_inc(route_exp, 1)
                run_steps(eng, step)

            @block.vector
            def _(eng):
                def gate_times_up(st, c):
                    k = c - 2 if c >= 2 else C - 2 + c
                    if k >= sh.NS and not (st.early(1) and c < 2):
                        eng.wait_ge(weighted_done, st.at(0 if c >= 2 else -1, RC, k - sh.NS + 1))
                    eng.wait_ge(tanh_done, st.at(0, C, c + 1))
                    eng.scalar_tensor_tensor(out=gated[c % 2][:, :], in0=tanh[c % 2][:, :], scalar=1.0,
                                             in1=bank_gate[c % 2][:, 0:S], op0=ALU.add, op1=ALU.mult)\
                        .then_inc(gated_done, 1)
                    eng.wait_ge(up_done, st.at(0, C, c + 1))
                    eng.wait_ge(gated_done, st.at(0, C, c + 1))
                    eng.scalar_tensor_tensor(out=hidden[c % 2][:, :], in0=gated[c % 2][:, :], scalar=0.5,
                                             in1=bank_up[c % 2][:, 0:S], op0=ALU.mult, op1=ALU.mult)\
                        .then_inc(hidden_done, 1)

                def norm_stats(st):
                    par = (st.n + 1) % 2
                    eng.wait_ge(h2_loaded[par], st.turn(1, 32, 32))
                    for t in range(NT):
                        eng.bn_stats(stats[0:T[t], t, :], h2[par][0:T[t], t, :]).then_inc(e_stats_done, 1)
                    for t in range(NT):
                        wait_alone(eng, e_stats_done, st.at(1, NT, t + 1), passed_dve)
                        eng.bn_aggr(moments[0:T[t], t, :], stats[0:T[t], t, :]).then_inc(e_moments_done, 1)

                def norm(st):
                    eng.wait_ge(e_rstd_done, st.at(1, 1, 1))
                    for t in range(NT):
                        eng.tensor_scalar(normed[0:T[t], t, :], h2[(st.n + 1) % 2][0:T[t], t, :],
                                          moments[0:T[t], t, 0:1], rstd[0:T[t], t:t + 1],
                                          ALU.subtract, ALU.mult).then_inc(e_normed_done, 1)

                def routing(st, part):
                    count = [0]

                    def link(ins):
                        ins.then_inc(route, 1)
                        count[0] += 1
                        wait_alone(eng, route, st.at(1, ROUTE, part[1] + count[0]), passed_dve)

                    if part[0] == 0:
                        eng.wait_ge(prep_done, st.at(1, 4, 3))
                        eng.tensor_copy(logits[:, 0:NT - 1, :],
                                        bank_prep[0][:, 0:(NT - 1) * E].rearrange("p (t e) -> p t e", e=E))
                        eng.tensor_copy(logits[0:T[-1], NT - 1, :], bank_prep[0][0:T[-1], (NT - 1) * E:NT * E])\
                            .then_inc(prep_read, 1)
                        wait_alone(eng, prep_read, st.at(1, 4, 3), passed_dve)
                        for t in range(NT):
                            ins = eng.max(top[:, t, :], logits[:, t, :])
                        link(ins)
                        for t in range(NT):
                            ins = eng.max_index(top_no[:, t, :], top[:, t, :], logits[:, t, :])
                        link(ins)
                        link(eng.tensor_copy(top_nof[:, :, :], top_no[:, :, 0:2]))
                        link(eng.tensor_tensor(shifted[:, :, :], logits[:, :, :],
                                               top[:, :, 0:1].broadcast_to([P, NT, E]), ALU.subtract))
                        link(eng.tensor_tensor(chosen[:, :, :], expert_no[:, :, :],
                                               top_nof[:, :, 0:1].broadcast_to([P, NT, E]), ALU.is_equal))
                        link(eng.tensor_tensor(chosen2[:, :, :], expert_no[:, :, :],
                                               top_nof[:, :, 1:2].broadcast_to([P, NT, E]), ALU.is_equal))
                        link(eng.tensor_tensor(chosen[:, :, :], chosen[:, :, :], chosen2[:, :, :], ALU.add))
                    else:
                        eng.wait_ge(route_exp, st.at(1, 1, 1))
                        link(eng.tensor_reduce(all_sum[:, :], exps[:, :, :], AX.X, ALU.add))
                        link(eng.tensor_tensor(chosen[:, :, :], chosen[:, :, :], exps[:, :, :], ALU.mult))
                        link(eng.tensor_reduce(top_sum[:, :], chosen[:, :, :], AX.X, ALU.add))
                        link(eng.scalar_tensor_tensor(out=top_sum[:, :], in0=all_sum[:, :], scalar=1e-9,
                                                      in1=top_sum[:, :], op0=ALU.mult, op1=ALU.add))
                        link(eng.reciprocal(inv_sum[:, :], top_sum[:, :]))
                        link(eng.tensor_tensor(comb[:, :, :], chosen[:, :, :],
                                               inv_sum[:, :].rearrange("p (t a) -> p t a", a=1)
                                               .broadcast_to([P, NT, E]), ALU.mult))

                def lo_of(st, shift, c):
                    eng.wait_ge(hi_done, st.at(shift, C, c + 1))
                    src = hidden[c % 2] if c < sh.NS else weighted[c % 2]
                    eng.tensor_tensor(ring(hid_lo, st.n + shift, c)[:, :], src[:, :],
                                      ring(hid_hi, st.n + shift, c)[:, :].bitcast(F32), ALU.subtract)\
                        .then_inc(lo_done, 1)

                def result(st):
                    eng.wait_ge(h2_kept, st.at(-1, 1, 1))
                    eng.wait_ge(down_done, st.at(-1, C, C))
                    rows = y_rows[(st.n - 1) % 2]
                    for b, tiles in enumerate(TILES):
                        for m, t in enumerate(tiles):
                            ins = eng.tensor_tensor(rows[0:T[t], t, :], bank_y[b][0:T[t], m * D:(m + 1) * D],
                                                    rows[0:T[t], t, :], ALU.add)
                    ins.then_inc(y_read, 1)

                def step(st):
                    for c in range(C):
                        if st.experts:
                            gate_times_up(st, c)
                        if c == 0 and st.finish:
                            lo_of(st, -1, C - 1)
                        if c >= 1 and st.experts:
                            lo_of(st, 0, c - 1)
                        if c == 1 and st.finish:
                            result(st)
                        if st.prep:
                            if c == 0:
                                norm_stats(st)
                            if c == 1:
                                norm(st)
                            if c == 3:
                                for j in range(2):
                                    eng.wait_ge(nT_hi_done, st.at(1, 2, j + 1))
                                    dst = nT[(st.n + 1) % 2]
                                    eng.tensor_tensor(dst[1][:, j, :], bank_prep[j][:, 0:S],
                                                      dst[0][:, j, :].bitcast(F32), ALU.subtract)\
                                        .then_inc(prep_read, 1)
                            if c == 5:
                                routing(st, (0, 0))
                            if c == 7:
                                routing(st, (1, 7))
                            if c == 8:
                                eng.wait_ge(prep_done, st.at(1, 4, 4))
                                eng.tensor_copy(combT[:, :], bank_prep[1][0:E, 0:S]).then_inc(prep_read, 1)
                run_steps(eng, step)

            @block.gpsimd
            def _(eng):
                def norm_scale(st):
                    wait_alone(eng, e_moments_done, st.at(1, NT, NT), passed_pool)
                    eng.tensor_scalar(var_eps[:, :], moments[:, :, 1], EPS, None, ALU.add).then_inc(e_var_done, 1)
                    eng.wait_ge(e_var_done, st.at(1, 1, 1))
                    eng.tensor_tensor(rstd[:, :], var_eps[:, :], minus_half[:, :], ALU.pow).then_inc(e_rstd_done, 1)

                def weigh(st, c):
                    eng.wait_ge(lo_done, st.at(0, C, c - 1))
                    wait_alone(eng, hidden_done, st.at(0, C, c + 1), passed_pool)
                    if c == sh.NS:
                        eng.wait_ge(comb_loaded[st.n % 2], st.turn(0, 32, 32))
                    eng.tensor_tensor(weighted[c % 2][:, :], hidden[c % 2][:, :],
                                      comb_all[st.n % 2][:, c - sh.NS, :], ALU.mult).then_inc(weighted_done, 1)

                def step(st):
                    if st.prep:
                        norm_scale(st)
                    if st.experts:
                        for c in range(sh.NS, C):
                            weigh(st, c)
                run_steps(eng, step)

            @block.sync
            def _(eng):
                def load_h2(par, n):
                    eng.dma_start(h2[par][:, 0:NT - 1, :],
                                  h2_dram[n, 0:FULL, :].rearrange("(t p) d -> p t d", p=P)).then_inc(h2_loaded[par], 16)
                    eng.dma_start(h2[par][0:T[-1], NT - 1, :], h2_dram[n, FULL:, :]).then_inc(h2_loaded[par], 16)

                def step(st):
                    if st.n == -1:
                        load_h2(0, 0)
                        load_h2(1, 1)
                    if st.finish:
                        n = st.n - 1 + 2 * st.i
                        rows = y_rows[(st.n - 1) % 2]
                        wait_alone(eng, y_read, st.at(-1, 1, 1), passed_sp)
                        eng.dma_start(out[n, 0:FULL, :].rearrange("(t p) d -> p t d", p=P),
                                      rows[:, 0:NT - 1, :]).then_inc(y_stored[(st.n - 1) % 2], 16)
                        eng.dma_start(out[n, FULL:, :], rows[0:T[-1], NT - 1, :])\
                            .then_inc(y_stored[(st.n - 1) % 2], 16)
                    if st.prep:
                        par = (st.n + 1) % 2
                        if st.load:
                            wait_alone(eng, h2_kept, st.at(1, 1, 1), passed_sp)
                            wait_alone(eng, e_normed_done, st.at(1, NT, NT), passed_sp)
                            load_h2(par, st.n + 3 + 2 * st.i)
                        eng.wait_ge(prep_read, st.at(1, 4, 4))
                        eng.dma_start(comb_dram[par], combT[:, :]).then_inc(comb_stored[par], 16)
                        wait_alone(eng, comb_stored[par], st.turn(1, 16, 16), passed_sp)
                        if not st.early(1):
                            eng.wait_ge(weighted_done, st.at(-1, RC, RC))
                        for e2 in range(2):
                            eng.dma_start(comb_all[par][64 * e2:64 * e2 + 64, :, :],
                                          bass.AP(comb_dram[par].tensor, e2 * S, [[0, 64], [2 * S, RC], [1, S]]))\
                                .then_inc(comb_loaded[par], 16)
                run_steps(eng, step)
                for par in range(2):
                    eng.wait_ge(y_stored[par], 32 * (B // 2))


def audio_tower(nc, x, tok_Wv, tok_bv, tok_Wo, tok_bo, decay_w, wq, bq, wk, bk, wv, bv, wo, bo,
                router_w, wg_r, wu_r, wd_r, wg_s, wu_s, wd_s, out):
    sh = Shapes(x, decay_w, wg_r, wg_s)
    h2_dram = nc.dram_tensor("h2_dram", [sh.B, sh.S, sh.D], F32, kind="Internal").ap()
    with ExitStack() as ctx:
        def sem(name):
            return ctx.enter_context(nc.semaphore(name))

        attention_phase(nc, sem, sh, h2_dram, x, tok_Wv, tok_bv, tok_Wo, tok_bo, decay_w,
                        wq, bq, wk, bk, wv, bv, wo, bo)
        expert_phase(nc, sem, sh, h2_dram, out, router_w, wg_r, wu_r, wd_r, wg_s, wu_s, wd_s)


_INS = ['x', 'L0_tok_Wv', 'L0_tok_bv', 'L0_tok_Wo', 'L0_tok_bo', 'L0_tok_decay_w', 'L0_attn_wq', 'L0_attn_bq',
        'L0_attn_wk', 'L0_attn_bk', 'L0_attn_wv', 'L0_attn_bv', 'L0_attn_wo', 'L0_attn_bo', 'L0_ffn_router_w',
        'L0_ffn_wg_r', 'L0_ffn_wu_r', 'L0_ffn_wd_r', 'L0_ffn_wg_s', 'L0_ffn_wu_s', 'L0_ffn_wd_s']


def kernel(**inputs):
    import numpy as _np
    import concourse.bacc as _bacc
    from concourse import mybir as _mybir
    from concourse.bass_utils import run_bass_kernel_spmd as _run

    nc = _bacc.Bacc("TRN2", target_bir_lowering=False, num_devices=1)
    arrays, args = {}, []
    for name in _INS:
        a = _np.ascontiguousarray(inputs[name])
        arrays[f"in_{name}_dram"] = a
        args.append(nc.dram_tensor(f"in_{name}_dram", a.shape, _mybir.dt.from_np(a.dtype), kind="ExternalInput").ap())
    batch, tokens, dim = inputs["x"].shape
    out = nc.dram_tensor("out_0_dram", (batch, tokens + 1, dim), F32, kind="ExternalOutput").ap()
    audio_tower(nc, *args, out)
    r = _run(nc, [arrays], core_ids=[0])
    return r.results[0]["out_0_dram"]
```

```python
from contextlib import ExitStack

import concourse.bass as bass
from concourse import mybir

F32 = mybir.dt.float32
F32R = mybir.dt.float32r
BF16 = mybir.dt.bfloat16
U32 = mybir.dt.uint32
ALU = mybir.AluOpType
ACT = mybir.ActivationFunctionType
AX = mybir.AxisListType

P = 128
BANK = 512
EPS = 1e-5
MASKED = -3.0e38


class Shapes:

    def __init__(self, x, decay_w, wg_r, wg_s):
        self.B, self.S_in, self.D = x.shape
        self.TAPS = decay_w.shape[0]
        self.S = self.S_in + 1
        self.KC = self.D // P
        self.H = 16
        self.HD = self.D // self.H
        self.NT = -(-self.S // P)
        self.T = [min(P, self.S - P * t) for t in range(self.NT)]
        self.T_in = [min(P, self.S_in - P * t) for t in range(self.NT)]
        self.E = wg_r.shape[0]
        self.MR = wg_r.shape[2]
        self.NS = wg_s.shape[0]
        self.RC = self.E * self.MR // P
        assert (self.D, self.NT, self.KC, self.HD, self.TAPS) == (256, 3, 2, 16, 32)
        assert self.E * self.MR == 8 * P and self.NS == 2 and wg_s.shape[2] == P


def wait_alone(eng, semaphore, value, passed):
    eng.wait_ge(semaphore, value)
    eng.sem_inc(passed, 1)


class ExpertWeights:

    def __init__(self, sh, sb, sem, router_w, wg_r, wu_r, wd_r, wg_s, wu_s, wd_s):
        self.sh = sh
        C = sh.RC + sh.NS
        self.gate = sb("raw_gate", [P, 2, C, P])
        self.up = sb("raw_up", [P, 2, C, P])
        self.down = sb("raw_down", [P, C, sh.D])
        self.router = sb("raw_router", [P, 2, sh.E])
        self.loaded = {name: sem(f"{name}_weights_loaded") for name in ("router", "gate", "up", "down")}
        self.LOADS = {"router": 16, "gate": 96, "up": 96, "down": 32}
        self.sources = router_w, wg_r, wu_r, wd_r, wg_s, wu_s, wd_s

    def load(self, eng, name):
        sh, RC, C = self.sh, self.sh.RC, self.sh.RC + self.sh.NS
        router_w, wg_r, wu_r, wd_r, wg_s, wu_s, wd_s = self.sources

        def one(dst, src):
            eng.dma_start(dst, src).then_inc(self.loaded[name], 16)
        if name in ("gate", "up"):
            raw_, routed, common = (self.gate, wg_r, wg_s) if name == "gate" else (self.up, wu_r, wu_s)
            for k in range(2):
                for e2 in range(2):
                    one(raw_[:, k, 0:RC, sh.MR * e2:sh.MR * (e2 + 1)],
                        routed.rearrange("(c e) (k p) m -> e k p c m", e=2, k=2)[e2, k])
                one(raw_[:, k, RC:C, :], common.rearrange("n (k p) m -> k p n m", k=2)[k])
        elif name == "down":
            one(self.down[:, 0:RC, :], wd_r.rearrange("(c e) m d -> (e m) c d", e=2))
            one(self.down[:, RC:C, :], wd_s.rearrange("n m d -> m n d"))
        else:
            one(self.router[:, :, :], router_w.rearrange("(k p) e -> p k e", k=2))


def attention_phase(nc, sem, sh, front, experts, h2_dram, x, tok_Wv, tok_bv, tok_Wo, tok_bo, decay_w,
                    wq, bq, wk, bk, wv, bv, wo, bo):
    S, D, NT, T, B = sh.S, sh.D, sh.NT, sh.T, sh.B
    BAND = P + sh.TAPS
    GROUPS, UNITS = 4, 7
    CUT = [S - P * t for t in range(NT)]
    OFF = [0, CUT[0], CUT[0] + CUT[1]]
    PW = sum(CUT)
    ROWS = 3 * sh.HD

    with ExitStack() as ctx:
        def sb(name, shape, dt=F32):
            return ctx.enter_context(nc.sbuf_tensor(name, shape, dt))

        bank = [ctx.enter_context(nc.psum_tensor(f"bank{i}", [P, BANK], F32)) for i in range(8)]
        bank_max, bank_exp = bank[0:2], bank[2:4]
        bank_pv = bank[4:6]
        bank_dense = bank[6:8]

        ident = sb("ident", [P, P])
        ident_bf = sb("ident_bf", [P, P], BF16)
        causal = sb("causal", [P, 4, P], BF16)
        band = sb("band", [P, BAND])
        strip_half = sb("strip_half", [P, 2])
        minus_half = sb("minus_half", [P, NT])
        w_mix = [sb(f"w_mix_{s}", [P, 2, D], F32R) for s in ("hi", "lo")]
        w_q = [sb(f"w_q_{s}", [P, 2, D], F32R) for s in ("hi", "lo")]
        w_k = [sb(f"w_k_{s}", [P, 2, D], F32R) for s in ("hi", "lo")]
        w_v = [sb(f"w_v_{s}", [P, 2, D], F32R) for s in ("hi", "lo")]
        w_o = sb("w_o", [P, 2, D])
        bias_mix = sb("bias_mix", [P, D])
        bias_v = sb("bias_v", [P, D])
        bias_o = sb("bias_o", [P, D])
        bias_q = sb("bias_q", [P, 2])
        bias_k = sb("bias_k", [P, 2])

        x_in = [sb(f"x_in{p}", [P, NT, D]) for p in range(2)]
        q_flat, k_flat, mixed, *nT = front
        hid = [sb(f"hid{p}", [P, NT, D]) for p in range(2)]
        resid = [sb(f"resid{p}", [P, NT, D]) for p in range(2)]
        out_rows = [sb(f"out_rows{p}", [P, NT, D]) for p in range(2)]
        normed = sb("normed", [P, NT, D])
        stats = sb("stats", [P, NT, 6])
        moments = sb("moments", [P, NT, 2])
        var_eps = sb("var_eps", [P, NT])
        rstd = sb("rstd", [P, NT])
        q_rows = [sb(f"q_rows{p}", [P, 8, S], F32R) for p in range(2)]
        k_rows = [sb(f"k_rows{p}", [P, 8, S], F32R) for p in range(2)]
        val = [sb(f"val{p}", [P, NT, 8, 64]) for p in range(2)]
        neg_max = sb("neg_max", [P, NT, 2, 8])
        maxT = [sb(f"maxT_{s}", [8, 2, S], F32R) for s in ("hi", "lo")]
        probs = [sb(f"probs{p}", [P, 4, PW]) for p in range(2)]
        attn_of = [sb(f"attn_of_{e}", [P, S]) for e in ("even", "odd")]
        sum_of = [sb(f"sum_of_{e}", [P, S]) for e in ("even", "odd")]
        attn_raw = sb("attn_raw", [P, S])
        sums_swapped = sb("sums_swapped", [P, S])
        sums = sb("sums", [P, S])
        recip = sb("recip", [P, S])
        attnT = sb("attnT", [P, 2, S])

        passed_dve, passed_pool, passed_sp = (sem(f"passed_{e}") for e in ("dve", "pool", "sp"))
        x_loaded = [sem(f"x_loaded{p}") for p in range(2)]
        rows_loaded = [[sem(f"rows_loaded{p}_{h}") for h in range(2)] for p in range(2)]
        max_loaded = [[sem(f"max_loaded{p}_{h}") for h in range(2)] for p in range(2)]
        stored = [sem(f"stored{p}") for p in range(2)]
        dense_done = sem("dense_done")
        dense_hi = sem("dense_hi")
        dense_read = sem("dense_read")
        moments_done = sem("moments_done")
        s_stats = sem("s_stats")
        var_done = sem("var_done")
        rstd_done = sem("rstd_done")
        normed_done = sem("normed_done")
        resid_done = sem("resid_done")
        max_scores = sem("max_scores")
        max_taken = sem("max_taken")
        exp_scores = sem("exp_scores")
        exp_done = sem("exp_done")
        probs_masked = sem("probs_masked")
        pv_done = sem("pv_done")
        even_kept = sem("even_kept")
        odd_kept = sem("odd_kept")
        joined = sem("joined")
        sums_ready = sem("sums_ready")
        recip_done = sem("recip_done")
        attn_done = sem("attn_done")

        flat0 = probs[0][:, :, :].rearrange("p a b -> p (a b)")
        flat1 = probs[1][:, :, :].rearrange("p a b -> p (a b)")
        raw = {n: flat0[:, 512 * i:512 * (i + 1)].rearrange("p (k d) -> p k d", k=2)
               for i, n in enumerate(("wq", "wk", "wv", "tv", "to"))}
        perm = {n: flat1[:, 512 * i:512 * (i + 1)].rearrange("p (k d) -> p k d", k=2)
                for i, n in enumerate(("wq", "wk"))}
        toT = flat1[:, 1024:1536].rearrange("p (k d) -> p k d", k=2)
        bvb = flat1[:, 2048:2304].rearrange("p (k m) -> p k m", k=2)
        row = flat1[0:1, 2304:2304 + P + BAND]
        toep = flat1[:, 2600:2600 + BAND]
        decay_b = flat0[:, 2560:2592]
        decay_sum = flat0[:, 2592:2593]
        bv_col = flat0[:, 2594:2596]
        bo_b = flat0[:, 2600:2856]
        bias_row = {n: resid[0][0:1, i, :] for i, n in enumerate(("wq", "wk"))}
        bias_perm = {n: out_rows[0][0:1, i, :] for i, n in enumerate(("wq", "wk"))}
        one = resid[0][0:1, 2, 0:1]
        taps_dram = nc.dram_tensor("taps_row", [1, P + BAND], F32, kind="Internal").ap()

        def chunked(w):
            return w.rearrange("(k p) d -> p k d", k=2)

        def per_row(v):
            return v.rearrange("(a d) -> a d", a=1).partition_broadcast(P)

        with nc.Block() as block:
            row_set = sem("row_set")
            taps_in = sem("taps_in")
            taps_out = sem("taps_out")
            toep_in = sem("toep_in")
            zeroed = sem("zeroed")
            idents = sem("idents")
            toT_ps = sem("toT_ps")
            toT_sb = sem("toT_sb")
            mix_ps = sem("mix_ps")
            v_chain = sem("v_chain")
            mix_loaded = sem("mix_loaded")
            qkv_loaded = sem("qkv_loaded")
            late_loaded = sem("late_loaded")
            bias_set = sem("bias_set")
            bias_ps = sem("bias_ps")
            MIX_LOADS, QKV_LOADS, LATE_LOADS = 16 * 6, 16 * 5, 16 * 3

            @block.sync
            def _(eng):
                eng.dma_start(raw["to"], chunked(tok_Wo)).then_inc(mix_loaded, 16)
                eng.wait_ge(row_set, 1)
                eng.dma_start(row[:, P - 1:P - 1 + sh.TAPS],
                              decay_w.rearrange("(a d) -> a d", a=1)).then_inc(taps_in, 16)
                eng.dma_start(raw["tv"], chunked(tok_Wv)).then_inc(mix_loaded, 16)
                for k in range(2):
                    eng.dma_start(bv_col[:, k:k + 1], tok_bv.rearrange("(k p a) -> k p a", k=2, a=1)[k])\
                        .then_inc(mix_loaded, 16)
                eng.dma_start(decay_b, per_row(decay_w)).then_inc(mix_loaded, 16)
                eng.dma_start(bo_b, per_row(tok_bo)).then_inc(mix_loaded, 16)
                eng.wait_ge(taps_in, 16)
                eng.dma_start(taps_dram, row).then_inc(taps_out, 16)
                eng.dma_start(raw["wq"], chunked(wq)).then_inc(qkv_loaded, 16)
                eng.dma_start(raw["wk"], chunked(wk)).then_inc(qkv_loaded, 16)
                eng.dma_start(raw["wv"], chunked(wv)).then_inc(qkv_loaded, 16)
                for n, b in (("wq", bq), ("wk", bk)):
                    eng.dma_start(bias_row[n], b.rearrange("(a d) -> a d", a=1)).then_inc(qkv_loaded, 16)
                eng.wait_ge(taps_out, 16)
                eng.dma_start(toep, bass.AP(taps_dram.tensor, 0, [[1, P], [1, BAND]])).then_inc(toep_in, 16)
                eng.dma_start(w_o[:, :, :], chunked(wo)).then_inc(late_loaded, 16)
                eng.dma_start(bias_v[:, :], per_row(bv)).then_inc(late_loaded, 16)
                eng.dma_start(bias_o[:, :], per_row(bo)).then_inc(late_loaded, 16)

            @block.gpsimd
            def _(eng):
                eng.memset(row, 0.0).then_inc(row_set, 1)
                eng.memset(ident[:, :], 0.0).then_inc(zeroed, 1)
                eng.memset(causal[:, :, :], 0.0).then_inc(zeroed, 1)
                eng.wait_ge(zeroed, 2)
                eng.affine_select(out=ident[:, :], in_=ident[:, :], compare_op=ALU.not_equal, fill=1.0,
                                  base=0, pattern=[[-1, P]], channel_multiplier=1).then_inc(idents, 1)
                eng.affine_select(out=causal[:, :, :], in_=causal[:, :, :], compare_op=ALU.is_ge,
                                  fill=MASKED, base=0, pattern=[[0, 4], [-1, P]],
                                  channel_multiplier=1).then_inc(idents, 1)
                eng.memset(minus_half[:, :], -0.5)
                eng.memset(moments[:, :, :], 1.0)
                for p in range(2):
                    eng.memset(val[p][:, :, :, :], 1.0)
                    eng.memset(k_rows[p][:, :, :].bitcast(F32), 1.0)
                    eng.memset(q_rows[p][:, :, :].bitcast(F32), 0.0)

            @block.tensor
            def _(eng):
                eng.wait_ge(idents, 2)
                eng.wait_ge(mix_loaded, MIX_LOADS)
                for i in range(2):
                    for j in range(2):
                        last = eng.transpose(bank[j][:, i * P:(i + 1) * P],
                                             raw["to"][:, i, j * P:(j + 1) * P], ident[:, :])
                last.then_inc(toT_ps, 1)
                eng.wait_ge(toT_sb, 1)
                for j in range(2):
                    for k in range(2):
                        eng.matmul(bank[2 + j][:, 0:D], raw["tv"][:, k, j * P:(j + 1) * P], toT[:, k, :],
                                   start=(k == 0), stop=(k == 1))
                for k in range(2):
                    last = eng.matmul(bank[4][:, 0:D], bvb[:, k, :], toT[:, k, :],
                                      start=(k == 0), stop=(k == 1))
                last.then_inc(mix_ps, 1)
                eng.wait_ge(bias_set, 1)
                for i, n in enumerate(("wq", "wk")):
                    for e in range(2):
                        last = eng.matmul(bank[5][:, 2 * i + e:2 * i + e + 1], bias_perm[n][:, e * P:(e + 1) * P],
                                          one, start=True, stop=True)
                last.then_inc(bias_ps, 1)

            @block.vector
            def _(eng):
                chain = [0]

                def link(ins):
                    chain[0] += 1
                    ins.then_inc(v_chain, 1)
                    eng.wait_ge(v_chain, chain[0])

                link(eng.memset(one, 1.0))
                eng.wait_ge(mix_loaded, MIX_LOADS)
                link(eng.tensor_reduce(decay_sum, decay_b, AX.X, ALU.add))
                link(eng.memset(bvb, 1.0))
                for k in range(2):
                    link(eng.tensor_scalar(bvb[:, k, :], bvb[:, k, :], bv_col[:, k:k + 1], decay_sum,
                                           ALU.mult, ALU.mult))
                eng.wait_ge(toT_ps, 1)
                eng.tensor_copy(toT[:, 0, :], bank[0][:, 0:D])
                link(eng.tensor_copy(toT[:, 1, :], bank[1][:, 0:D]))
                eng.sem_inc(toT_sb, 1)
                link(eng.tensor_copy(ident_bf[:, :], ident[:, :]))
                link(eng.tensor_reduce(strip_half[:, :], ident[:, :].rearrange("p (j e f) -> p e j f", j=4, e=2),
                                       AX.XY, ALU.add))
                eng.wait_ge(mix_ps, 1)
                for j in range(2):
                    link(eng.tensor_copy(w_mix[0][:, j, :], bank[2 + j][:, 0:D]))
                    link(eng.tensor_tensor(w_mix[1][:, j, :], bank[2 + j][:, 0:D], w_mix[0][:, j, :].bitcast(F32),
                                           ALU.subtract))
                link(eng.tensor_tensor(bias_mix[:, :], bank[4][:, 0:D], bo_b, ALU.add))
                eng.wait_ge(qkv_loaded, QKV_LOADS)
                for n, scale in (("wq", sh.HD ** -0.5), ("wk", 1.0)):
                    for e in range(2):
                        for h in range(2):
                            for k in range(2):
                                dst = perm[n][:, k, 128 * e + 64 * h:128 * e + 64 * h + 64]
                                src = raw[n][:, k, 128 * h:128 * h + 128].rearrange("p (j e f) -> p j e f", j=4, e=2)
                                eng.tensor_scalar(dst.rearrange("p (f j) -> p j f", j=4), src[:, :, e, :],
                                                  scale, None, ALU.mult)
                            dst = bias_perm[n][:, 128 * e + 64 * h:128 * e + 64 * h + 64]
                            src = bias_row[n][:, 128 * h:128 * h + 128].rearrange("p (j e f) -> p j e f", j=4, e=2)
                            last = eng.tensor_scalar(dst.rearrange("p (f j) -> p j f", j=4), src[:, :, e, :],
                                                     scale, None, ALU.mult)
                link(last)
                eng.sem_inc(bias_set, 1)
                for full, (hi, lo) in ((perm["wq"], w_q), (perm["wk"], w_k), (raw["wv"], w_v)):
                    link(eng.tensor_copy(hi[:, :, :], full))
                    link(eng.tensor_tensor(lo[:, :, :], full, hi[:, :, :].bitcast(F32), ALU.subtract))
                eng.wait_ge(bias_ps, 1)
                eng.tensor_copy(bias_q[:, :], bank[5][:, 0:2])
                eng.tensor_copy(bias_k[:, :], bank[5][:, 2:4])
                eng.wait_ge(toep_in, 16)
                eng.tensor_copy(band[:, :], toep[:, ::-1])
                eng.wait_ge(late_loaded, LATE_LOADS)

        FIRST, LAST = -3, B
        LOOP_FROM, LOOPS = 1, (B - 6) // 2
        DENSE = 16

        class Step:
            def __init__(self, b, i, first_dense):
                self.b, self.i, self.first = b, i, first_dense
                self.real = b + 2 * i if isinstance(i, int) else b
                self.mix = 0 <= self.real + 3 < B
                self.front = 0 <= self.real + 2 < B
                self.maxima = 0 <= self.real + 1 < B
                self.attend = 0 <= self.real < B
                self.finish = 0 <= self.real - 1 < B
                names = self.names(self.real)
                self.dense = {n: first_dense + k for k, n in enumerate(names)}
                self.after = first_dense + len(names)

            @staticmethod
            def names(b):
                mix, front, maxima, attend, finish = (0 <= b + d < B for d in (3, 2, 1, 0, -1))
                return (["hid0", "hid1"] * front + ["maxT1"] * attend + ["val0"] * maxima
                        + ["nT0", "nT1", "q0", "q1", "k0", "k1"] * front + ["maxT0"] * maxima
                        + ["out0", "out1"] * finish + ["conv0", "conv1"] * mix + ["val1"] * maxima)

            def at(self, stage_shift, per, c):
                return (self.b + stage_shift) * per + c + self.i * (2 * per)

            def turn(self, stage_shift, per=1, c=0):
                n = self.b + stage_shift
                return (n // 2) * per + c + self.i * per

            def product(self, name):
                k = self.dense[name]
                return k % 2, k + self.i * (2 * DENSE)

            def read_before(self, name):
                names = self.names(self.real - 1)
                return self.first - len(names) + names.index(name) + 1 + self.i * (2 * DENSE)

        def run_steps(eng, step_fn):
            at = 0
            for b in range(FIRST, LOOP_FROM):
                s = Step(b, 0, at)
                step_fn(s)
                at = s.after
            with eng.Fori(0, LOOPS) as i:
                for b in (LOOP_FROM, LOOP_FROM + 1):
                    s = Step(b, i, at)
                    assert s.after - at == DENSE
                    step_fn(s)
                    at = s.after
            for b in range(LOOP_FROM + 2, LAST - 2 * (LOOPS - 1) + 1):
                s = Step(b, LOOPS - 1, at)
                step_fn(s)
                at = s.after

        assert LOOP_FROM + 2 * LOOPS + 2 < B

        MAX_UNITS = [(0, (0, 1, 2, 3)), (1, (0, 1)), (1, (2, 3)), (2, (0,)), (2, (1,)), (2, (2,)), (2, (3,))]
        EXP_UNITS = [(0, (0,)), (0, (1,)), (0, (2,)), (0, (3,)), (1, (0, 1)), (1, (2, 3)), (2, (0, 1, 2, 3))]
        KEYS_OF = [P, 2 * P, S]

        with nc.Block() as block:

            @block.tensor
            def _(eng):
                def open_bank(st, name):
                    par, k = st.product(name)
                    if st.dense[name] >= 2:
                        eng.wait_ge(dense_read, k - 1)
                    return bank_dense[par]

                def close(ins):
                    ins.then_inc(dense_done, 1)

                def split_product(out, pairs):
                    terms = [(a[i], m[j]) for a, m in pairs for i, j in ((0, 0), (0, 1), (1, 0))]
                    for n, (a, m) in enumerate(terms):
                        last = eng.matmul(out, a, m, start=(n == 0), stop=(n == len(terms) - 1),
                                          skip_group_check=True)
                    return last

                def split_rows(bank_, out, pairs, first):
                    terms = [(a[i], m[j]) for a, m in pairs for i, j in ((0, 0), (0, 1), (1, 0))]
                    for n, (a, m) in enumerate(terms):
                        last = eng.matmul(out, a, m, start=(first and n == 0), stop=(n == len(terms) - 1),
                                          skip_group_check=True)
                    return last

                def conv(st, j):
                    if j == 0:
                        eng.wait_ge(x_loaded[(st.b + 1) % 2], st.turn(3, 32, 32))
                    ps = open_bank(st, f"conv{j}")
                    xs = x_in[(st.b + 1) % 2]
                    for t in range(NT):
                        n = min(BAND, S - t * P)
                        kk = sh.T_in[t]
                        last = eng.matmul(ps[:, t * P:t * P + n], xs[0:kk, t, j * P:(j + 1) * P],
                                          band[0:kk, 0:n], start=(t == 0), stop=(t == NT - 1),
                                          skip_group_check=True)
                    close(last)

                def by_token(st, name, tiles, lhs, rhs):
                    ps = open_bank(st, name)
                    for n, t in enumerate(tiles):
                        tok = slice(t * P, t * P + T[t])
                        last = split_rows(ps, ps[0:T[t], n * D:(n + 1) * D],
                                          [([lhs[0][:, k, tok], lhs[1][:, k, tok]],
                                            [rhs[0][:, k, :], rhs[1][:, k, :]]) for k in range(2)], n == 0)
                    close(last)

                def hid_rows(st, n):
                    if n == 0:
                        eng.wait_ge(dense_read, st.read_before("conv1"))
                    by_token(st, f"hid{n}", [(0, 1), (2,)][n], mixed, w_mix)

                def normed_T(st, j):
                    ps = open_bank(st, f"nT{j}")
                    if j == 0:
                        eng.wait_ge(normed_done, st.at(2, NT, NT))
                    for t in range(NT):
                        last = eng.transpose(ps[:, t * P:t * P + T[t]], normed[0:T[t], t, j * P:(j + 1) * P],
                                             ident[0:T[t], 0:T[t]])
                    close(last)

                def query_key(st, name, j, w):
                    ps = open_bank(st, f"{name}{j}")
                    if name == "q" and j == 0:
                        par, k = st.product("nT1")
                        eng.wait_ge(dense_read, k + 1)
                    src = nT[st.b % 2]
                    close(split_product(ps[:, 0:S], [([w[0][:, k, j * P:(j + 1) * P], w[1][:, k, j * P:(j + 1) * P]],
                                                      [src[0][:, k, :], src[1][:, k, :]]) for k in range(2)]))

                def values(st, n):
                    by_token(st, f"val{n}", [(0, 1), (2,)][n], nT[(st.b + 1) % 2], w_v)

                def out_rows_(st, n):
                    if n == 0:
                        eng.wait_ge(attn_done, st.at(-1, 2, 2))
                    ps = open_bank(st, f"out{n}")
                    for m, t in enumerate([(0, 1), (2,)][n]):
                        for k in range(2):
                            last = eng.matmul(ps[0:T[t], m * D:(m + 1) * D], attnT[:, k, t * P:t * P + T[t]],
                                              w_o[:, k, :], start=(m == 0 and k == 0), stop=(k == 1),
                                              skip_group_check=True)
                    close(last)

                def max_T(st, half, shift):
                    ps = open_bank(st, f"maxT{half}")
                    eng.wait_ge(max_taken, st.at(shift, GROUPS * UNITS, 2 * UNITS * (half + 1)))
                    for t in range(NT):
                        last = eng.transpose(ps[0:8, t * P:t * P + T[t]], neg_max[0:T[t], t, half, :],
                                             ident[0:T[t], 0:T[t]])
                    close(last)

                def scores_for_max(st, g, u):
                    n = g * UNITS + u
                    par = n % 2
                    if u == 0 and g % 2 == 0:
                        eng.wait_ge(rows_loaded[(st.b + 1) % 2][g // 2], st.turn(1, 224, 224))
                    if not (st.b + 1 == 0 and isinstance(st.i, int) and n < 2):
                        eng.wait_ge(max_taken, st.at(1, GROUPS * UNITS, n - 1))
                    ps = bank_max[par]
                    t, heads = MAX_UNITS[u]
                    q, k = q_rows[(st.b + 1) % 2], k_rows[(st.b + 1) % 2]
                    w = KEYS_OF[t]
                    c = g % 2
                    for m, j in enumerate(heads):
                        slot = 4 * (g // 2) + j
                        eng.matmul(ps[0:T[t], m * w:(m + 1) * w],
                                   q[64 * c:64 * c + 64, slot, t * P:t * P + T[t]],
                                   k[64 * c:64 * c + 64, slot, 0:w], start=(m == 0), stop=False,
                                   skip_group_check=True)
                    d = T[t]
                    dst = ps[0:d, 0:len(heads) * w].rearrange("q (m w) -> q m w", w=w)[:, :, t * P:t * P + d]
                    eng.matmul(dst, ident_bf[0:d, 0:d], causal[0:d, 0:len(heads), 0:d], start=False, stop=True,
                               skip_group_check=True).then_inc(max_scores, 1)

                def scores_for_exp(st, g, u):
                    n = g * UNITS + u
                    par = n % 2
                    if u == 0 and g % 2 == 0:
                        eng.wait_ge(max_loaded[st.b % 2][g // 2], st.turn(0, 64, 64))
                    if not (st.b == 0 and isinstance(st.i, int) and n < 2):
                        eng.wait_ge(exp_done, st.at(0, GROUPS * UNITS, n - 1))
                    ps = bank_exp[par]
                    t, heads = EXP_UNITS[u]
                    q, k = q_rows[st.b % 2], k_rows[st.b % 2]
                    w = CUT[t]
                    c = g % 2
                    for m, j in enumerate(heads):
                        slot = 4 * (g // 2) + j
                        last = eng.matmul(ps[0:T[t], m * w:(m + 1) * w],
                                          k[64 * c:64 * c + 64, slot, t * P:t * P + T[t]],
                                          q[64 * c:64 * c + 64, slot, t * P:S],
                                          start=(m == 0), stop=(m == len(heads) - 1), skip_group_check=True)
                    last.then_inc(exp_scores, 1)

                def products_with_values(st, g, shift, t):
                    par = (st.b + shift) % 2
                    e = g % 2
                    if g == 0 and t == 0:
                        eng.wait_ge(dense_read, st.read_before("val1"))
                    if t == 0 and not (st.b == 0 and isinstance(st.i, int) and g < 2):
                        eng.wait_ge(odd_kept if e else even_kept, st.at(shift, 2, g // 2))
                    eng.wait_ge(probs_masked, st.at(shift, GROUPS * NT, g * NT + t + 1))
                    kk = T[t]
                    for j in range(4):
                        last = eng.matmul(bank_pv[e][32 * j:32 * j + 32, t * P:S],
                                          val[par][0:kk, t, 4 * (g // 2) + j, 32 * e:32 * e + 32],
                                          probs[g % 2][0:kk, j, OFF[t]:OFF[t] + CUT[t]],
                                          start=(t == 0), stop=(t == NT - 1),
                                          tile_position=(0, 32 * j), skip_group_check=True)
                    if t == NT - 1:
                        last.then_inc(pv_done, 1)

                def step(st):
                    for n in range(GROUPS * UNITS):
                        g, u = divmod(n, UNITS)
                        if st.maxima:
                            scores_for_max(st, g, u)
                        if st.attend:
                            scores_for_exp(st, g, u)
                        if st.front and n in (0, 1):
                            hid_rows(st, n)
                        if n == 3 and st.attend:
                            max_T(st, 1, 0)
                        if 2 <= u < 2 + NT:
                            if g == 0 and st.finish:
                                products_with_values(st, 3, -1, u - 2)
                            if g > 0 and st.attend:
                                products_with_values(st, g - 1, 0, u - 2)
                        if st.maxima and n in (5, 26):
                            values(st, (5, 26).index(n))
                        if st.front and n in (7, 8):
                            normed_T(st, n - 7)
                        if st.front and n in (10, 12):
                            query_key(st, "q", (n - 10) // 2, w_q)
                        if st.front and n in (14, 15):
                            query_key(st, "k", n - 14, w_k)
                        if n == 16 and st.maxima:
                            max_T(st, 0, 1)
                        if st.finish and n in (20, 21):
                            out_rows_(st, n - 20)
                        if st.mix and n in (23, 24):
                            conv(st, n - 23)
                run_steps(eng, step)

            @block.scalar
            def _(eng):
                def take_hi(st, name, dst, rows=P, bias=None):
                    par, k = st.product(name)
                    eng.wait_ge(dense_done, k + 1)
                    src = bank_dense[par][0:rows, 0:S]
                    if bias is None:
                        ins = eng.activation(dst, src, ACT.Copy)
                    else:
                        ins = eng.activation(dst, src, ACT.Identity, bias=bias)
                    ins.then_inc(dense_hi, 1)

                def keep(st, g, shift):
                    half, e = divmod(g, 2)
                    if not (isinstance(st.i, int) and st.b + shift == 0 and half == 0):
                        eng.wait_ge(joined, st.at(shift, 2, half))
                    eng.wait_ge(pv_done, st.at(shift, GROUPS, g + 1))
                    eng.activation(sum_of[e][:, :], bank_pv[e][:, 0:S], ACT.Copy, scale=strip_half[:, 1 - e:2 - e])
                    eng.activation(attn_of[e][:, :], bank_pv[e][:, 0:S], ACT.Copy, scale=strip_half[:, e:e + 1])\
                        .then_inc(odd_kept if e else even_kept, 1)

                def exps(st, g, u):
                    n = g * UNITS + u
                    if u == 0 and not (isinstance(st.i, int) and st.b == 0 and g < 2):
                        eng.wait_ge(pv_done, st.at(0, GROUPS, g - 1))
                    eng.wait_ge(exp_scores, st.at(0, GROUPS * UNITS, n + 1))
                    t, heads = EXP_UNITS[u]
                    w = CUT[t]
                    first = heads[0]
                    eng.activation(probs[g % 2][0:T[t], first:first + len(heads), OFF[t]:OFF[t] + w],
                                   bank_exp[n % 2][0:T[t], 0:len(heads) * w].rearrange("k (m w) -> k m w", w=w),
                                   ACT.Exp).then_inc(exp_done, 1)

                def step(st):
                    for n in range(GROUPS * UNITS):
                        g, u = divmod(n, UNITS)
                        if st.attend:
                            exps(st, g, u)
                        if n == 3 and st.attend:
                            take_hi(st, "maxT1", maxT[0][0:8, 1, :], 8)
                        if st.front and n in (7, 8):
                            take_hi(st, f"nT{n - 7}", nT[st.b % 2][0][:, n - 7, :])
                        if n == 5 and st.finish:
                            keep(st, 3, -1)
                        if n in (12, 19, 26) and st.attend:
                            keep(st, (12, 19, 26).index(n), 0)
                        if st.front and n in (10, 12):
                            if n == 10:
                                if not (isinstance(st.i, int) and st.b == -2):
                                    for h in range(2):
                                        eng.wait_ge(rows_loaded[(st.b + 1) % 2][h], st.turn(1, 224, 224))
                            j = (n - 10) // 2
                            take_hi(st, f"q{j}", q_flat[0][:, j, :], bias=bias_q[:, j:j + 1])
                        if st.front and n in (14, 15):
                            take_hi(st, f"k{n - 14}", k_flat[0][:, n - 14, :], bias=bias_k[:, n - 14:n - 13])
                        if n == 16 and st.maxima:
                            take_hi(st, "maxT0", maxT[0][0:8, 0, :], 8)
                        if st.mix and n in (23, 24):
                            take_hi(st, f"conv{n - 23}", mixed[0][:, n - 23, :])
                run_steps(eng, step)

            @block.vector
            def _(eng):
                HALF_1_AT, HALF_0_AT = (10, 11, 12, 14, 15), (22, 23, 25, 26, 27)
                HI = ["maxT1", "nT0", "nT1", "q0", "q1", "k0", "k1", "maxT0", "conv0", "conv1"]

                def take_lo(st, name, dst, hi, rows=P, bias=None):
                    par, k = st.product(name)
                    eng.wait_ge(dense_hi, st.hi_at + [m for m in HI if m in st.dense].index(name) + 1)
                    src = bank_dense[par][0:rows, 0:S]
                    if bias is None:
                        ins = eng.tensor_tensor(dst, src, hi.bitcast(F32), ALU.subtract)
                    else:
                        ins = eng.scalar_tensor_tensor(out=dst, in0=src, scalar=bias, in1=hi.bitcast(F32),
                                                       op0=ALU.add, op1=ALU.subtract)
                    ins.then_inc(dense_read, 1)

                def maxima(st, g, u):
                    n = g * UNITS + u
                    eng.wait_ge(max_scores, st.at(1, GROUPS * UNITS, n + 1))
                    t, heads = MAX_UNITS[u]
                    hf, e = g // 2, g % 2
                    w = KEYS_OF[t]
                    src = bank_max[n % 2][0:T[t], 0:len(heads) * w].rearrange("q (m w) -> q m w", w=w)
                    first = 4 * e + heads[0]
                    dst = neg_max[0:T[t], t, hf, first:first + len(heads)]
                    eng.tensor_reduce(dst, src, AX.X, ALU.max, negate=True).then_inc(max_taken, 1)

                def hid_out(st, n):
                    par, k = st.product(f"hid{n}")
                    if n == 0 and not (isinstance(st.i, int) and st.b < 0):
                        eng.wait_ge(resid_done, st.at(0, NT, NT))
                    eng.wait_ge(dense_done, k + 1)
                    for m, t in enumerate([(0, 1), (2,)][n]):
                        last = eng.tensor_tensor(hid[st.b % 2][0:T[t], t, :], bank_dense[par][0:T[t], m * D:(m + 1) * D],
                                                 bias_mix[0:T[t], :], ALU.add)
                    last.then_inc(dense_read, 1)

                def norm_stats(st):
                    _, k = st.product("hid1")
                    eng.wait_ge(dense_read, k + 1)
                    for t in range(NT):
                        eng.bn_stats(stats[0:T[t], t, :], hid[st.b % 2][0:T[t], t, :]).then_inc(s_stats, 1)
                    for t in range(NT):
                        wait_alone(eng, s_stats, st.at(2, NT, t + 1), passed_dve)
                        eng.bn_aggr(moments[0:T[t], t, :], stats[0:T[t], t, :]).then_inc(moments_done, 1)

                def norm(st):
                    eng.wait_ge(rstd_done, st.at(2, 1, 1))
                    for t in range(NT):
                        eng.tensor_scalar(normed[0:T[t], t, :], hid[st.b % 2][0:T[t], t, :],
                                          moments[0:T[t], t, 0:1], rstd[0:T[t], t:t + 1],
                                          ALU.subtract, ALU.mult).then_inc(normed_done, 1)

                def values(st, n):
                    par, k = st.product(f"val{n}")
                    eng.wait_ge(dense_done, k + 1)
                    for m, t in enumerate([(0, 1), (2,)][n]):
                        dst = val[(st.b + 1) % 2][0:T[t], t, :, :].rearrange("k a (q f) -> k a q f", q=4)[:, :, 0::3, :]
                        src = bank_dense[par][0:T[t], m * D:(m + 1) * D].rearrange("k (a e f) -> k a e f", e=2, f=16)
                        b = bias_v[0:T[t], :].rearrange("k (a e f) -> k a e f", e=2, f=16)
                        last = eng.tensor_tensor(dst, src, b, ALU.add)
                    last.then_inc(dense_read, 1)

                def out_sum(st, n):
                    if n == 0:
                        eng.wait_ge(resid_done, st.at(-1, NT, NT))
                        if not (isinstance(st.i, int) and st.b - 1 < 2):
                            eng.wait_ge(stored[(st.b - 1) % 2], st.turn(-3, 32, 32))
                    par, k = st.product(f"out{n}")
                    eng.wait_ge(dense_done, k + 1)
                    for m, t in enumerate([(0, 1), (2,)][n]):
                        last = eng.tensor_tensor(out_rows[(st.b - 1) % 2][0:T[t], t, :],
                                          bank_dense[par][0:T[t], m * D:(m + 1) * D],
                                          resid[(st.b - 1) % 2][0:T[t], t, :], ALU.add)
                    last.then_inc(dense_read, 1)

                def gather_sums(st, half, shift, piece):
                    if piece == 0:
                        wait_alone(eng, joined, st.at(shift, 2, half + 1), passed_dve)
                        eng.stream_shuffle(sums[:, :], sums_swapped[:, :], [(i + 16) % 32 for i in range(32)])\
                            .then_inc(sums_ready, 1)
                    else:
                        if piece == 1:
                            eng.wait_ge(sums_ready, st.at(shift, 2, half + 1))
                        cols = slice((piece - 1) * (S // 4), piece * (S // 4))
                        eng.reciprocal(recip[:, cols], sums[:, cols]).then_inc(recip_done, 1)

                def step(st):
                    for n in range(GROUPS * UNITS):
                        g, u = divmod(n, UNITS)
                        if st.maxima:
                            maxima(st, g, u)
                        if st.front and n in (1, 2):
                            hid_out(st, n - 1)
                            if n == 2:
                                norm_stats(st)
                        if n == 4 and st.attend:
                            take_lo(st, "maxT1", maxT[1][0:8, 1, :], maxT[0][0:8, 1, :], 8)
                        if n == 4 and st.front:
                            norm(st)
                        if st.finish and n in HALF_1_AT:
                            gather_sums(st, 1, -1, HALF_1_AT.index(n))
                        if st.maxima and n in (6, 27):
                            values(st, (6, 27).index(n))
                        if st.front and n in (8, 9):
                            j = n - 8
                            take_lo(st, f"nT{j}", nT[st.b % 2][1][:, j, :], nT[st.b % 2][0][:, j, :])
                        if st.front and n in (11, 13):
                            j = (n - 11) // 2
                            take_lo(st, f"q{j}", q_flat[1][:, j, :], q_flat[0][:, j, :], bias=bias_q[:, j:j + 1])
                        if st.front and n in (15, 16):
                            j = n - 15
                            take_lo(st, f"k{j}", k_flat[1][:, j, :], k_flat[0][:, j, :], bias=bias_k[:, j:j + 1])
                        if n == 17 and st.maxima:
                            take_lo(st, "maxT0", maxT[1][0:8, 0, :], maxT[0][0:8, 0, :], 8)
                        if st.attend and n in HALF_0_AT:
                            gather_sums(st, 0, 0, HALF_0_AT.index(n))
                        if st.finish and n in (21, 22):
                            out_sum(st, n - 21)
                        if st.mix and n in (24, 25):
                            j = n - 24
                            take_lo(st, f"conv{j}", mixed[1][:, j, :], mixed[0][:, j, :])

                hi_count = [0]
                FULL_HI = len(HI)

                def counted(st):
                    st.hi_at = hi_count[0] + st.i * (2 * FULL_HI)
                    step(st)
                    hi_count[0] += len([m for m in HI if m in st.dense])
                run_steps(eng, counted)

            @block.gpsimd
            def _(eng):
                def mask(st, g, t):
                    last_unit = (4, 6, 7)[t]
                    wait_alone(eng, exp_done, st.at(0, GROUPS * UNITS, g * UNITS + last_unit), passed_pool)
                    d = T[t]
                    blk = probs[g % 2][0:d, :, OFF[t]:OFF[t] + d]
                    eng.affine_select(out=blk, in_=blk, compare_op=ALU.is_ge, fill=0.0, base=0,
                                      pattern=[[0, 4], [1, d]], channel_multiplier=-1).then_inc(probs_masked, 1)

                def norm_scale(st):
                    wait_alone(eng, moments_done, st.at(2, NT, NT), passed_pool)
                    eng.tensor_scalar(var_eps[:, :], moments[:, :, 1], EPS, None, ALU.add).then_inc(var_done, 1)
                    eng.wait_ge(var_done, st.at(2, 1, 1))
                    eng.tensor_tensor(rstd[:, :], var_eps[:, :], minus_half[:, :], ALU.pow).then_inc(rstd_done, 1)

                def normalise(st, half, shift):
                    if shift == 0:
                        if st.finish:
                            _, k = st.product("out1")
                            eng.wait_ge(dense_read, k + 1)
                    elif 0 <= st.real - 2:
                        eng.wait_ge(dense_read, st.read_before("out1"))
                    eng.wait_ge(joined, st.at(shift, 2, half + 1))
                    eng.wait_ge(recip_done, st.at(shift, 8, 4 * half + 4))
                    eng.tensor_tensor(attnT[:, half, :], attn_raw[:, :], recip[:, :], ALU.mult).then_inc(attn_done, 1)

                def join(st, half, shift):
                    if not (isinstance(st.i, int) and st.b + shift == 0 and half == 0):
                        eng.wait_ge(sums_ready, st.at(shift, 2, half))
                        eng.wait_ge(attn_done, st.at(shift, 2, half))
                    eng.wait_ge(even_kept, st.at(shift, 2, half + 1))
                    eng.wait_ge(odd_kept, st.at(shift, 2, half + 1))
                    eng.tensor_tensor(attn_raw[:, :], attn_of[0][:, :], attn_of[1][:, :], ALU.add)
                    eng.tensor_tensor(sums_swapped[:, :], sum_of[0][:, :], sum_of[1][:, :], ALU.add)\
                        .then_inc(joined, 1)

                def residual(st):
                    par = (st.b + 1) % 2
                    eng.wait_ge(dense_read, st.read_before("hid1"))
                    if st.finish:
                        _, k = st.product("out1")
                        eng.wait_ge(dense_read, k + 1)
                    for t in range(NT):
                        eng.tensor_tensor(resid[par][0:T[t], t, :], hid[par][0:T[t], t, :],
                                          bias_o[0:T[t], :], ALU.add).then_inc(resid_done, 1)

                def step(st):
                    if st.front:
                        norm_scale(st)
                    for g in range(GROUPS):
                        if st.attend:
                            for t in range(NT):
                                mask(st, g, t)
                        if g == 0 and st.finish:
                            join(st, 1, -1)
                        if g == 1 and st.finish:
                            normalise(st, 1, -1)
                        if g == 2 and st.attend:
                            join(st, 0, 0)
                        if g == 2 and st.maxima:
                            residual(st)
                    if st.attend:
                        normalise(st, 0, 0)
                run_steps(eng, step)

            @block.sync
            def _(eng):
                def load_x(st):
                    for shift in (3, 4, 5) if st.b == FIRST else (5,):
                        if isinstance(st.i, int) and st.b + shift + 2 * st.i >= B:
                            continue
                        par = (st.b + shift) % 2
                        if shift == 5:
                            _, k = st.product("conv1")
                            wait_alone(eng, dense_done, k + 1, passed_sp)
                        n = st.b + shift + 2 * st.i
                        full = P * (NT - 1)
                        eng.dma_start(x_in[par][:, 0:NT - 1, :],
                                      x[n, 0:full, :].rearrange("(t p) d -> p t d", p=P)).then_inc(x_loaded[par], 16)
                        eng.dma_start(x_in[par][0:sh.T_in[-1], NT - 1, :], x[n, full:, :])\
                            .then_inc(x_loaded[par], 16)

                def rows(st, half):
                    par = st.b % 2
                    if half == 0:
                        _, k = st.product("k1")
                        wait_alone(eng, dense_read, k + 1, passed_sp)
                    if st.attend:
                        eng.wait_ge(exp_done, st.at(0, GROUPS * UNITS, 2 * UNITS * (half + 1)))
                    for flat, dst, order in ((q_flat, q_rows, (0, 0, 1)), (k_flat, k_rows, (0, 1, 0))):
                        for c in range(2):
                            for n, part in enumerate(order):
                                eng.dma_start(dst[par][64 * c + 16 * n:64 * c + 16 * n + 16, 4 * half:4 * half + 4, :]
                                              .bitcast(F32),
                                              flat[part][64 * half:64 * half + 64, c, :].bitcast(F32)
                                              ).then_inc(rows_loaded[par][half], 16)
                    for c in range(2):
                        at, slots = 64 * c + ROWS, slice(4 * half, 4 * half + 4)
                        eng.dma_start(q_rows[par][at:at + 2, slots, :].bitcast(F32),
                                      q_rows[par][at + 2:at + 4, slots, :].bitcast(F32)
                                      ).then_inc(rows_loaded[par][half], 16)

                def max_rows(st, half, shift):
                    par = (st.b + shift) % 2
                    _, k = st.product(f"maxT{half}")
                    eng.wait_ge(dense_read, k + 1)
                    for c in range(2):
                        for part in range(2):
                            row_ = 64 * c + ROWS + part
                            eng.dma_start(q_rows[par][row_:row_ + 1, 4 * half:4 * half + 4, :].bitcast(F32),
                                          maxT[part][4 * c:4 * c + 4, half, :].bitcast(F32)).then_inc(max_loaded[par][half], 16)

                def load_experts(st):
                    for h in range(2):
                        eng.wait_ge(rows_loaded[st.b % 2][h], st.turn(0, 224, 224))
                    eng.wait_ge(dense_read, st.read_before("val1"))
                    for name in ("router", "gate", "up", "down"):
                        experts.load(eng, name)

                def store(st):
                    n = st.b - 1 + 2 * st.i
                    par = (st.b - 1) % 2
                    full = P * (NT - 1)
                    _, k = st.product("out1")
                    wait_alone(eng, dense_read, k + 1, passed_sp)
                    eng.dma_start(h2_dram[n, 0:full, :].rearrange("(t p) d -> p t d", p=P),
                                  out_rows[par][:, 0:NT - 1, :]).then_inc(stored[par], 16)
                    eng.dma_start(h2_dram[n, full:, :], out_rows[par][0:T[-1], NT - 1, :]).then_inc(stored[par], 16)

                def step(st):
                    if st.attend:
                        max_rows(st, 1, 0)
                    if isinstance(st.i, int) and st.real == B - 1:
                        load_experts(st)
                    if st.front:
                        rows(st, 0)
                    if st.maxima:
                        max_rows(st, 0, 1)
                    if st.finish:
                        store(st)
                    if st.mix:
                        load_x(st)
                    if st.front:
                        rows(st, 1)
                run_steps(eng, step)
                for par in range(2):
                    eng.wait_ge(stored[par], 32 * (B // 2))



def expert_phase(nc, sem, sh, experts, h2_dram, out):
    S, D, NT, T, B, E = sh.S, sh.D, sh.NT, sh.T, sh.B, sh.E
    RC = sh.RC
    C = RC + sh.NS
    RING = 4
    TILES = [(0, 1), (2,)]
    FULL = P * (NT - 1)

    with ExitStack() as ctx:
        def sb(name, shape, dt=F32):
            return ctx.enter_context(nc.sbuf_tensor(name, shape, dt))

        bank = [ctx.enter_context(nc.psum_tensor(f"ebank{i}", [P, BANK], F32)) for i in range(8)]
        bank_gate, bank_up, bank_y, bank_prep = bank[0:2], bank[2:4], bank[4:6], bank[6:8]

        ident = sb("e_ident", [P, P])
        minus_half = sb("e_minus_half", [P, NT])
        expert_no = sb("expert_no", [P, NT, E])
        w_gate = [sb(f"w_gate_{s}", [P, 2, C, P], F32R) for s in ("hi", "lo")]
        w_up = [sb(f"w_up_{s}", [P, 2, C, P], F32R) for s in ("hi", "lo")]
        w_down = [sb(f"w_down_{s}", [P, C, D], F32R) for s in ("hi", "lo")]
        w_router = sb("w_router", [P, 2, 2, E], F32R)
        h2 = [sb(f"h2_{p}", [P, NT, D]) for p in range(2)]
        y_rows = [sb(f"y_rows{p}", [P, NT, D]) for p in range(2)]
        normed = sb("e_normed", [P, NT, D])
        stats = sb("e_stats", [P, NT, 6])
        moments = sb("e_moments", [P, NT, 2])
        var_eps = sb("e_var_eps", [P, NT])
        rstd = sb("e_rstd", [P, NT])
        nT = [[sb(f"e_normedT{p}_{s}", [P, 2, S], F32R) for s in ("hi", "lo")] for p in range(2)]
        logits = sb("logits", [P, NT, E])
        top = sb("top", [P, NT, 8])
        top_no = sb("top_no", [P, NT, 8], U32)
        top_nof = sb("top_nof", [P, NT, 2])
        shifted = sb("shifted", [P, NT, E])
        exps = sb("exps", [P, NT, E])
        chosen = sb("chosen", [P, NT, E])
        chosen2 = sb("chosen2", [P, NT, E])
        all_sum = sb("all_sum", [P, NT])
        top_sum = sb("top_sum", [P, NT])
        inv_sum = sb("inv_sum", [P, NT])
        comb = sb("comb", [P, NT, E])
        combT = sb("combT", [E, S])
        comb_all = [sb(f"comb_all{p}", [P, RC, S]) for p in range(2)]
        tanh = [sb(f"tanh{p}", [P, S]) for p in range(2)]
        gated = [sb(f"gated{p}", [P, S]) for p in range(2)]
        hidden = [sb(f"hidden{p}", [P, S]) for p in range(2)]
        weighted = [sb(f"weighted{p}", [P, S]) for p in range(2)]
        hid_hi = [sb(f"hid_hi{p}", [P, S], F32R) for p in range(RING)]
        hid_lo = [sb(f"hid_lo{p}", [P, S], F32R) for p in range(RING)]

        comb_dram = [nc.dram_tensor(f"comb_dram{p}", [E, S], F32, kind="Internal").ap() for p in range(2)]

        split_hi = sem("split_hi")
        split_lo = sem("split_lo")
        passed_dve, passed_pool, passed_sp = (sem(f"e_passed_{e}") for e in ("dve", "pool", "sp"))
        e_zeroed = sem("e_zeroed")
        e_consts = sem("e_consts")
        h2_loaded = [sem(f"h2_loaded{p}") for p in range(2)]
        comb_stored = [sem(f"comb_stored{p}") for p in range(2)]
        comb_loaded = [sem(f"comb_loaded{p}") for p in range(2)]
        y_stored = [sem(f"y_stored{p}") for p in range(2)]
        e_stats_done = sem("e_stats_done")
        e_moments_done = sem("e_moments_done")
        e_var_done = sem("e_var_done")
        e_rstd_done = sem("e_rstd_done")
        e_normed_done = sem("e_normed_done")
        prep_done = sem("prep_done")
        nT_hi_done = sem("nT_hi_done")
        prep_read = sem("prep_read")
        route = sem("route")
        route_exp = sem("route_exp")
        gate_done = sem("gate_done")
        up_done = sem("up_done")
        tanh_done = sem("tanh_done")
        gated_done = sem("gated_done")
        hidden_done = sem("hidden_done")
        weighted_done = sem("weighted_done")
        hi_done = sem("hi_done")
        lo_done = sem("lo_done")
        down_done = sem("down_done")
        h2_kept = sem("h2_kept")
        y_read = sem("y_read")

        SPLIT_AT = {0: 0, 2: 1, 4: 2, 9: 3}
        SPLIT = [("router", experts.router, (w_router[:, :, 0, :], w_router[:, :, 1, :])), ("gate", experts.gate, w_gate), ("up", experts.up, w_up),
                 ("down", experts.down, w_down)]

        LOOPS = (B - 2) // 2

        class Step:
            def __init__(self, n, i):
                self.n, self.i = n, i
                real = n + 2 * i if isinstance(i, int) else n
                self.prep = real + 1 < B
                self.experts = 0 <= real < B
                self.finish = real >= 1 or not isinstance(i, int)
                self.load = not isinstance(i, int) or real + 3 < B

            def at(self, shift, per, c):
                return (self.n + shift) * per + c + self.i * (2 * per)

            def turn(self, shift, per, c=0):
                return ((self.n + shift) // 2) * per + c + self.i * per

            def early(self, n):
                return isinstance(self.i, int) and self.i == 0 and self.n < n

        def run_steps(eng, step_fn):
            step_fn(Step(-1, 0))
            step_fn(Step(0, 0))
            step_fn(Step(1, 0))
            with eng.Fori(1, LOOPS - 1) as i:
                step_fn(Step(0, i))
                step_fn(Step(1, i))
            for i in (LOOPS - 1, LOOPS):
                step_fn(Step(0, i))
                step_fn(Step(1, i))
            step_fn(Step(2, LOOPS))

        ROUTE = 13

        def weights_of(c):
            return RC + c if c < sh.NS else c - sh.NS

        def ring(parts, n, c):
            return parts[(n * C + c) % RING]

        with nc.Block() as block:

            @block.tensor
            def _(eng):
                eng.wait_ge(e_consts, 1)

                def split3(out, pairs, first):
                    terms = [(a[i], m[j]) for a, m in pairs for i, j in ((0, 0), (0, 1), (1, 0))]
                    for n, (a, m) in enumerate(terms):
                        last = eng.matmul(out, a, m, start=(first and n == 0), stop=(n == len(terms) - 1),
                                          skip_group_check=True)
                    return last

                def open_prep(st, c):
                    if not (st.n == -1 and c < 2):
                        eng.wait_ge(prep_read, st.at(1, 4, c - 1))

                def normed_T(st):
                    for j in range(2):
                        open_prep(st, j)
                        if j == 0:
                            eng.wait_ge(e_normed_done, st.at(1, NT, NT))
                        for t in range(NT):
                            last = eng.transpose(bank_prep[j][:, t * P:t * P + T[t]],
                                                 normed[0:T[t], t, j * P:(j + 1) * P], ident[0:T[t], 0:T[t]])
                        last.then_inc(prep_done, 1)

                def router(st):
                    if st.n == -1:
                        eng.wait_ge(split_lo, 1)
                    eng.wait_ge(prep_read, st.at(1, 4, 2))
                    src = nT[(st.n + 1) % 2]
                    for t in range(NT):
                        tok = slice(t * P, t * P + T[t])
                        for k in range(2):
                            eng.matmul(bank_prep[0][0:T[t], 2 * E * t:2 * E * (t + 1)], src[0][:, k, tok],
                                       w_router[:, k, :, :].rearrange("p a e -> p (a e)"),
                                       start=(t == 0 and k == 0), stop=False, skip_group_check=True)
                            last = eng.matmul(bank_prep[0][0:T[t], 2 * E * t:2 * E * t + E], src[1][:, k, tok],
                                              w_router[:, k, 0, :], start=False, stop=(k == 1),
                                              skip_group_check=True)
                    last.then_inc(prep_done, 1)

                def comb_T(st):
                    open_prep(st, 3)
                    eng.wait_ge(route, st.at(1, ROUTE, ROUTE))
                    for t in range(NT):
                        last = eng.transpose(bank_prep[1][0:E, t * P:t * P + T[t]], comb[0:T[t], t, :],
                                             ident[0:T[t], 0:T[t]])
                    last.then_inc(prep_done, 1)

                def gate_up(st, c):
                    src = nT[st.n % 2]
                    if not (st.early(1) and c < 2):
                        eng.wait_ge(hidden_done, st.at(0, C, c - 1))
                    for n, (w, ps, done) in enumerate(((w_gate, bank_gate, gate_done), (w_up, bank_up, up_done))):
                        if st.early(1) and c == 0:
                            eng.wait_ge(split_lo, 2 + n)
                        split3(ps[c % 2][:, 0:S], [([w[0][:, k, weights_of(c), :], w[1][:, k, weights_of(c), :]],
                                                    [src[0][:, k, :], src[1][:, k, :]]) for k in range(2)],
                               True).then_inc(done, 1)

                def down(st, shift, c):
                    if c == 0 and shift == 0:
                        if st.early(1):
                            eng.wait_ge(split_lo, 4)
                        else:
                            eng.wait_ge(y_read, st.at(0, 1, 0))
                    eng.wait_ge(lo_done, st.at(shift, C, c + 1))
                    hi, lo = ring(hid_hi, st.n + shift, c), ring(hid_lo, st.n + shift, c)
                    for b, tiles in enumerate(TILES):
                        for m, t in enumerate(tiles):
                            tok = slice(t * P, t * P + T[t])
                            last = split3(bank_y[b][0:T[t], m * D:(m + 1) * D],
                                          [([hi[:, tok], lo[:, tok]],
                                            [w_down[0][:, weights_of(c), :], w_down[1][:, weights_of(c), :]])],
                                          c == 0 and m == 0)
                    last.then_inc(down_done, 1)

                def step(st):
                    for c in range(C):
                        if st.experts:
                            gate_up(st, c)
                        if st.early(1) and st.n == 0 and c == 1:
                            comb_T(Step(-1, 0))
                        if c >= 2 and st.experts:
                            down(st, 0, c - 2)
                        if c < 2 and st.finish:
                            down(st, -1, C - 2 + c)
                        if st.prep:
                            if c == 3:
                                normed_T(st)
                            if c == 5:
                                router(st)
                            if c == 8 and st.n >= 0:
                                comb_T(st)
                run_steps(eng, step)

            @block.scalar
            def _(eng):
                def tanh_of(st, c):
                    if not (st.early(1) and c < 2):
                        eng.wait_ge(gated_done, st.at(0, C, c - 1))
                    eng.wait_ge(gate_done, st.at(0, C, c + 1))
                    eng.activation(tanh[c % 2][:, :], bank_gate[c % 2][:, 0:S], ACT.Tanh, scale=0.5)\
                        .then_inc(tanh_done, 1)

                def hi_of(st, shift, c):
                    if not (st.early(1) and c < RING):
                        eng.wait_ge(down_done, st.at(shift, C, c + 1 - RING))
                    if c < sh.NS:
                        eng.wait_ge(hidden_done, st.at(shift, C, c + 1))
                        src = hidden[c % 2]
                    else:
                        eng.wait_ge(weighted_done, st.at(shift, RC, c - sh.NS + 1))
                        src = weighted[c % 2]
                    eng.activation(ring(hid_hi, st.n + shift, c)[:, :], src[:, :], ACT.Copy).then_inc(hi_done, 1)

                def keep_h2(st):
                    par = (st.n + 1) % 2
                    eng.wait_ge(h2_loaded[par], st.turn(1, 32, 32))
                    if not st.early(1):
                        eng.wait_ge(y_stored[par], st.turn(-1, 32, 32))
                    eng.activation(y_rows[par][:, 0:NT - 1, :], h2[par][:, 0:NT - 1, :], ACT.Copy)
                    eng.activation(y_rows[par][0:T[-1], NT - 1, :], h2[par][0:T[-1], NT - 1, :], ACT.Copy)\
                        .then_inc(h2_kept, 1)

                def split(n):
                    name, full, (hi, lo) = SPLIT[n]
                    eng.wait_ge(experts.loaded[name], experts.LOADS[name])
                    eng.activation(hi[:], full[:], ACT.Copy).then_inc(split_hi, 1)

                def step(st):
                    for c in range(C):
                        if st.n == -1 and c in SPLIT_AT:
                            split(SPLIT_AT[c])
                        if st.experts:
                            tanh_of(st, c)
                        if c == 0 and st.finish:
                            hi_of(st, -1, C - 1)
                        if c >= 1 and st.experts:
                            hi_of(st, 0, c - 1)
                        if st.prep:
                            if c == 3:
                                for j in range(2):
                                    eng.wait_ge(prep_done, st.at(1, 4, j + 1))
                                    eng.activation(nT[(st.n + 1) % 2][0][:, j, :], bank_prep[j][:, 0:S], ACT.Copy)\
                                        .then_inc(nT_hi_done, 1)
                            if c == 5:
                                keep_h2(st)
                            if c == 6:
                                eng.wait_ge(route, st.at(1, ROUTE, 4))
                                eng.activation(exps[:, :, :], shifted[:, :, :], ACT.Exp).then_inc(route_exp, 1)
                run_steps(eng, step)

            @block.vector
            def _(eng):
                def gate_times_up(st, c):
                    k = c - 2 if c >= 2 else C - 2 + c
                    if k >= sh.NS and not (st.early(1) and c < 2):
                        eng.wait_ge(weighted_done, st.at(0 if c >= 2 else -1, RC, k - sh.NS + 1))
                    eng.wait_ge(tanh_done, st.at(0, C, c + 1))
                    eng.scalar_tensor_tensor(out=gated[c % 2][:, :], in0=tanh[c % 2][:, :], scalar=1.0,
                                             in1=bank_gate[c % 2][:, 0:S], op0=ALU.add, op1=ALU.mult)\
                        .then_inc(gated_done, 1)
                    eng.wait_ge(up_done, st.at(0, C, c + 1))
                    eng.wait_ge(gated_done, st.at(0, C, c + 1))
                    eng.scalar_tensor_tensor(out=hidden[c % 2][:, :], in0=gated[c % 2][:, :], scalar=0.5,
                                             in1=bank_up[c % 2][:, 0:S], op0=ALU.mult, op1=ALU.mult)\
                        .then_inc(hidden_done, 1)

                def norm_stats(st):
                    par = (st.n + 1) % 2
                    eng.wait_ge(h2_loaded[par], st.turn(1, 32, 32))
                    for t in range(NT):
                        eng.bn_stats(stats[0:T[t], t, :], h2[par][0:T[t], t, :]).then_inc(e_stats_done, 1)
                    for t in range(NT):
                        wait_alone(eng, e_stats_done, st.at(1, NT, t + 1), passed_dve)
                        eng.bn_aggr(moments[0:T[t], t, :], stats[0:T[t], t, :]).then_inc(e_moments_done, 1)

                def norm(st):
                    eng.wait_ge(e_rstd_done, st.at(1, 1, 1))
                    for t in range(NT):
                        eng.tensor_scalar(normed[0:T[t], t, :], h2[(st.n + 1) % 2][0:T[t], t, :],
                                          moments[0:T[t], t, 0:1], rstd[0:T[t], t:t + 1],
                                          ALU.subtract, ALU.mult).then_inc(e_normed_done, 1)

                def routing(st, part):
                    count = [0]

                    def link(ins):
                        ins.then_inc(route, 1)
                        count[0] += 1
                        wait_alone(eng, route, st.at(1, ROUTE, part[1] + count[0]), passed_dve)

                    if part[0] == 0:
                        eng.wait_ge(prep_done, st.at(1, 4, 3))
                        for t in range(NT):
                            both = bank_prep[0][0:T[t], 2 * E * t:2 * E * (t + 1)].rearrange("p (a e) -> p e a", a=2)
                            last = eng.tensor_reduce(logits[0:T[t], t, :], both, AX.X, ALU.add)
                        last.then_inc(prep_read, 1)
                        wait_alone(eng, prep_read, st.at(1, 4, 3), passed_dve)
                        for t in range(NT):
                            ins = eng.max(top[:, t, :], logits[:, t, :])
                        link(ins)
                        for t in range(NT):
                            ins = eng.max_index(top_no[:, t, :], top[:, t, :], logits[:, t, :])
                        link(ins)
                        link(eng.tensor_copy(top_nof[:, :, :], top_no[:, :, 0:2]))
                        link(eng.tensor_tensor(shifted[:, :, :], logits[:, :, :],
                                               top[:, :, 0:1].broadcast_to([P, NT, E]), ALU.subtract))
                        link(eng.tensor_tensor(chosen[:, :, :], expert_no[:, :, :],
                                               top_nof[:, :, 0:1].broadcast_to([P, NT, E]), ALU.is_equal))
                        link(eng.tensor_tensor(chosen2[:, :, :], expert_no[:, :, :],
                                               top_nof[:, :, 1:2].broadcast_to([P, NT, E]), ALU.is_equal))
                        link(eng.tensor_tensor(chosen[:, :, :], chosen[:, :, :], chosen2[:, :, :], ALU.add))
                    else:
                        eng.wait_ge(route_exp, st.at(1, 1, 1))
                        link(eng.tensor_reduce(all_sum[:, :], exps[:, :, :], AX.X, ALU.add))
                        link(eng.tensor_tensor(chosen[:, :, :], chosen[:, :, :], exps[:, :, :], ALU.mult))
                        link(eng.tensor_reduce(top_sum[:, :], chosen[:, :, :], AX.X, ALU.add))
                        link(eng.scalar_tensor_tensor(out=top_sum[:, :], in0=all_sum[:, :], scalar=1e-9,
                                                      in1=top_sum[:, :], op0=ALU.mult, op1=ALU.add))
                        link(eng.reciprocal(inv_sum[:, :], top_sum[:, :]))
                        link(eng.tensor_tensor(comb[:, :, :], chosen[:, :, :],
                                               inv_sum[:, :].rearrange("p (t a) -> p t a", a=1)
                                               .broadcast_to([P, NT, E]), ALU.mult))

                def lo_of(st, shift, c):
                    eng.wait_ge(hi_done, st.at(shift, C, c + 1))
                    src = hidden[c % 2] if c < sh.NS else weighted[c % 2]
                    eng.tensor_tensor(ring(hid_lo, st.n + shift, c)[:, :], src[:, :],
                                      ring(hid_hi, st.n + shift, c)[:, :].bitcast(F32), ALU.subtract)\
                        .then_inc(lo_done, 1)

                def result(st):
                    eng.wait_ge(h2_kept, st.at(-1, 1, 1))
                    eng.wait_ge(down_done, st.at(-1, C, C))
                    rows = y_rows[(st.n - 1) % 2]
                    for b, tiles in enumerate(TILES):
                        for m, t in enumerate(tiles):
                            ins = eng.tensor_tensor(rows[0:T[t], t, :], bank_y[b][0:T[t], m * D:(m + 1) * D],
                                                    rows[0:T[t], t, :], ALU.add)
                    ins.then_inc(y_read, 1)

                def split(n):
                    name, full, (hi, lo) = SPLIT[n]
                    eng.wait_ge(split_hi, n + 1)
                    eng.tensor_tensor(lo[:], full[:], hi[:].bitcast(F32), ALU.subtract).then_inc(split_lo, 1)

                eng.wait_ge(e_consts, 1)

                def step(st):
                    for c in range(C):
                        if st.n == -1 and c in SPLIT_AT:
                            split(SPLIT_AT[c])
                        if st.experts:
                            gate_times_up(st, c)
                        if c == 0 and st.finish:
                            lo_of(st, -1, C - 1)
                        if c >= 1 and st.experts:
                            lo_of(st, 0, c - 1)
                        if c == 1 and st.finish:
                            result(st)
                        if st.prep:
                            if c == 0:
                                norm_stats(st)
                            if c == 1:
                                norm(st)
                            if c == 3:
                                for j in range(2):
                                    eng.wait_ge(nT_hi_done, st.at(1, 2, j + 1))
                                    dst = nT[(st.n + 1) % 2]
                                    eng.tensor_tensor(dst[1][:, j, :], bank_prep[j][:, 0:S],
                                                      dst[0][:, j, :].bitcast(F32), ALU.subtract)\
                                        .then_inc(prep_read, 1)
                            if c == 5:
                                routing(st, (0, 0))
                            if c == 7:
                                routing(st, (1, 7))
                            if c == 8:
                                eng.wait_ge(prep_done, st.at(1, 4, 4))
                                eng.tensor_copy(combT[:, :], bank_prep[1][0:E, 0:S]).then_inc(prep_read, 1)
                run_steps(eng, step)

            @block.gpsimd
            def _(eng):
                eng.memset(ident[:, :], 0.0).then_inc(e_zeroed, 1)
                eng.wait_ge(e_zeroed, 1)
                eng.affine_select(out=ident[:, :], in_=ident[:, :], compare_op=ALU.not_equal, fill=1.0,
                                  base=0, pattern=[[-1, P]], channel_multiplier=1)
                eng.memset(minus_half[:, :], -0.5)
                eng.memset(moments[:, :, :], 1.0)
                eng.memset(logits[:, :, :], 0.0)
                eng.iota(expert_no[:, :, :], pattern=[[0, NT], [1, E]], base=0, channel_multiplier=0,
                         allow_small_or_imprecise_dtypes=True).then_inc(e_consts, 1)

                def norm_scale(st):
                    wait_alone(eng, e_moments_done, st.at(1, NT, NT), passed_pool)
                    eng.tensor_scalar(var_eps[:, :], moments[:, :, 1], EPS, None, ALU.add).then_inc(e_var_done, 1)
                    eng.wait_ge(e_var_done, st.at(1, 1, 1))
                    eng.tensor_tensor(rstd[:, :], var_eps[:, :], minus_half[:, :], ALU.pow).then_inc(e_rstd_done, 1)

                def weigh(st, c):
                    eng.wait_ge(lo_done, st.at(0, C, c - 1))
                    wait_alone(eng, hidden_done, st.at(0, C, c + 1), passed_pool)
                    if c == sh.NS:
                        eng.wait_ge(comb_loaded[st.n % 2], st.turn(0, 32, 32))
                    eng.tensor_tensor(weighted[c % 2][:, :], hidden[c % 2][:, :],
                                      comb_all[st.n % 2][:, c - sh.NS, :], ALU.mult).then_inc(weighted_done, 1)

                def step(st):
                    if st.prep:
                        norm_scale(st)
                    if st.experts:
                        for c in range(sh.NS, C):
                            weigh(st, c)
                run_steps(eng, step)

            @block.sync
            def _(eng):
                def load_h2(par, n):
                    eng.dma_start(h2[par][:, 0:NT - 1, :],
                                  h2_dram[n, 0:FULL, :].rearrange("(t p) d -> p t d", p=P)).then_inc(h2_loaded[par], 16)
                    eng.dma_start(h2[par][0:T[-1], NT - 1, :], h2_dram[n, FULL:, :]).then_inc(h2_loaded[par], 16)

                def step(st):
                    if st.n == -1:
                        load_h2(0, 0)
                        load_h2(1, 1)
                    if st.finish:
                        n = st.n - 1 + 2 * st.i
                        rows = y_rows[(st.n - 1) % 2]
                        wait_alone(eng, y_read, st.at(-1, 1, 1), passed_sp)
                        eng.dma_start(out[n, 0:FULL, :].rearrange("(t p) d -> p t d", p=P),
                                      rows[:, 0:NT - 1, :]).then_inc(y_stored[(st.n - 1) % 2], 16)
                        eng.dma_start(out[n, FULL:, :], rows[0:T[-1], NT - 1, :])\
                            .then_inc(y_stored[(st.n - 1) % 2], 16)
                    if st.prep:
                        par = (st.n + 1) % 2
                        if st.load:
                            wait_alone(eng, h2_kept, st.at(1, 1, 1), passed_sp)
                            wait_alone(eng, e_normed_done, st.at(1, NT, NT), passed_sp)
                            load_h2(par, st.n + 3 + 2 * st.i)
                        eng.wait_ge(prep_read, st.at(1, 4, 4))
                        eng.dma_start(comb_dram[par], combT[:, :]).then_inc(comb_stored[par], 16)
                        wait_alone(eng, comb_stored[par], st.turn(1, 16, 16), passed_sp)
                        if not st.early(1):
                            eng.wait_ge(weighted_done, st.at(-1, RC, RC))
                        for e2 in range(2):
                            eng.dma_start(comb_all[par][64 * e2:64 * e2 + 64, :, :],
                                          bass.AP(comb_dram[par].tensor, e2 * S, [[0, 64], [2 * S, RC], [1, S]]))\
                                .then_inc(comb_loaded[par], 16)
                run_steps(eng, step)
                for par in range(2):
                    eng.wait_ge(y_stored[par], 32 * (B // 2))


def audio_tower(nc, x, tok_Wv, tok_bv, tok_Wo, tok_bo, decay_w, wq, bq, wk, bk, wv, bv, wo, bo,
                router_w, wg_r, wu_r, wd_r, wg_s, wu_s, wd_s, out):
    sh = Shapes(x, decay_w, wg_r, wg_s)
    h2_dram = nc.dram_tensor("h2_dram", [sh.B, sh.S, sh.D], F32, kind="Internal").ap()
    with ExitStack() as ctx:
        def sem(name):
            return ctx.enter_context(nc.semaphore(name))

        def sb(name, shape, dt=F32):
            return ctx.enter_context(nc.sbuf_tensor(name, shape, dt))

        with ExitStack() as first_use:
            front = [[first_use.enter_context(nc.sbuf_tensor(f"{name}_{part}", [P, 2, sh.S], F32R))
                      for part in ("hi", "lo")] for name in ("q_flat", "k_flat", "mixed", "normedT0", "normedT1")]
        experts = ExpertWeights(sh, sb, sem, router_w, wg_r, wu_r, wd_r, wg_s, wu_s, wd_s)
        attention_phase(nc, sem, sh, front, experts, h2_dram, x, tok_Wv, tok_bv, tok_Wo, tok_bo, decay_w,
                        wq, bq, wk, bk, wv, bv, wo, bo)
        expert_phase(nc, sem, sh, experts, h2_dram, out)


_INS = ['x', 'L0_tok_Wv', 'L0_tok_bv', 'L0_tok_Wo', 'L0_tok_bo', 'L0_tok_decay_w', 'L0_attn_wq', 'L0_attn_bq',
        'L0_attn_wk', 'L0_attn_bk', 'L0_attn_wv', 'L0_attn_bv', 'L0_attn_wo', 'L0_attn_bo', 'L0_ffn_router_w',
        'L0_ffn_wg_r', 'L0_ffn_wu_r', 'L0_ffn_wd_r', 'L0_ffn_wg_s', 'L0_ffn_wu_s', 'L0_ffn_wd_s']


def kernel(**inputs):
    import numpy as _np
    import concourse.bacc as _bacc
    from concourse import mybir as _mybir
    from concourse.bass_utils import run_bass_kernel_spmd as _run

    nc = _bacc.Bacc("TRN2", target_bir_lowering=False, num_devices=1)
    arrays, args = {}, []
    for name in _INS:
        a = _np.ascontiguousarray(inputs[name])
        arrays[f"in_{name}_dram"] = a
        args.append(nc.dram_tensor(f"in_{name}_dram", a.shape, _mybir.dt.from_np(a.dtype), kind="ExternalInput").ap())
    batch, tokens, dim = inputs["x"].shape
    out = nc.dram_tensor("out_0_dram", (batch, tokens + 1, dim), F32, kind="ExternalOutput").ap()
    audio_tower(nc, *args, out)
    r = _run(nc, [arrays], core_ids=[0])
    return r.results[0]["out_0_dram"]
```
